# Optimizing a Trainium2 kernel written in Bass

```python
import numpy as np
import jax
import jax.numpy as jnp

def _softmax(x, axis=-1):
    return jax.nn.softmax(x, axis=axis)

def _gelu(x):
    return jax.nn.gelu(x, approximate=True)

def _silu(x):
    return jax.nn.silu(x)

def _sigmoid(x):
    return jax.nn.sigmoid(x)

def _layernorm(x, axis=-1, eps=1e-05):
    m = jnp.mean(x, axis=axis, keepdims=True)
    v = jnp.var(x, axis=axis, keepdims=True)
    return (x - m) / jnp.sqrt(v + eps)

def _scatter_add(tgt, idx, src, axis=0):
    return tgt.at[idx].add(src)

def _segment_sum(src, seg, n):
    return jax.ops.segment_sum(src, seg, n)
kernel_name = 'mk_gps_d1_gnn_r32_2ffeb4'

def setup_inputs(seed: int=0):
    np.random.seed(seed)
    _w = jnp.asarray

    def _rec_inputs():
        import jax
        import jax.numpy as jnp
        _gk = jax.random.key(seed)
        x = -0.0003929 + 0.9999 * jax.random.normal(jax.random.fold_in(_gk, 1), (512, 1024), jnp.float32)
        src = jax.random.randint(jax.random.fold_in(_gk, 2), (8192,), 0, 512, jnp.int32)
        dst = jax.random.randint(jax.random.fold_in(_gk, 3), (8192,), 0, 512, jnp.int32)
        _o = jnp.argsort(dst, stable=True)
        src = src[_o]
        dst = dst[_o]
        return (x, src, dst)
    x, src, dst = _rec_inputs()

    def _L0_gnn_setup():
        import jax, jax.numpy as jnp
        import numpy as np
        NH, NO = (128, 384)
        N = NH + NO
        E_HH, E_OO, E_HO = (256, 1280, 512)
        E = E_HH + E_OO + E_HO
        D = 1024
        key = jax.random.key(seed)
        ks = jax.random.split(key, 12)
        w = lambda k, s: jax.random.normal(k, s, jnp.float32) * 0.02
        return {'n_f': jax.random.normal(ks[0], (N, D), jnp.float32), 'W_hh': w(ks[1], (2 * D, D)), 'b_hh': jnp.zeros((D,), jnp.float32), 'W_oo': w(ks[2], (2 * D, D)), 'b_oo': jnp.zeros((D,), jnp.float32), 'W_ho': w(ks[3], (2 * D, D)), 'b_ho': jnp.zeros((D,), jnp.float32), 'W_a': w(ks[4], (D, 1)), 'b_a': jnp.zeros((1,), jnp.float32), 'W_hn': w(ks[5], (2 * D, D)), 'b_hn': jnp.zeros((D,), jnp.float32), 'W_on': w(ks[6], (2 * D, D)), 'b_on': jnp.zeros((D,), jnp.float32), 'edge_src': jax.random.randint(ks[7], (E,), 0, N, jnp.int32), 'edge_dst': jax.random.randint(ks[8], (E,), 0, N, jnp.int32)}
    _L0_gnn_all = _L0_gnn_setup()
    _L0_gnn_in = {k: v for k, v in _L0_gnn_all.items() if k in ('W_hh', 'b_hh', 'W_oo', 'b_oo', 'W_ho', 'b_ho', 'W_a', 'b_a', 'W_hn', 'b_hn', 'W_on', 'b_on')}
    del _L0_gnn_all

    def _L0_mix_setup():
        import jax, jax.numpy as jnp
        import numpy as np
        B, N, C, H = (4, 256, 1024, 16)
        D = C // H
        key = jax.random.key(seed)
        k1, k2, k3 = jax.random.split(key, 3)
        scale_in = 1.0 / np.sqrt(C)
        return {'x': jax.random.normal(k1, (B, N, C), dtype=jnp.float32), 'w_qkv': jax.random.normal(k2, (C, 3 * C), dtype=jnp.float32) * scale_in, 'b_qkv': jnp.zeros((3 * C,), dtype=jnp.float32), 'w_proj': jax.random.normal(k3, (C, C), dtype=jnp.float32) * scale_in, 'b_proj': jnp.zeros((C,), dtype=jnp.float32)}
    _L0_mix_all = _L0_mix_setup()
    _L0_mix_in = {k: v for k, v in _L0_mix_all.items() if k in ('w_qkv', 'b_qkv', 'w_proj', 'b_proj')}
    del _L0_mix_all

    def _L0_ffn_setup():
        import jax, jax.numpy as jnp
        import numpy as np
        LN_EPS = 1e-05

        def layernorm(x, g, b):
            mu = jnp.mean(x, axis=-1, keepdims=True)
            var = jnp.mean((x - mu) ** 2, axis=-1, keepdims=True)
            return (x - mu) * jax.lax.rsqrt(var + LN_EPS) * g + b

        def act_quant_fake(x):
            scale = 127.0 / jnp.clip(jnp.max(jnp.abs(x), axis=-1, keepdims=True), 1e-05)
            return jnp.clip(jnp.round(x * scale), -128.0, 127.0) / scale

        def weight_quant_fake(w):
            scale = 1.0 / jnp.clip(jnp.mean(jnp.abs(w)), 1e-05)
            return jnp.clip(jnp.round(w * scale), -1.0, 1.0) / scale

        def bitlinear(x, w, b):
            dqx = act_quant_fake(x)
            dqw = weight_quant_fake(w)
            return jnp.einsum('btd,hd->bth', dqx, dqw) + b
        key = jax.random.key(seed)
        ks = jax.random.split(key, 5)
        B, T, D, H = (8, 128, 1024, 128)
        return {'x': jax.random.normal(ks[0], (B, T, D), dtype=jnp.float32), 'ln1_g': jnp.ones((D,), jnp.float32), 'ln1_b': jnp.zeros((D,), jnp.float32), 'w1': jax.random.normal(ks[1], (H, D), dtype=jnp.float32) * (1.0 / np.sqrt(D)), 'b1': jax.random.normal(ks[2], (H,), dtype=jnp.float32) * 0.02, 'ln2_g': jnp.ones((H,), jnp.float32), 'ln2_b': jnp.zeros((H,), jnp.float32), 'w2': jax.random.normal(ks[3], (D, H), dtype=jnp.float32) * (1.0 / np.sqrt(H)), 'b2': jax.random.normal(ks[4], (D,), jnp.float32) * 0.02}
    _L0_ffn_all = _L0_ffn_setup()
    _L0_ffn_in = {k: v for k, v in _L0_ffn_all.items() if k in ('ln1_g', 'ln1_b', 'w1', 'b1', 'ln2_g', 'ln2_b', 'w2', 'b2')}
    del _L0_ffn_all
    return {'x': x, 'src': src, 'dst': dst, 'L0_gnn_W_hh': _L0_gnn_in['W_hh'], 'L0_gnn_b_hh': _L0_gnn_in['b_hh'], 'L0_gnn_W_oo': _L0_gnn_in['W_oo'], 'L0_gnn_b_oo': _L0_gnn_in['b_oo'], 'L0_gnn_W_ho': _L0_gnn_in['W_ho'], 'L0_gnn_b_ho': _L0_gnn_in['b_ho'], 'L0_gnn_W_a': _L0_gnn_in['W_a'], 'L0_gnn_b_a': _L0_gnn_in['b_a'], 'L0_gnn_W_hn': _L0_gnn_in['W_hn'], 'L0_gnn_b_hn': _L0_gnn_in['b_hn'], 'L0_gnn_W_on': _L0_gnn_in['W_on'], 'L0_gnn_b_on': _L0_gnn_in['b_on'], 'L0_mix_w_qkv': _L0_mix_in['w_qkv'], 'L0_mix_b_qkv': _L0_mix_in['b_qkv'], 'L0_mix_w_proj': _L0_mix_in['w_proj'], 'L0_mix_b_proj': _L0_mix_in['b_proj'], 'L0_ffn_ln1_g': _L0_ffn_in['ln1_g'], 'L0_ffn_ln1_b': _L0_ffn_in['ln1_b'], 'L0_ffn_w1': _L0_ffn_in['w1'], 'L0_ffn_b1': _L0_ffn_in['b1'], 'L0_ffn_ln2_g': _L0_ffn_in['ln2_g'], 'L0_ffn_ln2_b': _L0_ffn_in['ln2_b'], 'L0_ffn_w2': _L0_ffn_in['w2'], 'L0_ffn_b2': _L0_ffn_in['b2']}

def reference(x, src, dst, L0_gnn_W_hh, L0_gnn_b_hh, L0_gnn_W_oo, L0_gnn_b_oo, L0_gnn_W_ho, L0_gnn_b_ho, L0_gnn_W_a, L0_gnn_b_a, L0_gnn_W_hn, L0_gnn_b_hn, L0_gnn_W_on, L0_gnn_b_on, L0_mix_w_qkv, L0_mix_b_qkv, L0_mix_w_proj, L0_mix_b_proj, L0_ffn_ln1_g, L0_ffn_ln1_b, L0_ffn_w1, L0_ffn_b1, L0_ffn_ln2_g, L0_ffn_ln2_b, L0_ffn_w2, L0_ffn_b2):
    import jax
    import jax.numpy as jnp

    def _L0_gnn_ref(n_f, W_hh, b_hh, W_oo, b_oo, W_ho, b_ho, W_a, b_a, W_hn, b_hn, W_on, b_on, edge_src, edge_dst):
        import jax, jax.numpy as jnp
        import numpy as np
        NH, NO = (128, 384)
        N = NH + NO
        E_HH, E_OO, E_HO = (256, 1280, 512)
        E = E_HH + E_OO + E_HO
        D = 1024
        feat = jnp.concatenate([n_f[edge_src], n_f[edge_dst]], axis=1)
        e_hh = jax.nn.relu(feat[:E_HH] @ W_hh + b_hh)
        e_oo = jax.nn.relu(feat[E_HH:E_HH + E_OO] @ W_oo + b_oo)
        e_ho = jax.nn.relu(feat[E_HH + E_OO:] @ W_ho + b_ho)
        e_f = jnp.concatenate([e_hh, e_oo, e_ho], axis=0)
        logit = (e_f @ W_a + b_a)[:, 0]
        m = jax.lax.stop_gradient(jax.ops.segment_max(logit, edge_dst, num_segments=N))
        ex = jnp.exp(logit - m[edge_dst])
        den = jax.ops.segment_sum(ex, edge_dst, num_segments=N)
        alpha = ex / den[edge_dst]
        z_f = jax.ops.segment_sum(alpha[:, None] * n_f[edge_src], edge_dst, num_segments=N)
        nf2 = jnp.concatenate([n_f, z_f], axis=1)
        h_new = jax.nn.relu(nf2[:NH] @ W_hn + b_hn)
        o_new = jax.nn.relu(nf2[NH:] @ W_on + b_on)
        return jnp.concatenate([h_new, o_new], axis=0)

    def _L0_mix_ref(x, w_qkv, b_qkv, w_proj, b_proj):
        import jax, jax.numpy as jnp
        import numpy as np
        B, N, C, H = (4, 256, 1024, 16)
        D = C // H
        Bx, Nx, Cx = x.shape
        qkv = x @ w_qkv + b_qkv
        qkv = qkv.reshape(Bx, Nx, 3, H, D)
        qkv = jnp.transpose(qkv, (2, 0, 3, 1, 4))
        q, k, v = (qkv[0], qkv[1], qkv[2])
        q = jax.nn.elu(q) + 1.0
        k = jax.nn.elu(k) + 1.0
        kv = jnp.einsum('bhnd,bhne->bhde', k, v)
        out = jnp.einsum('bhnd,bhde->bhne', q, kv)
        z = 1.0 / (jnp.einsum('bhnd,bhd->bhn', q, k.sum(axis=2)) + 1e-08)
        out = out * z[..., None]
        out = jnp.transpose(out, (0, 2, 1, 3)).reshape(Bx, Nx, Cx)
        out = out @ w_proj + b_proj
        return out

    def _L0_ffn_ref(x, ln1_g, ln1_b, w1, b1, ln2_g, ln2_b, w2, b2):
        import jax, jax.numpy as jnp
        import numpy as np
        LN_EPS = 1e-05

        def layernorm(x, g, b):
            mu = jnp.mean(x, axis=-1, keepdims=True)
            var = jnp.mean((x - mu) ** 2, axis=-1, keepdims=True)
            return (x - mu) * jax.lax.rsqrt(var + LN_EPS) * g + b

        def act_quant_fake(x):
            scale = 127.0 / jnp.clip(jnp.max(jnp.abs(x), axis=-1, keepdims=True), 1e-05)
            return jnp.clip(jnp.round(x * scale), -128.0, 127.0) / scale

        def weight_quant_fake(w):
            scale = 1.0 / jnp.clip(jnp.mean(jnp.abs(w)), 1e-05)
            return jnp.clip(jnp.round(w * scale), -1.0, 1.0) / scale

        def bitlinear(x, w, b):
            dqx = act_quant_fake(x)
            dqw = weight_quant_fake(w)
            return jnp.einsum('btd,hd->bth', dqx, dqw) + b
        h = layernorm(x, ln1_g, ln1_b)
        h = bitlinear(h, w1, b1)
        h = jax.nn.gelu(h, approximate=False)
        h = layernorm(h, ln2_g, ln2_b)
        h = bitlinear(h, w2, b2)
        return h
    xn = _layernorm(x, axis=-1)
    x = x + _L0_gnn_ref(xn, L0_gnn_W_hh, L0_gnn_b_hh, L0_gnn_W_oo, L0_gnn_b_oo, L0_gnn_W_ho, L0_gnn_b_ho, L0_gnn_W_a, L0_gnn_b_a, L0_gnn_W_hn, L0_gnn_b_hn, L0_gnn_W_on, L0_gnn_b_on, src, dst) + _L0_mix_ref(xn[None], L0_mix_w_qkv, L0_mix_b_qkv, L0_mix_w_proj, L0_mix_b_proj)[0]
    x = x + _L0_ffn_ref(_layernorm(x, axis=-1)[None], L0_ffn_ln1_g, L0_ffn_ln1_b, L0_ffn_w1, L0_ffn_b1, L0_ffn_ln2_g, L0_ffn_ln2_b, L0_ffn_w2, L0_ffn_b2)[0]
    return x

_drawn_inputs = setup_inputs


def setup_inputs(seed=0):
    import zlib

    import numpy as np

    out = dict(_drawn_inputs(seed))
    spreads = {'L0_gnn_b_hh': (0.0, 0.8),
     'L0_gnn_b_oo': (0.0, 0.8),
     'L0_gnn_b_ho': (0.0, 0.8),
     'L0_gnn_b_hn': (0.0, 0.287),
     'L0_gnn_b_on': (0.0, 0.1),
     'L0_mix_b_qkv': (0.0, 0.1),
     'L0_mix_b_proj': (0.0, 0.1),
     'L0_ffn_ln1_g': (1.0, 0.2),
     'L0_ffn_ln1_b': (0.0, 0.1),
     'L0_ffn_ln2_g': (1.0, 0.2),
     'L0_ffn_ln2_b': (0.0, 0.1)}
    factors = {'L0_gnn_W_hh': 8.0, 'L0_gnn_W_oo': 6.434, 'L0_ffn_b1': 3.599, 'L0_ffn_b2': 3.769}
    for name, (base, spread) in spreads.items():
        noise = np.random.default_rng([zlib.crc32(name.encode()), seed]).standard_normal(out[name].shape)
        drawn = base * np.exp(spread * noise) if base else spread * noise
        out[name] = jnp.asarray(drawn.astype(out[name].dtype))
    for name, factor in factors.items():
        out[name] = (out[name] * factor).astype(out[name].dtype)
    return out
```

```python
import numpy as np

import concourse.bass as bass
from concourse import mybir

F32 = mybir.dt.float32
F32R = mybir.dt.float32r
BF16 = mybir.dt.bfloat16
FP16 = mybir.dt.float16
I32 = mybir.dt.int32
U32 = mybir.dt.uint32
ALU = mybir.AluOpType
ACT = mybir.ActivationFunctionType
AX = mybir.AxisListType
RMAX = bass.bass_isa.ReduceOp.max
RADD = bass.bass_isa.ReduceOp.add

P = 128
N = 512
D = 1024
H = 128
HEADS = 16
HD = D // HEADS
MT = N // P
KT = D // P
CW = 512
HALF = KT * CW // 2
E = 8192
ET = E // P
E_HH, E_OO = 256, 1280
T_HO = (E - E_HH - E_OO) // P
T_OO = E_OO // P
LN_EPS = 1e-5
ROUND = 12582912.0
NEG = -3.0e38

TABLES = 8
(HN0, HN1, HHT0, HHB0, HHT1, HHB1, K0, V0, K1, V1, Q0, Q1, ON0, ON1, PR0, PR1,
 BHN0, BHN1, BON0, BON1) = range(TABLES, TABLES + 20)
CHUNKS = TABLES + 20
BIASED = [c for c in range(TABLES) if c % 4 < 2] + [HN0, HN1, HHT0, HHT1, K0, V0, K1, V1, ON0, ON1, PR0, PR1]
STORED = list(range(TABLES)) + [HN0, HN1, ON0, ON1, PR0, PR1]
HH = (HHT0, HHB0, HHT1, HHB1)
ROWS = {c: list(range(MT)) for c in range(CHUNKS)}
ROWS.update({c: [0] for c in (HN0, HN1, BHN0, BHN1)})
ROWS.update({c: [1, 2, 3] for c in (ON0, ON1, BON0, BON1)})
ROWS.update({c: [0, 1] for c in HH})
FIRST = {}
_n = 0
for _c in range(CHUNKS):
    FIRST[_c] = _n
    _n += len(ROWS[_c])
T_GATHERED = T_HO + T_OO
PAIRS = {4: 2, 5: 2, 6: 2, 7: 2, HN0: 0, HN1: 1, HHT0: 1, HHB0: 1, HHT1: 1, HHB1: 1, K0: 2, V0: 3, K1: 2, V1: 3,
         Q0: 2, Q1: 2, ON0: 2, ON1: 2, PR0: 0}
assert sum(PAIRS.values()) * 2 <= T_GATHERED
PAIRS[PR0] = T_GATHERED // 2 - sum(PAIRS.values())


def slot_of(t):
    return t % 4 if t < T_HO else (t - T_HO) % 3


def fills(t):
    return sum(slot_of(u) == slot_of(t) for u in range(t + 1))


def slot_before(t):
    return max(u for u in range(t) if slot_of(u) == slot_of(t))


HEAD = 4


POWERS = [(0, "r1"), (0, "r2"), (1, "r1"), (1, "r2"), (0, "r3"), (2, "r1"), (2, "r2"), (1, "r3"),
          (3, "r1"), (3, "r2"), (2, "r3"), (3, "r3")]


USES = [("k", a, j) for a in range(2) for j in range(4)] + [("q", 0, j) for j in range(4)] + \
       [("q", 1, 0), ("q", 1, 1), ("q", 1, 2), ("z", 0, 0), ("z", 0, 1), ("q", 1, 3), ("z", 0, 2), ("z", 0, 3)] + \
       [("z", 1, j) for j in range(4)]
ATTEND = {(Q1, 2): [(0, 0), (0, 1)], (Q1, 3): [(0, 2), (0, 3)], (ON0, 2): [(1, 0), (1, 1)], (ON1, 0): [(1, 2), (1, 3)]}
DEN8 = {(Q1, 0): 0, (ON0, 0): 1}


def build(nc, x, src, dst, wt, bias_rows, bq, w_a, b_a, ln1_g, ln1_b, w1, b1, ln2_g, ln2_b, w2, b2, out):
    xn_d = nc.dram_tensor("xn_scratch", (MT, P, D), F32, kind="Internal").ap()
    table_d = nc.dram_tensor("edge_tables", (2 * 2 * N, D), F32, kind="Internal").ap()
    table_tiles = table_d.rearrange("(b m p) d -> b m p d", m=MT, p=P)
    top_d = nc.dram_tensor("node_top", (MT, P, D), F32, kind="Internal").ap()
    mix_d = nc.dram_tensor("mix_out", (MT, P, D), F32, kind="Internal").ap()

    place = [16512]

    def region(nbytes):
        at = place[0]
        place[0] += (nbytes + 31) // 32 * 32
        assert place[0] <= 229344, place[0]
        return at

    def sb(name, shape, dt, at=None):
        size = int(np.prod(shape[1:])) * mybir.dt.size(dt)
        return nc.alloc_sbuf_tensor_at(name, shape, dt, offset=region(size) if at is None else at)

    xT_hi = sb("xT_hi", [P, KT, N], F32R)
    xT_lo = sb("xT_lo", [P, KT, N], F32R)
    raw = sb("w_raw", [P, 2, HALF], F32)
    w_hi = sb("w_hi", [P, 2, KT * CW], F32R)
    w_lo = sb("w_lo", [P, 2, KT * CW], F32R)
    at_b = region(16384)
    w1_raw = sb("w1_raw", [P, D], F32, at_b)
    w2_raw = sb("w2_raw", [P, KT, H], F32, at_b + 4096)
    wq_tmp = sb("wq_tmp", [P, D], F32, at_b + 8192)
    feat_raw = sb("feat_raw", [P, 2, 2, D], F32, at_b)
    feat_dst_hi = sb("feat_dst_hi", [P, KT, E_HH], F32R, at_b)
    feat_dst_lo = sb("feat_dst_lo", [P, KT, E_HH], F32R, at_b + 8192)
    kbuf = sb("kbuf", [P, MT, CW], F32, at_b)
    vbuf = sb("vbuf", [P, MT, CW], F32, at_b + 8192)
    qT1 = sb("qT1", [P, 4, N], F32, at_b)
    xn_raw = sb("xn_raw", [P, MT, D], F32, at_b)
    top = sb("top", [P, MT, D], F32, at_b)
    q8 = [sb(f"q8_{m}", [P, D], BF16, at_b + 4096 * m) for m in range(MT)]
    q8T = [sb(f"q8T_{m}", [P, KT, P], BF16, at_b + 4096 * m + 2048) for m in range(MT)]
    at_edge = region(4096 + 2048)
    wa_bc = sb("wa_bc", [P, D], F32, at_edge)
    other = sb("other_node", [P, 2, N], BF16, at_edge + 4096)
    hot_src = sb("hot_src", [P, 2, N], FP16, at_edge)
    hot_hi = sb("hot_hi", [P, 2, N], FP16, at_edge + 2048)
    hot_lo = sb("hot_lo", [P, 2, N], FP16, at_edge + 4096)
    hot_z = sb("z_scaled_T", [P, 2, N], F32, at_edge)
    at_stage = region(4096)
    stage = sb("stage", [P, 2, CW], F32, at_stage)
    y1 = [sb(f"y1_{m}", [P, H], F32, at_stage + 1024 * m) for m in range(MT)]
    y2 = [sb(f"y2_{m}", [P, H], F32, at_stage + 1024 * m + 512) for m in range(MT)]
    at_big = region(32768)
    x_in = sb("x_in", [P, MT, D], F32, at_big)
    xn = sb("xn", [P, MT, D], F32, at_big + 16384)
    gp = sb("gathered_src", [P, 4, D], F32, at_big)
    gq = sb("gathered_dst", [P, 4, D], F32, at_big + 16384)
    xn_hi = sb("xn_hi", [P, MT, D], F32R, at_big)
    xn_lo = sb("xn_lo", [P, MT, D], F32R, at_big + 16384)
    x2 = sb("x2", [P, MT, D], F32, at_big)
    hbuf = sb("hbuf", [P, MT, D], F32, at_big + 16384)
    at_q = region(8192)
    feat_src_hi = sb("feat_src_hi", [P, KT, E_HH], F32R, at_q)
    qT0 = sb("qT0", [P, 4, N], F32, at_q)
    AT_hi = sb("AT_hi", [P, MT, N], F32R, at_q)
    g1_bc = sb("g1_bc", [P, D], F32, at_q)
    bb1_bc = sb("bb1_bc", [P, D], F32, at_q + 4096)
    oT_hi = [sb(f"oT_hi{k}", [P, N], F32R, (at_b + 8192, at_big + 3 * 4096, at_big + 7 * 4096)[(k >= 4) + (k >= 6)] + 2048 * (k % 4 if k < 4 else k % 2))
             for k in range(KT)]
    oT_lo = [sb(f"oT_lo{k}", [P, N], F32R, (at_q, at_b)[k // 4] + 2048 * (k % 4)) for k in range(KT)]
    at_kv = region(8192)
    feat_src_lo = sb("feat_src_lo", [P, KT, E_HH], F32R, at_kv)
    tmp = sb("tmp", [P, 2, N], F32, at_kv)
    kvb = sb("kvb", [P, KT, P], F32, at_kv + 4096)
    AT_lo = sb("AT_lo", [P, MT, N], F32R, at_kv)
    b2_bc = sb("b2_bc", [P, D], F32, at_kv)
    b1_bc = sb("b1_bc", [P, H], F32, at_kv + 4096)
    g2_bc = sb("g2_bc", [P, H], F32, at_kv + 4608)
    bb2_bc = sb("bb2_bc", [P, H], F32, at_kv + 5120)
    at_braw = region(2048)
    b_raw = sb("b_raw", [P, CW], F32, at_braw)
    q2 = [sb(f"q2_{m}", [P, H], BF16, at_braw + 512 * m) for m in range(MT)]
    q2T = [sb(f"q2T_{m}", [P, P], BF16, at_braw + 512 * m + 256) for m in range(MT)]
    at_bhl = region(4096)
    b_hl = sb("b_hl", [P, 2, CW], F32R, at_bhl)
    at_run = region(4096)
    run = sb("running_max", [P, N], F32, at_run)
    m_bc = sb("max_bc", [P, N], F32, at_run + 2048)
    den_tmp = sb("den_tmp", [P, N], F32, at_run)
    rden = sb("rden", [P, N], F32, at_run + 2048)
    iota = sb("iota", [P, N], FP16)
    junk = sb("junk", [P, 1], F32)
    ks8 = sb("ks8", [P, KT * 8], F32)
    rz = sb("rz", [P, N], F32, at_braw)[64:72, :]
    sel8 = sb("sel8", [P, 4, P], F32, at_bhl)[64:72, :, :]
    ident = sb("ident", [P, P], F32)
    ident16 = sb("ident16", [P, P], BF16)
    ones_b = sb("ones_b", [64, P], F32R)
    ones_r = sb("ones_r", [P, P], F32R)
    ones2 = sb("ones2", [P, 2], F32)
    zeros = sb("zeros", [P, P], FP16)
    w1T = sb("w1T", [P, KT, H], BF16)
    w2T = sb("w2T", [P, D], BF16)
    src_i = sb("src_i", [P, ET], I32)
    dst_i = sb("dst_i", [P, ET], I32)
    src_f = sb("src_f", [P, ET], F32)
    dst_f = sb("dst_f", [P, ET], F32)
    src_row = sb("src_row", [P, ET], I32)
    dst_row = sb("dst_row", [P, ET], I32)
    idx_now = sb("idx_now", [P, 2, 2, 4], I32)
    logit_hh = sb("logit_hh", [P, 2, 2], F32)
    logit = sb("logit", [P, ET], F32)
    mx_e = sb("max_of_edge", [P, ET], F32)
    ex = sb("ex", [P, ET], F32)
    ex16 = sb("ex16", [P, ET], FP16)
    ex_hi = sb("ex_hi", [P, ET], F32)
    ex_lo = sb("ex_lo", [P, ET], F32)
    bq_sb = sb("bq_sb", [P, KT], F32)
    nbq = sb("nbq", [P, KT], F32)
    ba_sb = sb("ba_sb", [P, 1], F32)
    eps_c = sb("eps_c", [P, 1], F32)
    nhalf = sb("nhalf", [P, MT], F32)
    stats = sb("stats", [P, MT, 2, 6], F32)
    mv = sb("mv", [P, MT, 2], F32)
    sm = sb("small", [P, 16, MT], F32)
    wsum = sb("wsum", [P, 2], F32)
    wtot = sb("wtot", [P, 2], F32)
    wmean = sb("wmean", [P, 2], F32)
    wscale = sb("wscale", [P, 2], F32)
    wback = sb("wback", [P, 2], F32)
    mv2 = sb("mv2", [P, MT, 2], F32)

    bank = [nc.alloc_psum_tensor(f"bank{i}", [P, CW], F32) for i in range(8)]

    def sem(name):
        return nc.alloc_semaphore(name)

    x_loaded = [sem(f"x_loaded{m}") for m in range(MT)]
    small_loaded = sem("small_loaded")
    w12_loaded = sem("w12_loaded")
    raw_loaded = [sem(f"raw_loaded{h}") for h in range(2)]
    bias_loaded = sem("bias_loaded")
    consts_ready = sem("consts_ready")
    dve_consts = sem("dve_consts")
    idx_ready = sem("idx_ready")
    rstd_asked = sem("rstd_asked")
    rstd_done = sem("rstd_done")
    xn_ready = sem("xn_ready")
    xn_stored = sem("xn_stored")
    xT_psum = sem("xT_psum")
    xT_hi_done = sem("xT_hi_done")
    xT_lo_done = sem("xT_lo_done")
    w_hi_done = sem("w_hi_done")
    w_lo_done = sem("w_lo_done")
    bias_hi_done = sem("bias_hi_done")
    bias_lo_done = sem("bias_lo_done")
    prod_ready = sem("prod_ready")
    evac_done = sem("evac_done")
    stage_stored = [sem(f"stage_stored{s}") for s in range(2)]
    feat_gathered = sem("feat_gathered")
    feat_psum = sem("feat_psum")
    feat_hi_done = sem("feat_hi_done")
    feat_lo_done = sem("feat_lo_done")
    hh_read = sem("hh_read")
    kv_cleared = sem("kv_cleared")
    wsum_done = sem("wsum_done")
    wtot_done = sem("wtot_done")
    wq_done = sem("wq_done")
    wqT_psum = sem("wqT_psum")
    wqT_done = sem("wqT_done")
    idx_copied = sem("idx_copied")
    gathered = [sem(f"gathered{s}") for s in range(4)]
    edge_sum = sem("edge_sum")
    edge_dot = sem("edge_dot")
    edge_mask = sem("edge_mask")
    edge_max = sem("edge_max")
    kq_exp_done = sem("kq_exp_done")
    tmp_used = sem("tmp_used")
    v_done = sem("v_done")
    kv_psum = sem("kv_psum")
    kvb_done = sem("kvb_done")
    ks_done = sem("ks_done")
    den8_psum = sem("den8_psum")
    rz_done = sem("rz_done")
    att_psum = sem("att_psum")
    zb_copied = sem("zb_copied")
    oT_hi_done = sem("oT_hi_done")
    oT_lo_done = sem("oT_lo_done")
    max_done = sem("max_done")
    mx_gathered = sem("mx_gathered")
    ex_asked = sem("ex_asked")
    ex_done = sem("ex_done")
    hot_done = sem("hot_done")
    hot_used = sem("hot_used")
    A_psum = sem("A_psum")
    A_hi_done = sem("A_hi_done")
    A_lo_done = sem("A_lo_done")
    den_psum = sem("den_psum")
    z_psum = sem("z_psum")
    z_scaled = sem("z_scaled")
    z_hi_done = sem("z_hi_done")
    z_lo_done = sem("z_lo_done")
    xnr_loaded = sem("xnr_loaded")
    xn_hi_done = sem("xn_hi_done")
    xn_lo_done = sem("xn_lo_done")
    mix_loaded = sem("mix_loaded")
    top_loaded = sem("top_loaded")
    bc_loaded = sem("bc_loaded")
    xm_done = sem("xm_done")
    bot_evac = sem("bot_evac")
    x2_done = sem("x2_done")
    xb_done = sem("xb_done")
    q_ready = sem("q_ready")
    qT_psum = sem("qT_psum")
    qT_done = sem("qT_done")
    y_psum = sem("y_psum")
    y_read = sem("y_read")
    gelu_done = sem("gelu_done")
    q2_ready = sem("q2_ready")
    q2T_psum = sem("q2T_psum")
    q2T_done = sem("q2T_done")
    o_psum = sem("o_psum")
    o_done = sem("o_done")
    out_stored = sem("out_stored")
    pool_turn = sem("pool_turn")
    dve_step = sem("dve_step")
    act_step = sem("act_step")
    pool_step = sem("pool_step")

    qT = (qT0, qT1)
    xT, feat_src, feat_dst = ([[t[:, k, :] for k in range(KT)] for t in pair]
                              for pair in ((xT_hi, xT_lo), (feat_src_hi, feat_src_lo), (feat_dst_hi, feat_dst_lo)))
    oT = [[t[:, :] for t in half] for half in (oT_hi, oT_lo)]
    ZT = [hot_z[:, k % 2, :] for k in range(KT)]

    def f32(ap):
        return ap.bitcast(F32)

    def use_of(kind, a, j):
        return USES.index((kind, a, j))

    def bias_no(c):
        return sum(b < c for b in BIASED)

    def evac_no(c, i):
        return FIRST[c] + i + 1 - sum(len(ROWS[b]) for b in HH if b < c)

    bank_of, bank_free, last = {}, {}, {}
    turn = 0
    for c in range(BHN0):
        for i in range(len(ROWS[c])):
            if c in (HHB0, HHB1):
                bank_of[c, i] = bank_of[c - 1, i]
                bank_free[c, i] = None
                last[bank_of[c, i]] = ("hh", 2 * (c == HHB1) + i + 1)
            else:
                b = bank_of[c, i] = turn % 4
                turn += 1
                bank_free[c, i] = last.get(b)
                last[b] = ("act", evac_no(c, i))

    def stored_no(c):
        return sum(len(ROWS[b]) for b in STORED if b < c)

    block_cm = nc.Block()
    block = block_cm.__enter__()

    @block.sync
    def _(sp):
        for m in range(MT):
            sp.dma_start(x_in[:, m, :], x[m]).then_inc(x_loaded[m], 16)

        def load_half(c, h):
            sp.dma_start(raw[:, h, :], wt[c, :, h * HALF:(h + 1) * HALF]).then_inc(raw_loaded[h], 16)

        def load_bias(b):
            for row in (0, 32):
                sp.dma_start(b_raw[row:row + 1, :], bias_rows[b]).then_inc(bias_loaded, 16)

        def store(n_tile, slot, dram):
            sp.wait_ge(evac_done, n_tile + HEAD)
            sp.dma_start(dram, stage[:, slot, :]).then_inc(stage_stored[slot], 16)

        load_half(0, 0)
        load_half(0, 1)
        sp.wait_ge(dve_consts, 1)
        load_bias(0)
        sp.dma_start(w1_raw[:, :], w1).then_inc(w12_loaded, 16)
        sp.dma_start(w2_raw[:, :, :], w2).then_inc(w12_loaded, 16)
        for h in range(2):
            sp.wait_ge(w_lo_done, h + 1)
            load_half(1, h)
        sp.wait_ge(bias_lo_done, 1)
        load_bias(1)
        for m in range(MT):
            sp.wait_ge(xn_ready, m + 1)
            sp.dma_start(xn_d[m], xn[:, m, :]).then_inc(xn_stored, 16)

        with sp.Fori(0, TABLES // 4) as i:
            for cc in range(4):
                c = i * 4 + cc
                for h in range(2):
                    sp.wait_ge(w_lo_done, i * 8 + (2 * (cc + 1) + h + 1))
                    load_half(c + 2, h)
                if cc >= 2:
                    sp.wait_ge(bias_lo_done, i * 2 + cc)
                    load_bias(i * 2 + cc)
                for m in range(MT):
                    store(i * 16 + (4 * cc + m + 1), m % 2,
                          table_tiles[i * 2 + cc // 2, m, :, (cc % 2) * CW:(cc % 2 + 1) * CW])
        for c in range(TABLES, PR1 + 1):
            if c + 2 <= BHN1:
                if c + 2 == BHN1:
                    break
                for h in range(2):
                    sp.wait_ge(w_lo_done, 2 * (c + 1) + h + 1)
                    load_half(c + 2, h)
                if c + 2 in BIASED:
                    sp.wait_ge(bias_lo_done, bias_no(c + 2))
                    load_bias(bias_no(c + 2))
            if c in STORED:
                dram = mix_d if c in (PR0, PR1) else top_d
                col = 0 if c in (HN0, ON0, PR0) else CW
                for i, m in enumerate(ROWS[c]):
                    s = (stored_no(c) + i) % 2
                    store(evac_no(c, i), s, dram[m, :, col:col + CW])
        for i, m in enumerate(ROWS[PR1]):
            store(evac_no(PR1, i), (stored_no(PR1) + i) % 2, mix_d[m, :, CW:D])
        sp.wait_ge(prod_ready, FIRST[BHN0] + HEAD)
        sp.wait_ge(xn_stored, 16 * MT)
        for m in range(MT):
            sp.dma_start(xn_raw[:, m, :], xn_d[m]).then_inc(xnr_loaded, 16)
        for c in (BHN1, BON0):
            for h in range(2):
                sp.wait_ge(w_lo_done, 2 * (c - 1) + h + 1)
                load_half(c, h)
        for s in range(2):
            sp.wait_ge(stage_stored[s], 16 * (stored_no(PR1 + 1) // 2))
        sp.wait_ge(xn_lo_done, MT)
        for m in range(MT):
            sp.dma_start(top[:, m, :], top_d[m]).then_inc(top_loaded, 16)
        sp.wait_ge(z_psum, KT)
        sp.dma_start(g1_bc[:, :], ln1_g.partition_broadcast(P)).then_inc(bc_loaded, 16)
        sp.dma_start(bb1_bc[:, :], ln1_b.partition_broadcast(P)).then_inc(bc_loaded, 16)
        for m in range(MT):
            sp.dma_start(x2[:, m, :], mix_d[m]).then_inc(mix_loaded, 16)
            sp.dma_start(hbuf[:, m, :], x[m]).then_inc(mix_loaded, 16)
        sp.dma_start(b2_bc[:, :], b2.partition_broadcast(P)).then_inc(bc_loaded, 16)
        sp.dma_start(b1_bc[:, :], b1.partition_broadcast(P)).then_inc(bc_loaded, 16)
        sp.dma_start(g2_bc[:, :], ln2_g.partition_broadcast(P)).then_inc(bc_loaded, 16)
        sp.dma_start(bb2_bc[:, :], ln2_b.partition_broadcast(P)).then_inc(bc_loaded, 16)
        for h in range(2):
            sp.wait_ge(w_lo_done, 2 * BON0 + h + 1)
            load_half(BON1, h)
        for m in range(MT):
            sp.wait_ge(o_done, 2 * (m + 1))
            sp.dma_start(out[m], hbuf[:, m, :]).then_inc(out_stored, 16)
        sp.wait_ge(out_stored, 16 * MT)

    @block.gpsimd
    def _(pool):
        pool.memset(ident[:, :], 0.0).then_inc(pool_step, 1)
        pool.memset(ident16[:, :], 0.0).then_inc(pool_step, 1)
        pool.iota(iota[:, :], pattern=[[1, N]], base=0, channel_multiplier=0,
                  allow_small_or_imprecise_dtypes=True).then_inc(consts_ready, 1)
        pool.memset(nhalf[:, :], -0.5).then_inc(consts_ready, 1)
        pool.wait_ge(pool_step, 2)
        pool.affine_select(out=ident[:, :], in_=ident[:, :], compare_op=ALU.not_equal, fill=1.0,
                           base=0, pattern=[[-1, P]], channel_multiplier=1).then_inc(consts_ready, 1)
        pool.affine_select(out=ident16[:, :], in_=ident16[:, :], compare_op=ALU.not_equal, fill=1.0,
                           base=0, pattern=[[-1, P]], channel_multiplier=1).then_inc(consts_ready, 1)
        pool.wait_ge(dve_consts, 1)
        pool.wait_ge(consts_ready, 4)
        sel_v = sel8.rearrange("r j (g e) -> r j g e", g=2)
        pool.affine_select(out=sel_v, in_=sel_v, compare_op=ALU.not_equal, fill=1.0,
                           base=0, pattern=[[-2, 4], [-1, 2], [0, HD]], channel_multiplier=1).then_inc(consts_ready, 1)
        pool.wait_ge(consts_ready, 5)
        for m in range(MT):
            pool.wait_ge(rstd_asked, m + 1)
            pool.tensor_tensor(sm[:, 1, m:m + 1], sm[:, 0, m:m + 1], nhalf[:, 0:1], ALU.pow).then_inc(rstd_done, 1)
        pool.wait_ge(wsum_done, 2)
        pool.partition_all_reduce(wtot[:, :], wsum[:, :], P, RADD).then_inc(wtot_done, 1)

        pool.wait_ge(idx_ready, 1)
        pool.wait_ge(wq_done, 2)
        pool.wait_ge(xn_stored, 16 * MT)
        for side, index in enumerate((src_i, dst_i)):
            for u in range(2):
                pool.indirect_dma_start(
                    feat_raw[:, side, u, :], None, xn_d.rearrange("m p d -> (m p) d"),
                    bass.IndirectOffsetOnAxis(ap=index[:, T_GATHERED + u:T_GATHERED + u + 1].bitcast(U32), axis=0),
                ).then_inc(feat_gathered, 16)
        for s in range(2):
            pool.wait_ge(stage_stored[s], 16 * (4 * MT // 2))

        def gather_tile(s, cols, rows):
            for buf, index in zip((gp, gq), cols):
                pool.indirect_dma_start(
                    buf[:, s, :], None, table_d[0:rows, :],
                    bass.IndirectOffsetOnAxis(ap=index.bitcast(U32), axis=0),
                ).then_inc(gathered[s], 16)

        with pool.Fori(0, T_HO // 8) as i:
            for b in range(2):
                pool.wait_ge(edge_dot, i * 8 + (4 * b + 4))
                pool.sem_inc(pool_turn, 1)
                pool.tensor_copy(idx_now[:, b, 0, :], src_row[:, bass.ds(i * 8 + 4 * b, 4)]).then_inc(idx_copied, 1)
                pool.tensor_copy(idx_now[:, b, 1, :], dst_row[:, bass.ds(i * 8 + 4 * b, 4)]).then_inc(idx_copied, 1)
                pool.wait_ge(idx_copied, i * 4 + 2 * (b + 1))
                pool.sem_inc(pool_turn, 1)
                for u in range(4):
                    pool.wait_ge(edge_dot, i * 8 + (4 * b + u + 5))
                    pool.sem_inc(pool_turn, 1)
                    gather_tile(u, [idx_now[:, b, side, u:u + 1] for side in range(2)], 2 * N)
        for t in range(T_HO // 8 * 8, T_GATHERED):
            if t == T_HO:
                for s in range(2):
                    pool.wait_ge(stage_stored[s], 16 * (TABLES * MT // 2))
            pool.wait_ge(edge_dot, slot_before(t) + 1 + 8)
            gather_tile(slot_of(t), [src_row[:, t:t + 1], dst_row[:, t:t + 1]], 2 * N if t < T_HO else 4 * N)

        pool.wait_ge(edge_max, ET)
        pool.partition_all_reduce(m_bc[:, :], run[:, :], P, RMAX).then_inc(max_done, 1)
        for m in range(MT):
            pool.wait_ge(xn_hi_done, m + 1)
            pool.tensor_tensor(xn_lo[:, m, :], xn_raw[:, m, :], f32(xn_hi[:, m, :]), ALU.subtract).then_inc(xn_lo_done, 1)
        for m in range(MT):
            pool.wait_ge(mix_loaded, 32 * MT)
            pool.tensor_tensor(x2[:, m, :], x2[:, m, :], hbuf[:, m, :], ALU.add).then_inc(xm_done, 1)

        def power(n):
            pool.wait_ge(rstd_asked, n + MT + 1)
            m, which = POWERS[n]
            src_c, dst_c = {"r1": (0, 1), "r2": (2, 3), "r3": (8, 9)}[which]
            pool.tensor_tensor(sm[:, dst_c, m:m + 1], sm[:, src_c, m:m + 1], nhalf[:, 0:1], ALU.pow).then_inc(rstd_done, 1)

        for n, (m, which) in enumerate(POWERS):
            power(n)
            if which == "r2":
                pool.wait_ge(bc_loaded, 16 * 6)
                pool.wait_ge(x2_done, m + 1)
                pool.tensor_tensor(x2[:, m, :], x2[:, m, :], b2_bc[:, :], ALU.add).then_inc(xb_done, 1)

    @block.scalar
    def _(act):
        act.sem_inc(evac_done, HEAD)
        act.dma_start(src_i[:, :], src).then_inc(small_loaded, 16)
        act.dma_start(dst_i[:, :], dst).then_inc(small_loaded, 16)
        act.dma_start(bq_sb[:, :], bq).then_inc(small_loaded, 16)
        act.dma_start(ba_sb[:, :], b_a.partition_broadcast(P)).then_inc(small_loaded, 16)
        act.dma_start(wa_bc[:, :], w_a.partition_broadcast(P)).then_inc(small_loaded, 16)
        steps = [0]

        def step(ins):
            steps[0] += 1
            ins.then_inc(act_step, 1)
            act.wait_ge(act_step, steps[0])

        def split_hi(loaded, prod, slot, bias=None):
            act.wait_ge(prod_ready, prod)
            for h in range(2):
                act.wait_ge(raw_loaded[h], loaded)
                act.activation(w_hi[:, slot, h * HALF:(h + 1) * HALF], raw[:, h, :], ACT.Copy).then_inc(w_hi_done, 1)
            if bias is not None:
                n, bs = bias
                act.wait_ge(bias_loaded, n * 32 + 32)
                act.activation(b_hl[0:64, bs, :], b_raw[0:64, :], ACT.Copy).then_inc(bias_hi_done, 1)

        def split_chunk(c):
            split_hi(16 * (c + 1), FIRST[c - 1] + HEAD, c % 2, (bias_no(c), bias_no(c) % 2) if c in BIASED else None)

        act.wait_ge(dve_consts, 1)
        split_hi(16, HEAD, 0, (0, 0))
        for k in range(KT):
            act.wait_ge(xT_psum, k + 1)
            act.activation(xT_hi[:, k, :], bank[k][:, :], ACT.Copy).then_inc(xT_hi_done, 1)

        def evac_stage(n, slot, free, b):
            act.wait_ge(prod_ready, n + 1 + HEAD)
            if not (isinstance(free, int) and free == 0):
                act.wait_ge(stage_stored[slot], free)
            act.activation(stage[:, slot, :], bank[b][:, :], ACT.Copy).then_inc(evac_done, 1)

        def four_tables(i):
            for cc in range(4):
                nb = {3: i * 2 + 2, 0: i * 2 + 1}.get(cc)
                split_hi(i * 64 + 16 * (cc + 2), i * 16 + (4 * cc + HEAD), (cc + 1) % 2,
                         None if nb is None else (nb, {3: 0, 0: 1}[cc]))
                for m in range(MT):
                    evac_stage(i * 16 + (4 * cc + m), m % 2, i * 128 + 16 * ((4 * cc + m) // 2), m)

        four_tables(0)
        with act.Fori(1, TABLES // 4) as i:
            four_tables(i)

        def split_feat(side):
            dest = (feat_src_hi, feat_dst_hi)[side]
            act.wait_ge(feat_psum, side + 1)
            for b in range(4):
                act.activation(dest[:, 2 * b:2 * b + 2, :].rearrange("p k e -> p (k e)"), bank[4 + b][:, :], ACT.Copy).then_inc(feat_hi_done, 1)

        def copy_mlp_weights():
            for n, (b, dest) in enumerate(((4, w1T[:, :, :].rearrange("p k h -> p (k h)")), (5, w2T[:, :]))):
                act.wait_ge(wqT_psum, n + 1)
                act.activation(dest, bank[b][:, :].bitcast(BF16), ACT.Copy).then_inc(wqT_done, 1)

        def positive_part(c, i, use, dest, **by):
            t, ps = tmp[:, use % 2, :], bank[bank_of[c, i]][:, :]
            act.wait_ge(prod_ready, FIRST[c] + i + 1 + HEAD)
            if use >= 2:
                act.wait_ge(tmp_used, use - 1)
            neg = by.get("neg", 0.0)
            step(act.activation(t, ps, ACT.Relu, scale=-1.0, bias=neg))
            act.activation(dest, ps, ACT.Relu, bias=by.get("pos", 0.0)).then_inc(evac_done, 1)
            act.activation(t, t, ACT.Exp, scale=-1.0).then_inc(kq_exp_done, 1)

        def copy_kv(a):
            act.wait_ge(kv_psum, a + 1)
            act.wait_ge(kv_cleared, 1)
            pv = bank[6][:, :].rearrange("p (j e) -> p j e", j=4)
            for g in range(2):
                r = slice(64 * g, 64 * g + 64)
                act.activation(kvb[r, 4 * a:4 * a + 4, r], pv[r, :, r], ACT.Copy).then_inc(kvb_done, 1)

        def attend(a, j):
            u = use_of("z", a, j)
            act.wait_ge(att_psum, 4 * a + j + 1)
            act.wait_ge(tmp_used, u - 1)
            act.activation(tmp[:, u % 2, :], bank[6][:, :], ACT.Copy).then_inc(zb_copied, 1)
            act.wait_ge(tmp_used, u + 1)
            act.activation(oT_hi[4 * a + j][:, :], qT[a][:, j, :], ACT.Copy).then_inc(oT_hi_done, 1)

        act.wait_ge(dve_consts, 2)
        for c in range(TABLES, BHN0):
            if c + 1 < BHN0:
                split_chunk(c + 1)
            if c == HN0:
                split_feat(0)
            for i, m in enumerate(ROWS[c]):
                n = FIRST[c] + i
                if c in (K0, K1):
                    a = (c - K0) // 2
                    if a:
                        act.wait_ge(kv_psum, 1)
                    positive_part(c, i, use_of("k", a, m), kbuf[:, m, :])
                elif c in (V0, V1):
                    act.wait_ge(prod_ready, n + 1 + HEAD)
                    act.activation(vbuf[:, m, :], bank[bank_of[c, i]][:, :], ACT.Copy).then_inc(evac_done, 1)
                elif c in (Q0, Q1):
                    a = int(c == Q1)
                    if a:
                        act.wait_ge(kv_psum, 2)
                    pair = 4 * a + i
                    positive_part(c, i, use_of("q", a, i), qT[a][:, i, :], neg=nbq[:, pair:pair + 1], pos=bq_sb[:, pair:pair + 1])
                elif c not in HH:
                    s = stored_no(c) + i
                    evac_stage(n, s % 2, 16 * (s // 2), bank_of[c, i])
                for a, j in ATTEND.get((c, i), ()):
                    attend(a, j)
            if c == HN1:
                split_feat(1)
            if c == HHB1:
                copy_mlp_weights()
            if c == V0:
                copy_kv(0)
            if c == V1:
                copy_kv(1)

        split_chunk(BHN0)
        act.wait_ge(ex_asked, 1)
        act.activation(ex[:, :], ex[:, :], ACT.Exp).then_inc(ex_done, 1)
        for m in range(MT):
            act.wait_ge(xnr_loaded, 16 * MT)
            act.activation(xn_hi[:, m, :], xn_raw[:, m, :], ACT.Copy).then_inc(xn_hi_done, 1)
        split_chunk(BHN1)
        act.wait_ge(A_psum, 1)
        for s in range(MT):
            act.activation(AT_hi[:, s, :], bank[4 + s][:, :], ACT.Copy).then_inc(A_hi_done, 1)
        for k in range(KT):
            act.wait_ge(z_scaled, k + 1)
            act.activation(xT_hi[:, k, :], ZT[k], ACT.Copy).then_inc(z_hi_done, 1)
        split_chunk(BON0)
        split_chunk(BON1)

        def copy_qT(m):
            act.wait_ge(qT_psum, m + 1)
            act.activation(q8T[m][:, :, :].rearrange("p k h -> p (k h)"), bank[4][:, :].bitcast(BF16), ACT.Copy).then_inc(qT_done, 1)

        def gelu(m):
            act.wait_ge(y_read, m + 1)
            act.activation(y1[m][:, :], y1[m][:, :], ACT.Gelu).then_inc(gelu_done, 1)

        def copy_q2T(m):
            act.wait_ge(q2T_psum, m + 1)
            act.activation(q2T[m][:, :], bank[6][:, 0:P // 2].bitcast(BF16), ACT.Copy).then_inc(q2T_done, 1)

        copy_qT(0)
        copy_qT(1)
        gelu(0)
        copy_q2T(0)
        copy_qT(2)
        gelu(1)
        copy_q2T(1)
        copy_qT(3)
        gelu(2)
        copy_q2T(2)
        gelu(3)
        copy_q2T(3)

    @block.vector
    def _(dve):
        steps = [0]
        asked = [0]

        def step(ins):
            steps[0] += 1
            ins.then_inc(dve_step, 1)
            dve.wait_ge(dve_step, steps[0])

        def ask(ins):
            asked[0] += 1
            ins.then_inc(rstd_asked, 1)
            return asked[0]

        dve.memset(sel8, 0.0)
        dve.memset(b_raw[0:64, :], 0.0).then_inc(dve_consts, 1)
        dve.sem_inc(edge_dot, 8)
        dve.sem_inc(hot_used, 2)
        dve.memset(ones2[:, :], 1.0)
        dve.memset(zeros[:, :], 0.0)
        dve.memset(f32(ones_r[:, :]), 1.0)
        dve.memset(f32(ones_b[:, :]), 0.0).then_inc(dve_step, 1)
        dve.memset(run[:, :], NEG).then_inc(dve_step, 1)
        dve.memset(ks8[:, :], 0.0)
        steps[0] += 2
        dve.wait_ge(dve_step, steps[0])
        dve.memset(f32(ones_b[0:1, :]), 1.0)
        step(dve.memset(f32(ones_b[32:33, :]), 1.0))

        def normalise(m):
            dve.wait_ge(rstd_done, m + 1)
            v, y, a, r = (sm[:, i, m:m + 1] for i in range(4))
            step(dve.tensor_tensor(a, y, y, ALU.mult))
            step(dve.tensor_tensor(a, a, v, ALU.mult))
            step(dve.tensor_scalar(a, a, -0.5, 1.5, ALU.mult, ALU.add))
            step(dve.tensor_tensor(r, y, a, ALU.mult))
            dve.tensor_scalar(xn[:, m, :], x_in[:, m, :], mv[:, m, 0:1], r, ALU.subtract, ALU.mult).then_inc(xn_ready, 1)

        for m in range(MT):
            dve.wait_ge(x_loaded[m], 16)
            dve.bn_stats(stats[:, m, 0, :], x_in[:, m, 0:512])
            step(dve.bn_stats(stats[:, m, 1, :], x_in[:, m, 512:1024]))
            step(dve.bn_aggr(mv[:, m, :], stats[:, m, :, :]))
            ask(dve.tensor_scalar(sm[:, 0, m:m + 1], mv[:, m, 1:2], LN_EPS, None, ALU.add))
            if m:
                normalise(m - 1)
        normalise(MT - 1)

        def split_lo(hi_count, slot, bias=None):
            for h in range(2):
                dve.wait_ge(w_hi_done, hi_count + h)
                dve.tensor_tensor(w_lo[:, slot, h * HALF:(h + 1) * HALF], raw[:, h, :],
                                  f32(w_hi[:, slot, h * HALF:(h + 1) * HALF]), ALU.subtract).then_inc(w_lo_done, 1)
            if bias is not None:
                n, bs = bias
                dve.wait_ge(bias_hi_done, n + 1)
                dve.tensor_tensor(b_hl[32:64, bs, :], b_raw[32:64, :], f32(b_hl[32:64, bs, :]), ALU.subtract).then_inc(bias_lo_done, 1)

        def split_chunk(c):
            split_lo(2 * c + 1, c % 2, (bias_no(c), bias_no(c) % 2) if c in BIASED else None)

        split_chunk(0)
        for k in range(KT):
            dve.wait_ge(xT_hi_done, k + 1)
            dve.tensor_tensor(xT_lo[:, k, :], bank[k][:, :], f32(xT_hi[:, k, :]), ALU.subtract).then_inc(xT_lo_done, 1)

        split_chunk(1)
        dve.wait_ge(small_loaded, 16 * 5)
        dve.tensor_scalar(nbq[:, :], bq_sb[:, :], -1.0, None, ALU.mult).then_inc(dve_consts, 1)
        dve.tensor_copy(src_f[:, :], src_i[:, :])
        step(dve.tensor_copy(dst_f[:, :], dst_i[:, :]))
        for kind, (a, b) in enumerate(((0, T_HO), (T_HO, T_HO + T_OO), (T_HO + T_OO, ET))):
            dve.tensor_scalar(src_row[:, a:b], src_f[:, a:b], float(2 * kind * N), None, ALU.add)
            last = dve.tensor_scalar(dst_row[:, a:b], dst_f[:, a:b], float((2 * kind + 1) * N), None, ALU.add)
        last.then_inc(idx_ready, 1)

        dve.wait_ge(w12_loaded, 32)
        w2_flat = w2_raw[:, :, :].rearrange("p k h -> p (k h)")
        for n, w in enumerate((w1_raw[:, :], w2_flat)):
            dve.tensor_reduce(wsum[:, n:n + 1], w, AX.X, ALU.add, apply_absolute_value=True).then_inc(wsum_done, 1)
        split_chunk(2)
        dve.wait_ge(wtot_done, 1)
        step(dve.tensor_scalar(wmean[:, :], wtot[:, :], 1.0 / (H * D), 1e-5, ALU.mult, ALU.max))
        step(dve.reciprocal(wscale[:, :], wmean[:, :]))
        step(dve.tensor_scalar(wback[:, :], wmean[:, :], 1.0 / 127.0, None, ALU.mult))
        for n, (w, dest) in enumerate(((w1_raw[:, :], w1T[:, :, :].rearrange("p k h -> p (k h)")), (w2_flat, w2T[:, :]))):
            step(dve.tensor_scalar(wq_tmp[:, :], w, wscale[:, n:n + 1], ROUND, ALU.mult, ALU.add))
            step(dve.tensor_scalar(wq_tmp[:, :], wq_tmp[:, :], ROUND + 1.0, ROUND - 1.0, ALU.min, ALU.max))
            ins = dve.tensor_scalar(dest, wq_tmp[:, :], ROUND, None, ALU.subtract)
            ins.then_inc(wq_done, 1)
            dve.wait_ge(wq_done, n + 1)
        split_chunk(3)
        split_chunk(4)

        def edge_pair(t):
            for u in range(2):
                s = slot_of(t + u)
                dve.wait_ge(gathered[s], 32 * fills(t + u))
                dve.tensor_tensor(gp[:, s, :], gp[:, s, :], gq[:, s, :], ALU.add).then_inc(edge_sum, 1)
            for u in range(2):
                s = slot_of(t + u)
                mask_others(t + u)
                dve.wait_ge(edge_sum, t + u + 1)
                dve.scalar_tensor_tensor(out=gp[:, s, :], in0=gp[:, s, :], scalar=0.0, in1=wa_bc[:, :], op0=ALU.max, op1=ALU.mult,
                                         accum_out=logit[:, t + u:t + u + 1]).then_inc(edge_dot, 1)
            for u in range(2):
                dve.wait_ge(edge_dot, t + u + 9)
                take_max(t + u)

        def mask_others(t):
            dve.tensor_scalar(other[:, t % 2, :], iota[:, :], dst_f[:, t:t + 1], NEG, ALU.not_equal, ALU.mult).then_inc(edge_mask, 1)

        def take_max(t):
            k = order_of_max[0] = order_of_max[0] + 1
            dve.wait_ge(edge_mask, k)
            dve.scalar_tensor_tensor(out=run[:, :], in0=other[:, t % 2, :], scalar=logit[:, t:t + 1], in1=run[:, :],
                                     op0=ALU.add, op1=ALU.max).then_inc(edge_max, 1)
            dve.wait_ge(edge_max, k)

        order_of_max = [0]
        next_pair = [0]

        def edge_work(c, between=()):
            between = list(between)
            for i in range(PAIRS.get(c, 0)):
                edge_pair(2 * next_pair[0])
                next_pair[0] += 1
                share = -(-len(between) // (PAIRS[c] - i))
                for w in between[:share]:
                    w()
                del between[:share]
            for w in between:
                w()

        def split_feat(side):
            dest, hi = ((feat_src_lo, feat_src_hi), (feat_dst_lo, feat_dst_hi))[side]
            for b in range(4):
                dve.wait_ge(feat_hi_done, 4 * side + b + 1)
                two = (slice(None), slice(2 * b, 2 * b + 2), slice(None))
                dve.tensor_tensor(dest[two].rearrange("p k e -> p (k e)"), bank[4 + b][:, :],
                                  f32(hi[two]).rearrange("p k e -> p (k e)"), ALU.subtract).then_inc(feat_lo_done, 1)

        def hh_logits(half, i):
            c = (HHB0, HHB1)[half]
            dve.wait_ge(prod_ready, FIRST[c] + i + 1 + HEAD)
            dve.scalar_tensor_tensor(out=other[:, i, :], in0=bank[bank_of[c, i]][:, :], scalar=0.0,
                                     in1=wa_bc[:, half * CW:(half + 1) * CW], op0=ALU.max, op1=ALU.mult,
                                     accum_out=logit_hh[:, half, i:i + 1]).then_inc(hh_read, 1)
            dve.wait_ge(hh_read, 2 * half + i + 1)

        def finish_hh():
            dve.wait_ge(hh_read, 4)
            step(dve.tensor_tensor(logit[:, T_GATHERED:ET], logit_hh[:, 0, :], logit_hh[:, 1, :], ALU.add))
            for t in (T_GATHERED, T_GATHERED + 1):
                mask_others(t)
            for t in (T_GATHERED, T_GATHERED + 1):
                take_max(t)

        dve.wait_ge(consts_ready, 5)
        for c in range(4, TABLES):
            split_chunk(c + 1)
            edge_work(c)

        def add_kq(kind, a, j):
            u = use_of(kind, a, j)
            n_exp = {("k", 0): 0, ("k", 1): 4, ("q", 0): 8, ("q", 1): 12}[kind, a] + j
            dest = kbuf[:, j, :] if kind == "k" else qT[a][:, j, :]
            dve.wait_ge(kq_exp_done, n_exp + 1)
            dve.tensor_tensor(dest, dest, tmp[:, u % 2, :], ALU.add).then_inc(tmp_used, 1)

        def spread_ks(a):
            dve.wait_ge(kv_psum, a + 1)
            for g in range(2):
                r = slice(64 * g, 64 * g + 64)
                dve.tensor_copy(ks8[r, 32 * a + g:32 * a + g + 31:10], bank[7][r, 0:8:2]).then_inc(ks_done, 1)

        def attend(a, j):
            u = use_of("z", a, j)
            dve.wait_ge(zb_copied, 4 * a + j + 1)
            dve.tensor_tensor(qT[a][:, j, :], bank[4 + j % 2][:, :], tmp[:, u % 2, :], ALU.mult).then_inc(tmp_used, 1)
            dve.wait_ge(oT_hi_done, 4 * a + j + 1)
            dve.tensor_tensor(oT_lo[4 * a + j][:, :], qT[a][:, j, :], f32(oT_hi[4 * a + j][:, :]), ALU.subtract).then_inc(oT_lo_done, 1)

        def invert_den(a):
            dve.wait_ge(den8_psum, a + 1)
            if a:
                dve.wait_ge(att_psum, 4)
            step(dve.tensor_scalar(rz, bank[7][0:8, :], 1e-8, None, ALU.add))
            dve.reciprocal(rz, rz).then_inc(rz_done, 1)

        for c in range(TABLES, PR1 + 1):
            if c + 1 < BHN0:
                split_chunk(c + 1)
            work = []
            if c == HN0:
                split_feat(0)
            if c == HHT0:
                split_feat(1)
            if c in (HHB0, HHB1):
                work = [lambda i=i, half=int(c == HHB1): hh_logits(half, i) for i in range(2)]
            if c == K0:
                finish_hh()
                dve.memset(kvb[:, :, :], 0.0).then_inc(kv_cleared, 1)
            if c in (K0, K1):
                work = [lambda j=j, a=(c - K0) // 2: add_kq("k", a, j) for j in range(4)]
            if c == K1:
                spread_ks(0)
            if c == Q0:
                spread_ks(1)
                work = [lambda j=j: add_kq("q", 0, j) for j in range(4)]
            if c == Q1:
                work = [lambda: add_kq("q", 1, 0), lambda: invert_den(0), lambda: add_kq("q", 1, 1), lambda: add_kq("q", 1, 2),
                        lambda: attend(0, 0), lambda: attend(0, 1), lambda: add_kq("q", 1, 3), lambda: attend(0, 2), lambda: attend(0, 3)]
            if c == ON0:
                work = [lambda: invert_den(1), lambda: attend(1, 0), lambda: attend(1, 1)]
            if c == ON1:
                work = [lambda: attend(1, 2), lambda: attend(1, 3)]
            edge_work(c, work)

        dve.wait_ge(max_done, 1)
        dve.sem_inc(mx_gathered, 2)
        with dve.Fori(0, ET // 4) as i:
            for u in range(4):
                dve.wait_ge(mx_gathered, i * 4 + (u + 1))
                dve.scalar_tensor_tensor(out=other[:, u % 2, :], in0=iota[:, :], scalar=dst_f[:, bass.ds(i * 4 + u, 1)],
                                         in1=m_bc[:, :], op0=ALU.is_equal, op1=ALU.mult,
                                         accum_out=mx_e[:, bass.ds(i * 4 + u, 1)]).then_inc(mx_gathered, 1)
        dve.wait_ge(mx_gathered, ET + 2)
        step(dve.tensor_scalar(logit[:, :], logit[:, :], ba_sb[:, 0:1], None, ALU.add))
        step(dve.tensor_scalar(mx_e[:, :], mx_e[:, :], ba_sb[:, 0:1], None, ALU.add))
        dve.tensor_tensor(ex[:, :], logit[:, :], mx_e[:, :], ALU.subtract).then_inc(ex_asked, 1)
        dve.wait_ge(ex_done, 1)
        step(dve.tensor_copy(ex16[:, :], ex[:, :]))
        step(dve.tensor_copy(ex_hi[:, :], ex16[:, :]))
        step(dve.tensor_tensor(ex_lo[:, :], ex[:, :], ex_hi[:, :], ALU.subtract))

        def hot_rows(t, s):
            dve.wait_ge(hot_used, t + 1)
            dve.tensor_scalar(hot_src[:, s, :], iota[:, :], src_f[:, bass.ds(t, 1)], None, ALU.is_equal).then_inc(hot_done, 1)
            dve.tensor_scalar(hot_hi[:, s, :], iota[:, :], dst_f[:, bass.ds(t, 1)], ex_hi[:, bass.ds(t, 1)], ALU.is_equal, ALU.mult).then_inc(hot_done, 1)
            dve.tensor_scalar(hot_lo[:, s, :], iota[:, :], dst_f[:, bass.ds(t, 1)], ex_lo[:, bass.ds(t, 1)], ALU.is_equal, ALU.mult).then_inc(hot_done, 1)

        with dve.Fori(0, 2) as i:
            for s in range(2):
                hot_rows(i * 2 + s, s)
        split_chunk(BHN0)
        with dve.Fori(2, 6) as i:
            for s in range(2):
                hot_rows(i * 2 + s, s)
        split_chunk(BHN1)
        with dve.Fori(6, ET // 2) as i:
            for s in range(2):
                hot_rows(i * 2 + s, s)
        for s in range(MT):
            dve.wait_ge(A_hi_done, s + 1)
            dve.tensor_tensor(AT_lo[:, s, :], bank[4 + s][:, :], f32(AT_hi[:, s, :]), ALU.subtract).then_inc(A_lo_done, 1)
        dve.wait_ge(den_psum, 1)
        step(dve.tensor_scalar(den_tmp[:, :], bank[0][:, :], 1e-30, None, ALU.max))
        step(dve.reciprocal(rden[:, :], den_tmp[:, :]))
        for k in range(KT):
            dve.wait_ge(z_psum, k + 1)
            if k >= 2:
                dve.wait_ge(z_lo_done, k - 1)
            dve.tensor_tensor(ZT[k], bank[1 + k % 3][:, :], rden[:, :], ALU.mult).then_inc(z_scaled, 1)
            dve.wait_ge(z_hi_done, k + 1)
            dve.tensor_tensor(xT_lo[:, k, :], ZT[k], f32(xT_hi[:, k, :]), ALU.subtract).then_inc(z_lo_done, 1)

        dve.wait_ge(top_loaded, 16 * MT)

        def finish_rows(q):
            m, c = divmod(q, 2)
            col = c * CW
            t, d = top[:, m, col:col + CW], x2[:, m, col:col + CW]
            dve.wait_ge(prod_ready, FIRST[BHN0] + q + 1 + HEAD)
            dve.wait_ge(xm_done, m + 1)
            dve.tensor_tensor(t, bank[q % 3][:, :], t, ALU.add).then_inc(bot_evac, 1)
            dve.wait_ge(bot_evac, q + 1)
            dve.scalar_tensor_tensor(out=d, in0=t, scalar=0.0, in1=d, op0=ALU.max, op1=ALU.add).then_inc(dve_step, 1)
            steps[0] += 1

        def small(i, m):
            return sm[:, i, m:m + 1]

        def rstd_wait(n):
            dve.wait_ge(rstd_done, n)

        def quantise(h, amax_col, scale_col, back_col, m, which, dest):
            step(dve.tensor_reduce(small(amax_col, m), h, AX.X, ALU.max, apply_absolute_value=True))
            step(dve.tensor_scalar(small(amax_col, m), small(amax_col, m), 1e-5, None, ALU.max))
            step(dve.reciprocal(small(scale_col, m), small(amax_col, m)))
            step(dve.tensor_scalar(small(scale_col, m), small(scale_col, m), 127.0, None, ALU.mult))
            dve.tensor_scalar(small(back_col, m), small(amax_col, m), wback[:, which:which + 1], None, ALU.mult)
            step(dve.tensor_scalar(h, h, small(scale_col, m), ROUND, ALU.mult, ALU.add))
            return dve.tensor_scalar(dest, h, ROUND + 127.0, ROUND, ALU.min, ALU.subtract)

        def mlp_in(m):
            h = hbuf[:, m, :]
            dve.wait_ge(dve_step, steps[0])
            dve.bn_stats(stats[:, m, 0, :], x2[:, m, 0:512])
            step(dve.bn_stats(stats[:, m, 1, :], x2[:, m, 512:1024]))
            step(dve.bn_aggr(mv[:, m, :], stats[:, m, :, :]))
            n = ask(dve.tensor_scalar(small(0, m), mv[:, m, 1:2], LN_EPS, None, ALU.add))
            dve.wait_ge(bc_loaded, 16 * 6)
            dve.scalar_tensor_tensor(out=h, in0=x2[:, m, :], scalar=mv[:, m, 0:1], in1=g1_bc[:, :], op0=ALU.subtract,
                                     op1=ALU.mult).then_inc(x2_done, 1)
            rstd_wait(n)
            step(dve.tensor_tensor(small(2, m), small(1, m), small(1, m), ALU.mult))
            n = ask(dve.tensor_scalar(small(2, m), small(2, m), mv[:, m, 1:2], LN_EPS, ALU.mult, ALU.add))
            rstd_wait(n)
            step(dve.tensor_tensor(small(3, m), small(3, m), small(1, m), ALU.mult))
            dve.wait_ge(x2_done, m + 1)
            step(dve.scalar_tensor_tensor(out=h, in0=h, scalar=small(3, m), in1=bb1_bc[:, :], op0=ALU.mult, op1=ALU.add))
            quantise(h, 4, 5, 6, m, 0, q8[m][:, :]).then_inc(q_ready, 1)

        def mlp_mid(m):
            y, yn = y1[m][:, :], y2[m][:, :]
            dve.wait_ge(y_psum, m + 1)
            dve.scalar_tensor_tensor(out=y, in0=bank[5][:, 0:H], scalar=small(6, m), in1=b1_bc[:, :], op0=ALU.mult,
                                     op1=ALU.add).then_inc(y_read, 1)
            dve.wait_ge(gelu_done, m + 1)
            step(dve.bn_stats(stats[:, m, 0, :], y))
            step(dve.bn_aggr(mv2[:, m, :], stats[:, m, 0, :]))
            n = ask(dve.tensor_scalar(small(8, m), mv2[:, m, 1:2], LN_EPS, None, ALU.add))
            step(dve.scalar_tensor_tensor(out=yn, in0=y, scalar=mv2[:, m, 0:1], in1=g2_bc[:, :], op0=ALU.subtract, op1=ALU.mult))
            rstd_wait(n)
            step(dve.scalar_tensor_tensor(out=yn, in0=yn, scalar=small(9, m), in1=bb2_bc[:, :], op0=ALU.mult, op1=ALU.add))
            quantise(yn, 10, 11, 12, m, 1, q2[m][:, :]).then_inc(q2_ready, 1)

        def mlp_out(m):
            dve.wait_ge(xb_done, m + 1)
            for c in range(2):
                col = slice(c * CW, (c + 1) * CW)
                dve.wait_ge(o_psum, 2 * m + c + 1)
                dve.scalar_tensor_tensor(out=hbuf[:, m, col], in0=bank[7 if c == 0 else 3][:, :], scalar=small(12, m),
                                         in1=x2[:, m, col], op0=ALU.mult, op1=ALU.add).then_inc(o_done, 1)

        finish_rows(0)
        split_chunk(BON0)
        finish_rows(1)
        split_chunk(BON1)
        mlp_in(0)
        finish_rows(2)
        finish_rows(3)
        mlp_in(1)
        mlp_mid(0)
        finish_rows(4)
        finish_rows(5)
        mlp_in(2)
        mlp_mid(1)
        mlp_out(0)
        finish_rows(6)
        finish_rows(7)
        mlp_in(3)
        mlp_mid(2)
        mlp_out(1)
        mlp_mid(3)
        mlp_out(2)
        mlp_out(3)

    @block.tensor
    def _(pe):
        pe.sem_inc(prod_ready, HEAD)
        pe.wait_ge(consts_ready, 5)
        pe.wait_ge(dve_consts, 1)
        for m in range(MT):
            pe.wait_ge(xn_ready, m + 1)
            for k in range(KT):
                ins = pe.transpose(bank[k][:, m * P:(m + 1) * P], xn[:, m, k * P:(k + 1) * P], ident[:, :])
                if m == MT - 1:
                    ins.then_inc(xT_psum, 1)

        def split_product(dest, pairs, start, stop):
            last = None
            for i, (lh, ll, rh, rl) in enumerate(pairs):
                last_one = stop and i == len(pairs) - 1
                pe.matmul(dest, lh, rh, start=start and i == 0, stop=False)
                pe.matmul(dest, lh, rl, start=False, stop=False)
                last = pe.matmul(dest, ll, rh, start=False, stop=last_one)
            return last

        def rows_product(b, slot, m, lhs_hi, lhs_lo, bias_slot=None, start=True, stop=True, each_k=None):
            if bias_slot is not None:
                pe.matmul(bank[b][:, :], ones_b[:, :], b_hl[0:64, bias_slot, :], start=True, stop=False)
            for k in range(KT):
                if each_k:
                    each_k(k)
                pair = (lhs_hi[k][:, m * P:(m + 1) * P], lhs_lo[k][:, m * P:(m + 1) * P],
                        w_hi[:, slot, k * CW:(k + 1) * CW], w_lo[:, slot, k * CW:(k + 1) * CW])
                last = split_product(bank[b][:, :], [pair], start and bias_slot is None and k == 0, stop and k == KT - 1)
            return last

        with pe.Fori(0, TABLES // 4) as i:
            for cc in range(4):
                pe.wait_ge(w_lo_done, i * 8 + 2 * (cc + 1))
                if cc < 2:
                    pe.wait_ge(bias_lo_done, i * 2 + (cc + 1))
                for m in range(MT):
                    pe.wait_ge(evac_done, i * 16 + (4 * cc + m + 1))
                    if cc == 0 and m == 0:
                        pe.wait_ge(xT_lo_done, 4)
                    rows_product(m, cc % 2, m, *xT, cc if cc < 2 else None,
                                 each_k=(lambda k: pe.wait_ge(xT_lo_done, k + 1)) if cc == 0 and m == 0 else None).then_inc(prod_ready, 1)

        def transpose_feat(side):
            pe.wait_ge(feat_gathered, 64)
            if side:
                pe.wait_ge(feat_lo_done, 4)
            for k in range(KT):
                for u in range(2):
                    ins = pe.transpose(bank[4 + k // 2][:, (k % 2) * E_HH + u * P:(k % 2) * E_HH + (u + 1) * P],
                                       feat_raw[:, side, u, k * P:(k + 1) * P], ident[:, :])
            ins.then_inc(feat_psum, 1)

        def transpose_mlp_weights():
            pe.wait_ge(feat_lo_done, 8)
            pe.wait_ge(wq_done, 2)
            for k in range(KT):
                last = pe.transpose(bank[4][:, :].bitcast(BF16)[:, k * P:(k + 1) * P], w1T[:, k, :], ident16[:, :])
            last.then_inc(wqT_psum, 1)
            for k in range(KT):
                last = pe.transpose(bank[5][:, :].bitcast(BF16)[:, k * P:(k + 1) * P], w2T[:, k * H:(k + 1) * H], ident16[:, :])
            last.then_inc(wqT_psum, 1)

        def kv_product(a):
            pe.wait_ge(tmp_used, use_of("k", a, 3) + 1)
            pe.wait_ge(evac_done, evac_no((V0, V1)[a], 3) + HEAD)
            if a:
                pe.wait_ge(kvb_done, 2)
                pe.wait_ge(ks_done, 2)
            for j in range(4):
                cols = slice(j * P, (j + 1) * P)
                for m in range(MT):
                    pe.matmul(bank[6][:, j * P:(j + 1) * P], kbuf[:, m, cols], vbuf[:, m, cols], start=m == 0, stop=m == MT - 1)
                for m in range(MT):
                    last = pe.matmul(bank[7][:, 2 * j:2 * j + 2], kbuf[:, m, cols], ones2[:, :], start=m == 0, stop=m == MT - 1)
            last.then_inc(kv_psum, 1)

        def den8(a):
            pe.wait_ge(tmp_used, use_of("q", a, 3) + 1)
            pe.wait_ge(ks_done, 4)
            if a:
                pe.wait_ge(rz_done, 1)
            for j in range(4):
                pair = 4 * a + j
                last = pe.matmul(bank[7][0:8, :], ks8[:, 8 * pair:8 * pair + 8], qT[a][:, j, :], start=j == 0, stop=j == 3)
            last.then_inc(den8_psum, 1)

        def attend(a, j):
            n = 4 * a + j
            if j == 0:
                pe.wait_ge(rz_done, a + 1)
                pe.wait_ge(kvb_done, 4)
                if a == 0:
                    pe.wait_ge(wqT_done, 2)
            if j >= 2:
                pe.wait_ge(tmp_used, use_of("z", a, j - 2) + 1)
            if n >= 1:
                pe.wait_ge(zb_copied, n)
            pe.matmul(bank[4 + j % 2][:, :], kvb[:, n, :], qT[a][:, j, :], start=True, stop=True)
            pe.matmul(bank[6][:, :], sel8[:, j, :], rz, start=True, stop=True).then_inc(att_psum, 1)

        def free(c, i):
            reader = bank_free[c, i]
            if reader:
                pe.wait_ge(*((hh_read, reader[1]) if reader[0] == "hh" else (evac_done, reader[1] + HEAD)))

        transpose_feat(0)
        for c in range(TABLES, BHN0):
            slot = c % 2
            pe.wait_ge(w_lo_done, 2 * (c + 1))
            if c in BIASED:
                pe.wait_ge(bias_lo_done, bias_no(c) + 1)
            if c == PR0:
                pe.wait_ge(oT_lo_done, KT)
            if c == HHT0:
                pe.wait_ge(feat_lo_done, 4)
            if c == HHB0:
                pe.wait_ge(feat_lo_done, 8)
            lhs = {PR0: oT, PR1: oT, HHT0: feat_src, HHT1: feat_src, HHB0: feat_dst, HHB1: feat_dst}.get(c, xT)
            for i, m in enumerate(ROWS[c]):
                b = bank_of[c, i]
                free(c, i)
                if c in (Q0, Q1):
                    pairs = [(w_hi[:, slot, k * CW + i * P:k * CW + (i + 1) * P], w_lo[:, slot, k * CW + i * P:k * CW + (i + 1) * P],
                              xT_hi[:, k, :], xT_lo[:, k, :]) for k in range(KT)]
                    last = split_product(bank[b][:, :], pairs, True, True)
                else:
                    last = rows_product(b, slot, m, *lhs, bias_no(c) % 2 if c in BIASED else None,
                                        start=c not in (HHB0, HHB1), stop=c not in (HHT0, HHT1))
                last.then_inc(prod_ready, 1)
                if (c, i) in DEN8:
                    den8(DEN8[c, i])
                for a, j in ATTEND.get((c, i), ()):
                    attend(a, j)
            if c == HN1:
                transpose_feat(1)
            if c == HHB1:
                transpose_mlp_weights()
            if c == V0:
                kv_product(0)
            if c == V1:
                kv_product(1)

        pe.wait_ge(tmp_used, use_of("z", 1, 3) + 1)
        for s in range(MT):
            pe.matmul(bank[4 + s][:, :], zeros[:, :], iota[:, :], start=True, stop=True)
        with pe.Fori(0, ET // 2) as i:
            for u in range(2):
                pe.wait_ge(hot_done, i * 6 + 3 * (u + 1))
                for s in range(MT):
                    pe.matmul(bank[4 + s][:, :], hot_src[:, u, s * P:(s + 1) * P], hot_hi[:, u, :], start=False, stop=True, skip_group_check=True)
                    last = pe.matmul(bank[4 + s][:, :], hot_src[:, u, s * P:(s + 1) * P], hot_lo[:, u, :], start=False, stop=True, skip_group_check=True)
                last.then_inc(hot_used, 1)
        pe.matmul(bank[7][:, :], zeros[:, :], iota[:, :], start=False, stop=True, skip_group_check=True).then_inc(A_psum, 1)

        pe.wait_ge(evac_done, evac_no(PR1, 3) + HEAD)
        for s in range(MT):
            pe.wait_ge(A_lo_done, s + 1)
            pe.matmul(bank[0][:, :], ones_r[:, :], AT_hi[:, s, :], start=s == 0, stop=False)
            last = pe.matmul(bank[0][:, :], ones_r[:, :], AT_lo[:, s, :], start=False, stop=s == MT - 1)
        last.then_inc(den_psum, 1)
        pe.wait_ge(xn_lo_done, MT)
        for k in range(KT):
            if k >= 3:
                pe.wait_ge(z_scaled, k - 2)
            pairs = [(xn_hi[:, s, k * P:(k + 1) * P], xn_lo[:, s, k * P:(k + 1) * P], AT_hi[:, s, :], AT_lo[:, s, :]) for s in range(MT)]
            split_product(bank[1 + k % 3][:, :], pairs, True, True).then_inc(z_psum, 1)
        pe.wait_ge(z_lo_done, KT)
        def up(m):
            pe.wait_ge(q_ready, m + 1)
            if m >= 1:
                pe.wait_ge(qT_done, m)
            for k in range(KT):
                last = pe.transpose(bank[4][:, :].bitcast(BF16)[:, k * P:(k + 1) * P], q8[m][:, k * P:(k + 1) * P], ident16[:, :])
            last.then_inc(qT_psum, 1)
            pe.wait_ge(qT_done, m + 1)
            if m >= 1:
                pe.wait_ge(y_read, m)
            for k in range(KT):
                last = pe.matmul(bank[5][:, 0:H], q8T[m][:, k, :], w1T[:, k, :], start=k == 0, stop=k == KT - 1)
            last.then_inc(y_psum, 1)

        def down(m):
            pe.wait_ge(q2_ready, m + 1)
            if m >= 1:
                pe.wait_ge(q2T_done, m)
            pe.transpose(bank[6][:, 0:P // 2].bitcast(BF16), q2[m][:, :], ident16[:, :]).then_inc(q2T_psum, 1)
            pe.wait_ge(q2T_done, m + 1)
            for c in range(2):
                if m >= 1:
                    pe.wait_ge(o_done, 2 * m + c - 1)
                pe.matmul(bank[7 if c == 0 else 3][:, :], q2T[m][:, :], w2T[:, c * CW:(c + 1) * CW], start=True, stop=True).then_inc(o_psum, 1)

        def bottoms(m):
            for c in range(2):
                q = 2 * m + c
                chunk = ((BHN0, BHN1) if m == 0 else (BON0, BON1))[c]
                pe.wait_ge(w_lo_done, 2 * (chunk + 1))
                if q >= 3:
                    pe.wait_ge(bot_evac, q - 2)
                rows_product(q % 3, chunk % 2, m, *xT).then_inc(prod_ready, 1)

        bottoms(0)
        bottoms(1)
        up(0)
        bottoms(2)
        up(1)
        down(0)
        bottoms(3)
        up(2)
        down(1)
        up(3)
        down(2)
        down(3)

    block_cm.__exit__(None, None, None)


def kernel(**inputs):
    import concourse.bacc as bacc
    from concourse.bass_utils import run_bass_kernel_spmd

    def arr(name):
        return np.ascontiguousarray(inputs[name])

    def chunk(w, col):
        return w[:, col:col + CW].reshape(KT, P, CW).transpose(1, 0, 2).reshape(P, KT * CW)

    def halves(w):
        return [w[0:D], w[D:2 * D]]

    chunks = []
    for kind in ("ho", "oo"):
        for w in halves(arr(f"L0_gnn_W_{kind}")):
            chunks += [chunk(w, 0), chunk(w, CW)]
    qkv = arr("L0_mix_w_qkv")
    wq, wk, wv = qkv[:, 0:D], qkv[:, D:2 * D], qkv[:, 2 * D:3 * D]
    hn, on, pr = halves(arr("L0_gnn_W_hn")), halves(arr("L0_gnn_W_on")), arr("L0_mix_w_proj")
    hh = halves(arr("L0_gnn_W_hh"))
    chunks += [chunk(hn[0], 0), chunk(hn[0], CW), chunk(hh[0], 0), chunk(hh[1], 0), chunk(hh[0], CW), chunk(hh[1], CW),
               chunk(wk, 0), chunk(wv, 0), chunk(wk, CW), chunk(wv, CW), chunk(wq, 0), chunk(wq, CW),
               chunk(on[0], 0), chunk(on[0], CW), chunk(pr, 0), chunk(pr, CW),
               chunk(hn[1], 0), chunk(hn[1], CW), chunk(on[1], 0), chunk(on[1], CW)]
    bqkv = arr("L0_mix_b_qkv")
    b_hn, b_on, b_pr = arr("L0_gnn_b_hn"), arr("L0_gnn_b_on"), arr("L0_mix_b_proj")
    bk, bv = bqkv[D:2 * D], bqkv[2 * D:3 * D]
    rows = []
    for kind in ("ho", "oo"):
        b = arr(f"L0_gnn_b_{kind}")
        rows += [b[0:CW], b[CW:D]]
    b_hh = arr("L0_gnn_b_hh")
    rows += [b_hn[0:CW], b_hn[CW:D], b_hh[0:CW], b_hh[CW:D], bk[0:CW], bv[0:CW], bk[CW:D], bv[CW:D],
             b_on[0:CW], b_on[CW:D], b_pr[0:CW], b_pr[CW:D]]

    def edge_cols(name):
        e = arr(name)
        e = np.concatenate([e[E_HH + E_OO:], e[E_HH:E_HH + E_OO], e[:E_HH]])
        return np.ascontiguousarray(e.reshape(ET, P).T)

    laid = {
        "x": arr("x").reshape(MT, P, D),
        "src": edge_cols("src"),
        "dst": edge_cols("dst"),
        "wt": np.stack(chunks),
        "bias_rows": np.stack(rows).reshape(len(BIASED), 1, CW),
        "bq": np.ascontiguousarray(bqkv[0:D].reshape(KT, P).T),
        "w_a": arr("L0_gnn_W_a").reshape(D),
        "b_a": arr("L0_gnn_b_a"),
        "ln1_g": arr("L0_ffn_ln1_g"),
        "ln1_b": arr("L0_ffn_ln1_b"),
        "w1": arr("L0_ffn_w1"),
        "b1": arr("L0_ffn_b1"),
        "ln2_g": arr("L0_ffn_ln2_g"),
        "ln2_b": arr("L0_ffn_ln2_b"),
        "w2": np.ascontiguousarray(arr("L0_ffn_w2").reshape(KT, P, H).transpose(1, 0, 2)),
        "b2": arr("L0_ffn_b2"),
    }
    nc = bacc.Bacc("TRN2", target_bir_lowering=False, num_devices=1)
    args = {n: nc.dram_tensor(f"in_{n}", a.shape, mybir.dt.from_np(a.dtype), kind="ExternalInput").ap() for n, a in laid.items()}
    out = nc.dram_tensor("out_x", (MT, P, D), F32, kind="ExternalOutput").ap()
    build(nc, **args, out=out)
    r = run_bass_kernel_spmd(nc, [{f"in_{n}": a for n, a in laid.items()}], core_ids=[0])
    return r.results[0]["out_x"].reshape(N, D)
```

```python
import numpy as np

import concourse.bass as bass
from concourse import mybir

F32 = mybir.dt.float32
F32R = mybir.dt.float32r
BF16 = mybir.dt.bfloat16
FP16 = mybir.dt.float16
I32 = mybir.dt.int32
U32 = mybir.dt.uint32
ALU = mybir.AluOpType
ACT = mybir.ActivationFunctionType
AX = mybir.AxisListType
RMAX = bass.bass_isa.ReduceOp.max
RADD = bass.bass_isa.ReduceOp.add

P = 128
N = 512
D = 1024
H = 128
HEADS = 16
HD = D // HEADS
MT = N // P
KT = D // P
CW = 512
HALF = KT * CW // 2
E = 8192
ET = E // P
E_HH, E_OO = 256, 1280
T_HO = (E - E_HH - E_OO) // P
T_OO = E_OO // P
LN_EPS = 1e-5
ROUND = 12582912.0
NEG = -3.0e38

TABLES = 8
(HHT0, HHB0, HHT1, HHB1, K0, HN0, V0, HN1, K1, V1, Q0, Q1, ON0, ON1, PR0, PR1,
 BON0, BON1, BHN0, BHN1) = range(TABLES, TABLES + 20)
CHUNKS = TABLES + 20
BIASED = [c for c in range(TABLES) if c % 4 < 2] + [HHT0, HHT1, K0, HN0, V0, HN1, K1, V1, ON0, ON1, PR0, PR1]
STORED = list(range(TABLES)) + [HN0, HN1, ON0, ON1, PR0, PR1]
HH = (HHT0, HHB0, HHT1, HHB1)
ROWS = {c: list(range(MT)) for c in range(CHUNKS)}
ROWS.update({c: [0] for c in (HN0, HN1, BHN0, BHN1)})
ROWS.update({c: [1, 2, 3] for c in (ON0, ON1, BON0, BON1)})
ROWS.update({c: [0, 1] for c in HH})
FIRST = {}
_n = 0
for _c in range(CHUNKS):
    FIRST[_c] = _n
    _n += len(ROWS[_c])
T_GATHERED = T_HO + T_OO
PAIRS = {4: 2, 5: 2, 6: 2, 7: 2, HHT0: 1, HHB0: 1, HHT1: 1, HHB1: 1, K0: 2, V0: 3, K1: 3, V1: 3, Q0: 3, Q1: 2, ON0: 3}
assert sum(PAIRS.values()) * 2 == T_GATHERED
MAXIMA = {ON1: (0, 12), PR0: (12, 32), PR1: (32, 48)}
T_EARLY = 48
SLOTS = 6
HEAD = 4


ORDER = [1, 2, 3, 0]
POWERS = [(ORDER[j], r) for j, r in ((0, "r1"), (0, "r2"), (1, "r1"), (1, "r2"), (0, "r3"), (2, "r1"), (2, "r2"), (1, "r3"),
                                     (2, "r3"), (3, "r1"), (3, "r2"), (3, "r3"))]


USES = [("k", a, j) for a in range(2) for j in range(4)] + [("q", 0, j) for j in range(4)] + \
       [("q", 1, 0), ("q", 1, 1), ("q", 1, 2), ("z", 0, 0), ("z", 0, 1), ("q", 1, 3), ("z", 0, 2), ("z", 0, 3)] + \
       [("z", 1, j) for j in range(4)]
ATTEND = {(Q1, 2): [(0, 0), (0, 1)], (Q1, 3): [(0, 2), (0, 3)], (ON0, 2): [(1, 0), (1, 1)], (ON1, 0): [(1, 2), (1, 3)]}
DEN8 = {(Q1, 0): 0, (ON0, 0): 1}


def build(nc, x, src, dst, wt, bias_rows, bq, w_a, b_a, ln1_g, ln1_b, w1, b1, ln2_g, ln2_b, w2, b2, out):
    xn_d = nc.dram_tensor("xn_scratch", (MT, P, D), F32, kind="Internal").ap()
    table_d = nc.dram_tensor("edge_tables", (2 * 2 * N, D), F32, kind="Internal").ap()
    table_tiles = table_d.rearrange("(b m p) d -> b m p d", m=MT, p=P)
    top_d = nc.dram_tensor("node_top", (MT, P, D), F32, kind="Internal").ap()
    mix_d = nc.dram_tensor("mix_out", (MT, P, D), F32, kind="Internal").ap()

    place = [16512]

    def region(nbytes):
        at = place[0]
        place[0] += (nbytes + 31) // 32 * 32
        assert place[0] <= 229344, place[0]
        return at

    def sb(name, shape, dt, at=None):
        size = int(np.prod(shape[1:])) * mybir.dt.size(dt)
        return nc.alloc_sbuf_tensor_at(name, shape, dt, offset=region(size) if at is None else at)

    xT_hi = sb("xT_hi", [P, KT, N], F32R)
    xT_lo = sb("xT_lo", [P, KT, N], F32R)
    raw = sb("w_raw", [P, 2, HALF], F32)
    w_hi = sb("w_hi", [P, 2, KT * CW], F32R)
    w_lo = sb("w_lo", [P, 2, KT * CW], F32R)
    at_b = region(16384)
    w1_raw = sb("w1_raw", [P, D], F32, at_b)
    w2_raw = sb("w2_raw", [P, KT, H], F32, at_b + 4096)
    wq_tmp = sb("wq_tmp", [P, D], F32, at_b + 8192)
    feat_raw = sb("feat_raw", [P, 2, 2, D], F32, at_b)
    feat_dst_hi = sb("feat_dst_hi", [P, KT, E_HH], F32R, at_b)
    feat_dst_lo = sb("feat_dst_lo", [P, KT, E_HH], F32R, at_b + 8192)
    kbuf = sb("kbuf", [P, MT, CW], F32, at_b)
    vbuf = sb("vbuf", [P, MT, CW], F32, at_b + 8192)
    qT1 = sb("qT1", [P, 4, N], F32, at_b)
    xn_raw = sb("xn_raw", [P, MT, D], F32, at_b)
    top = sb("top", [P, MT, D], F32, at_b)
    q8 = [sb(f"q8_{m}", [P, D], BF16, at_b + 4096 * m) for m in range(MT)]
    q8T = [sb(f"q8T_{m}", [P, KT, P], BF16, at_b + 4096 * m + 2048) for m in range(MT)]
    at_edge = region(4096 + 2048)
    wa_bc = sb("wa_bc", [P, D], F32, at_edge)
    other = sb("other_node", [P, 2, N], BF16, at_edge + 4096)
    hot_src = sb("hot_src", [P, 2, N], FP16, at_edge)
    hot_hi = sb("hot_hi", [P, 2, N], FP16, at_edge + 2048)
    hot_lo = sb("hot_lo", [P, 2, N], FP16, at_edge + 4096)
    hot_z = sb("z_scaled_T", [P, 2, N], F32, at_edge)
    at_stage = region(4096)
    stage = sb("stage", [P, 2, CW], F32, at_stage)
    y1 = [sb(f"y1_{m}", [P, H], F32, at_stage + 1024 * m) for m in range(MT)]
    y2 = [sb(f"y2_{m}", [P, H], F32, at_stage + 1024 * m + 512) for m in range(MT)]
    at_big = region(32768)
    x_in = sb("x_in", [P, MT, D], F32, at_big)
    xn = sb("xn", [P, MT, D], F32, at_big + 16384)
    rows_sum = sb("gathered_rows", [P, SLOTS, D], F32, at_big)
    xn_hi = [sb(f"xn_hi{k}", [P, MT, P], F32R, at_big + 4096 * k) for k in range(KT)]
    xn_lo = [sb(f"xn_lo{k}", [P, MT, P], F32R, at_big + 4096 * k + 2048) for k in range(KT)]
    x2 = sb("x2", [P, MT, D], F32, at_big)
    hbuf = sb("hbuf", [P, MT, D], F32, at_big + 16384)
    at_q = region(8192)
    feat_src_hi = sb("feat_src_hi", [P, KT, E_HH], F32R, at_q)
    qT0 = sb("qT0", [P, 4, N], F32, at_q)
    AT_hi = sb("AT_hi", [P, MT, N], F32R, at_q)
    g1_bc = sb("g1_bc", [P, D], F32, at_q)
    bb1_bc = sb("bb1_bc", [P, D], F32, at_q + 4096)
    oT_hi = [sb(f"oT_hi{k}", [P, N], F32R, (at_b + 8192, at_big + SLOTS * 4096)[k // 4] + 2048 * (k % 4))
             for k in range(KT)]
    oT_lo = [sb(f"oT_lo{k}", [P, N], F32R, (at_q, at_b)[k // 4] + 2048 * (k % 4)) for k in range(KT)]
    at_kv = region(8192)
    feat_src_lo = sb("feat_src_lo", [P, KT, E_HH], F32R, at_kv)
    tmp = sb("tmp", [P, 2, N], F32, at_kv)
    x_part = sb("x_part", [P, MT, CW], F32, at_kv)
    kvb = sb("kvb", [P, KT, P], F32, at_kv + 4096)
    AT_lo = sb("AT_lo", [P, MT, N], F32R, at_kv)
    b2_bc = sb("b2_bc", [P, D], F32, at_kv)
    b1_bc = sb("b1_bc", [P, H], F32, at_kv + 4096)
    g2_bc = sb("g2_bc", [P, H], F32, at_kv + 4608)
    bb2_bc = sb("bb2_bc", [P, H], F32, at_kv + 5120)
    at_braw = region(2048)
    b_raw = sb("b_raw", [P, CW], F32, at_braw)
    q2 = [sb(f"q2_{m}", [P, H], BF16, at_braw + 512 * m) for m in range(MT)]
    q2T = [sb(f"q2T_{m}", [P, P], BF16, at_braw + 512 * m + 256) for m in range(MT)]
    at_bhl = region(4096)
    b_hl = sb("b_hl", [P, 2, CW], F32R, at_bhl)
    at_run = region(4096)
    run = sb("running_max", [P, N], F32, at_run)
    m_bc = sb("max_bc", [P, N], F32, at_run + 2048)
    thrown_away = sb("thrown_away", [P, 2, N], BF16, at_run)
    den_tmp = sb("den_tmp", [P, N], F32, at_run)
    rden = sb("rden", [P, N], F32, at_run + 2048)
    iota = sb("iota", [P, N], FP16)
    junk = sb("junk", [P, 1], F32)
    ks8 = sb("ks8", [P, KT * 8], F32)
    rz = sb("rz", [P, N], F32, at_braw)[64:72, :]
    sel8 = sb("sel8", [P, 4, P], F32, at_bhl)[64:72, :, :]
    ident = sb("ident", [P, P], F32)
    ident16 = sb("ident16", [P, P], BF16)
    ones_b = sb("ones_b", [64, P], F32R)
    ones_r = sb("ones_r", [P, P], F32R)
    ones2 = sb("ones2", [P, 2], F32)
    zeros = sb("zeros", [P, P], FP16)
    w1T = sb("w1T", [P, KT, H], BF16)
    w2T = sb("w2T", [P, D], BF16)
    src_i = sb("src_i", [P, ET], I32)
    dst_i = sb("dst_i", [P, ET], I32)
    src_f = sb("src_f", [P, ET], F32)
    dst_f = sb("dst_f", [P, ET], F32)
    src_row = sb("src_row", [P, ET], I32)
    dst_row = sb("dst_row", [P, ET], I32)
    idx_now = sb("idx_now", [P, 2, 2, SLOTS // 2], I32)
    logit_hh = sb("logit_hh", [P, 2, 2], F32)
    logit = sb("logit", [P, ET], F32)
    mx_e = sb("max_of_edge", [P, ET], F32)
    ex = sb("ex", [P, ET], F32)
    ex16 = sb("ex16", [P, ET], FP16)
    ex_hi = sb("ex_hi", [P, ET], F32)
    ex_lo = sb("ex_lo", [P, ET], F32)
    bq_sb = sb("bq_sb", [P, KT], F32)
    nbq = sb("nbq", [P, KT], F32)
    ba_sb = sb("ba_sb", [P, 1], F32)
    eps_c = sb("eps_c", [P, 1], F32)
    nhalf = sb("nhalf", [P, MT], F32)
    stats = sb("stats", [P, MT, 2, 6], F32)
    mv = sb("mv", [P, MT, 2], F32)
    sm = sb("small", [P, 16, MT], F32)
    wsum = sb("wsum", [P, 2], F32)
    wtot = sb("wtot", [P, 2], F32)
    wmean = sb("wmean", [P, 2], F32)
    wscale = sb("wscale", [P, 2], F32)
    wback = sb("wback", [P, 2], F32)
    mv2 = sb("mv2", [P, MT, 2], F32)

    bank = [nc.alloc_psum_tensor(f"bank{i}", [P, CW], F32) for i in range(8)]

    def sem(name):
        return nc.alloc_semaphore(name)

    x_loaded = [sem(f"x_loaded{m}") for m in range(MT)]
    small_loaded = sem("small_loaded")
    w12_loaded = sem("w12_loaded")
    raw_loaded = [sem(f"raw_loaded{h}") for h in range(2)]
    bias_loaded = sem("bias_loaded")
    consts_ready = sem("consts_ready")
    dve_consts = sem("dve_consts")
    idx_ready = sem("idx_ready")
    rstd_asked = sem("rstd_asked")
    rstd_done = sem("rstd_done")
    xn_ready = sem("xn_ready")
    xn_stored = sem("xn_stored")
    xT_psum = sem("xT_psum")
    xT_hi_done = sem("xT_hi_done")
    xT_lo_done = sem("xT_lo_done")
    w_hi_done = sem("w_hi_done")
    w_lo_done = sem("w_lo_done")
    bias_hi_done = sem("bias_hi_done")
    bias_lo_done = sem("bias_lo_done")
    prod_ready = sem("prod_ready")
    evac_done = sem("evac_done")
    stage_stored = [sem(f"stage_stored{s}") for s in range(2)]
    feat_gathered = sem("feat_gathered")
    feat_psum = sem("feat_psum")
    feat_hi_done = sem("feat_hi_done")
    feat_lo_done = sem("feat_lo_done")
    hh_read = sem("hh_read")
    kv_cleared = sem("kv_cleared")
    wsum_done = sem("wsum_done")
    wtot_done = sem("wtot_done")
    wq_done = sem("wq_done")
    wqT_psum = sem("wqT_psum")
    wqT_done = sem("wqT_done")
    idx_copied = sem("idx_copied")
    src_landed = [sem(f"src_landed{s}") for s in range(SLOTS)]
    dst_added = [sem(f"dst_added{s}") for s in range(SLOTS)]
    edge_dot = sem("edge_dot")
    edge_mask = sem("edge_mask")
    edge_max = sem("edge_max")
    kq_exp_done = sem("kq_exp_done")
    tmp_used = sem("tmp_used")
    v_done = sem("v_done")
    kv_psum = sem("kv_psum")
    kvb_done = sem("kvb_done")
    ks_done = sem("ks_done")
    den8_psum = sem("den8_psum")
    rz_done = sem("rz_done")
    att_psum = sem("att_psum")
    zb_copied = sem("zb_copied")
    oT_hi_done = sem("oT_hi_done")
    oT_lo_done = sem("oT_lo_done")
    max_done = sem("max_done")
    mx_gathered = sem("mx_gathered")
    ex_asked = sem("ex_asked")
    ex_done = sem("ex_done")
    hot_done = sem("hot_done")
    hot_used = sem("hot_used")
    A_psum = sem("A_psum")
    A_hi_done = sem("A_hi_done")
    A_lo_done = sem("A_lo_done")
    den_psum = sem("den_psum")
    z_psum = sem("z_psum")
    z_scaled = sem("z_scaled")
    z_hi_done = sem("z_hi_done")
    z_lo_done = sem("z_lo_done")
    xnr_loaded = sem("xnr_loaded")
    xn_hi_done = sem("xn_hi_done")
    xn_lo_done = sem("xn_lo_done")
    x_part_loaded = sem("x_part_loaded")
    x_added = sem("x_added")
    mix_loaded = [sem(f"mix_loaded{m}") for m in range(MT)]
    top_loaded = sem("top_loaded")
    bc_loaded = sem("bc_loaded")
    bot_evac = sem("bot_evac")
    x2_done = sem("x2_done")
    xb_done = sem("xb_done")
    q_ready = sem("q_ready")
    qT_psum = sem("qT_psum")
    qT_done = sem("qT_done")
    y_psum = sem("y_psum")
    y_read = sem("y_read")
    gelu_done = sem("gelu_done")
    q2_ready = sem("q2_ready")
    q2T_psum = sem("q2T_psum")
    q2T_done = sem("q2T_done")
    o_psum = sem("o_psum")
    o_done = sem("o_done")
    out_stored = sem("out_stored")
    pool_turn = sem("pool_turn")
    dve_step = sem("dve_step")
    act_step = sem("act_step")
    pool_step = sem("pool_step")

    qT = (qT0, qT1)
    xT, feat_src, feat_dst = ([[t[:, k, :] for k in range(KT)] for t in pair]
                              for pair in ((xT_hi, xT_lo), (feat_src_hi, feat_src_lo), (feat_dst_hi, feat_dst_lo)))
    oT = [[t[:, :] for t in half] for half in (oT_hi, oT_lo)]
    ZT = [hot_z[:, k % 2, :] for k in range(KT)]

    def f32(ap):
        return ap.bitcast(F32)

    def use_of(kind, a, j):
        return USES.index((kind, a, j))

    def bias_no(c):
        return sum(b < c for b in BIASED)

    def evac_no(c, i):
        return FIRST[c] + i + 1 - sum(len(ROWS[b]) for b in HH if b < c)

    bank_of, bank_free, last = {}, {}, {}
    turn = 0
    for c in range(BON0):
        for i in range(len(ROWS[c])):
            if c in (HHB0, HHB1):
                bank_of[c, i] = bank_of[c - 1, i]
                bank_free[c, i] = None
                last[bank_of[c, i]] = ("hh", 2 * (c == HHB1) + i + 1)
            else:
                b = bank_of[c, i] = turn % 4
                turn += 1
                bank_free[c, i] = last.get(b)
                last[b] = ("act", evac_no(c, i))

    def stored_no(c):
        return sum(len(ROWS[b]) for b in STORED if b < c)

    block_cm = nc.Block()
    block = block_cm.__enter__()

    @block.sync
    def _(sp):
        for m in range(MT):
            sp.dma_start(x_in[:, m, :], x[m]).then_inc(x_loaded[m], 16)

        def load_half(c, h):
            sp.dma_start(raw[:, h, :], wt[c, :, h * HALF:(h + 1) * HALF]).then_inc(raw_loaded[h], 16)

        def load_bias(b):
            for row in (0, 32):
                sp.dma_start(b_raw[row:row + 1, :], bias_rows[b]).then_inc(bias_loaded, 16)

        def store(n_tile, slot, dram, ready=None):
            sp.wait_ge(*(ready or (evac_done, n_tile + HEAD)))
            sp.dma_start(dram, stage[:, slot, :]).then_inc(stage_stored[slot], 16)

        def load_x_part(c):
            col = 0 if c == PR0 else CW
            if c == PR0:
                sp.wait_ge(oT_lo_done, KT)
            else:
                sp.wait_ge(x_added, MT)
            for m in range(MT):
                sp.dma_start(x_part[:, m, :], x[m, :, col:col + CW]).then_inc(x_part_loaded, 16)

        load_half(0, 0)
        load_half(0, 1)
        sp.wait_ge(dve_consts, 1)
        load_bias(0)
        sp.dma_start(w1_raw[:, :], w1).then_inc(w12_loaded, 16)
        sp.dma_start(w2_raw[:, :, :], w2).then_inc(w12_loaded, 16)
        for h in range(2):
            sp.wait_ge(w_lo_done, h + 1)
            load_half(1, h)
        sp.wait_ge(bias_lo_done, 1)
        load_bias(1)
        for m in range(MT):
            sp.wait_ge(xn_ready, m + 1)
            sp.dma_start(xn_d[m], xn[:, m, :]).then_inc(xn_stored, 16)

        for c in range(TABLES):
            for h in range(2):
                sp.wait_ge(w_lo_done, 2 * (c + 1) + h + 1)
                load_half(c + 2, h)
            if c + 2 in BIASED:
                sp.wait_ge(bias_lo_done, bias_no(c + 2))
                load_bias(bias_no(c + 2))
            for m in range(MT):
                store(4 * c + m + 1, m % 2, table_tiles[c // 2, m, :, (c % 2) * CW:(c % 2 + 1) * CW])
        for c in range(TABLES, PR1 + 1):
            if c + 2 <= BON1:
                if c + 2 == BON1:
                    break
                for h in range(2):
                    sp.wait_ge(w_lo_done, 2 * (c + 1) + h + 1)
                    load_half(c + 2, h)
                if c + 2 in BIASED:
                    sp.wait_ge(bias_lo_done, bias_no(c + 2))
                    load_bias(bias_no(c + 2))
            if c in STORED:
                dram = mix_d if c in (PR0, PR1) else top_d
                if c in (PR0, PR1):
                    load_x_part(c)
                col = 0 if c in (HN0, ON0, PR0) else CW
                for i, m in enumerate(ROWS[c]):
                    s = (stored_no(c) + i) % 2
                    store(evac_no(c, i), s, dram[m, :, col:col + CW], (x_added, i + 1) if c == PR0 else None)
        load_x_part(PR1)
        for i, m in enumerate(ROWS[PR1]):
            store(evac_no(PR1, i), (stored_no(PR1) + i) % 2, mix_d[m, :, CW:D], (x_added, MT + i + 1))
        sp.wait_ge(prod_ready, FIRST[BON0] + HEAD)
        sp.wait_ge(xn_stored, 16 * MT)
        for m in range(MT):
            sp.dma_start(xn_raw[:, m, :], xn_d[m]).then_inc(xnr_loaded, 16)
        for c in (BON1, BHN0):
            for h in range(2):
                sp.wait_ge(w_lo_done, 2 * (c - 1) + h + 1)
                load_half(c, h)
        for s in range(2):
            sp.wait_ge(stage_stored[s], 16 * (stored_no(PR1 + 1) // 2))
        sp.wait_ge(xn_lo_done, KT)
        for m in range(MT):
            sp.dma_start(top[:, m, :], top_d[m]).then_inc(top_loaded, 16)
        for m in range(MT):
            sp.wait_ge(z_psum, m + 1)
            sp.dma_start(x2[:, m, :], mix_d[m]).then_inc(mix_loaded[m], 16)
        sp.wait_ge(z_psum, KT)
        sp.dma_start(g1_bc[:, :], ln1_g.partition_broadcast(P)).then_inc(bc_loaded, 16)
        sp.dma_start(bb1_bc[:, :], ln1_b.partition_broadcast(P)).then_inc(bc_loaded, 16)
        sp.dma_start(b2_bc[:, :], b2.partition_broadcast(P)).then_inc(bc_loaded, 16)
        sp.dma_start(b1_bc[:, :], b1.partition_broadcast(P)).then_inc(bc_loaded, 16)
        sp.dma_start(g2_bc[:, :], ln2_g.partition_broadcast(P)).then_inc(bc_loaded, 16)
        sp.dma_start(bb2_bc[:, :], ln2_b.partition_broadcast(P)).then_inc(bc_loaded, 16)
        for h in range(2):
            sp.wait_ge(w_lo_done, 2 * BHN0 + h + 1)
            load_half(BHN1, h)
        for j, m in enumerate(ORDER):
            sp.wait_ge(o_done, 2 * (j + 1))
            sp.dma_start(out[m], hbuf[:, m, :]).then_inc(out_stored, 16)
        sp.wait_ge(out_stored, 16 * MT)

    @block.gpsimd
    def _(pool):
        pool.memset(ident[:, :], 0.0).then_inc(pool_step, 1)
        pool.memset(ident16[:, :], 0.0).then_inc(pool_step, 1)
        pool.iota(iota[:, :], pattern=[[1, N]], base=0, channel_multiplier=0,
                  allow_small_or_imprecise_dtypes=True).then_inc(consts_ready, 1)
        pool.memset(nhalf[:, :], -0.5).then_inc(consts_ready, 1)
        pool.wait_ge(pool_step, 2)
        pool.affine_select(out=ident[:, :], in_=ident[:, :], compare_op=ALU.not_equal, fill=1.0,
                           base=0, pattern=[[-1, P]], channel_multiplier=1).then_inc(consts_ready, 1)
        pool.affine_select(out=ident16[:, :], in_=ident16[:, :], compare_op=ALU.not_equal, fill=1.0,
                           base=0, pattern=[[-1, P]], channel_multiplier=1).then_inc(consts_ready, 1)
        pool.wait_ge(dve_consts, 1)
        pool.wait_ge(consts_ready, 4)
        sel_v = sel8.rearrange("r j (g e) -> r j g e", g=2)
        pool.affine_select(out=sel_v, in_=sel_v, compare_op=ALU.not_equal, fill=1.0,
                           base=0, pattern=[[-2, 4], [-1, 2], [0, HD]], channel_multiplier=1).then_inc(consts_ready, 1)
        pool.wait_ge(consts_ready, 5)
        for m in range(MT):
            pool.wait_ge(rstd_asked, m + 1)
            pool.tensor_tensor(sm[:, 1, m:m + 1], sm[:, 0, m:m + 1], nhalf[:, 0:1], ALU.pow).then_inc(rstd_done, 1)
        pool.wait_ge(wsum_done, 2)
        pool.partition_all_reduce(wtot[:, :], wsum[:, :], P, RADD).then_inc(wtot_done, 1)

        pool.wait_ge(idx_ready, 1)
        pool.wait_ge(wq_done, 2)
        pool.wait_ge(xn_stored, 16 * MT)
        for side, index in enumerate((src_i, dst_i)):
            for u in range(2):
                pool.indirect_dma_start(
                    feat_raw[:, side, u, :], None, xn_d.rearrange("m p d -> (m p) d"),
                    bass.IndirectOffsetOnAxis(ap=index[:, T_GATHERED + u:T_GATHERED + u + 1].bitcast(U32), axis=0),
                ).then_inc(feat_gathered, 16)
        for s in range(2):
            pool.wait_ge(stage_stored[s], 16 * (4 * MT // 2))

        def gather(s, index, rows, landed, op=ALU.bypass):
            pool.indirect_dma_start(
                rows_sum[:, s, :], None, table_d[0:rows, :],
                bass.IndirectOffsetOnAxis(ap=index.bitcast(U32), axis=0), compute_op=op,
            ).then_inc(landed[s], 16)

        HB = SLOTS // 2
        with pool.Fori(0, T_HO // SLOTS) as i:
            for b in range(2):
                pool.wait_ge(edge_dot, i * SLOTS + (HB * (b + 1) - SLOTS + 8))
                pool.sem_inc(pool_turn, 1)
                pool.tensor_copy(idx_now[:, b, 0, :], src_row[:, bass.ds(i * SLOTS + HB * b, HB)]).then_inc(idx_copied, 1)
                pool.tensor_copy(idx_now[:, b, 1, :], dst_row[:, bass.ds(i * SLOTS + HB * b, HB)]).then_inc(idx_copied, 1)
                pool.wait_ge(idx_copied, i * 4 + 2 * (b + 1))
                pool.sem_inc(pool_turn, 1)
                for u in range(HB + 1):
                    if u < HB:
                        s = HB * b + u
                        pool.wait_ge(edge_dot, i * SLOTS + (s + 1 - SLOTS + 8))
                        pool.sem_inc(pool_turn, 1)
                        gather(s, idx_now[:, b, 0, u:u + 1], 2 * N, src_landed)
                    if u:
                        s = HB * b + u - 1
                        pool.wait_ge(src_landed[s], i * 16 + 16)
                        pool.sem_inc(pool_turn, 1)
                        gather(s, idx_now[:, b, 1, u - 1:u], 2 * N, dst_added, ALU.add)
        first = T_HO // SLOTS * SLOTS
        for t in range(first, T_GATHERED + 1):
            if t == T_HO:
                for s in range(2):
                    pool.wait_ge(stage_stored[s], 16 * (TABLES * MT // 2))
            if t < T_GATHERED:
                pool.wait_ge(edge_dot, t + 1 - SLOTS + 8)
                gather(t % SLOTS, src_row[:, t:t + 1], 2 * N if t < T_HO else 4 * N, src_landed)
            if t > first:
                pool.wait_ge(src_landed[(t - 1) % SLOTS], 16 * ((t - 1) // SLOTS + 1))
                gather((t - 1) % SLOTS, dst_row[:, t - 1:t], 2 * N if t - 1 < T_HO else 4 * N, dst_added, ALU.add)

        pool.wait_ge(edge_max, ET)
        pool.partition_all_reduce(m_bc[:, :], run[:, :], P, RMAX).then_inc(max_done, 1)
        for c in (PR0, PR1):
            for i in range(MT):
                n = MT * int(c == PR1) + i
                pool.wait_ge(evac_done, evac_no(c, i) + HEAD)
                pool.wait_ge(x_part_loaded, 16 * MT * (1 + int(c == PR1)))
                s = (stored_no(c) + i) % 2
                pool.tensor_tensor(stage[:, s, :], stage[:, s, :], x_part[:, i, :], ALU.add).then_inc(x_added, 1)
        for k in range(KT):
            pool.wait_ge(xn_hi_done, k + 1)
            pool.tensor_tensor(xn_lo[k][:, :, :], xn_raw[:, :, k * P:(k + 1) * P], f32(xn_hi[k][:, :, :]), ALU.subtract).then_inc(xn_lo_done, 1)

        def power(n):
            pool.wait_ge(rstd_asked, n + MT + 1)
            m, which = POWERS[n]
            src_c, dst_c = {"r1": (0, 1), "r2": (2, 3), "r3": (8, 9)}[which]
            pool.tensor_tensor(sm[:, dst_c, m:m + 1], sm[:, src_c, m:m + 1], nhalf[:, 0:1], ALU.pow).then_inc(rstd_done, 1)

        for n, (m, which) in enumerate(POWERS):
            power(n)
            if which == "r2":
                pool.wait_ge(bc_loaded, 16 * 6)
                pool.wait_ge(x2_done, ORDER.index(m) + 1)
                pool.tensor_tensor(x2[:, m, :], x2[:, m, :], b2_bc[:, :], ALU.add).then_inc(xb_done, 1)

    @block.scalar
    def _(act):
        act.sem_inc(evac_done, HEAD)
        act.dma_start(src_i[:, :], src).then_inc(small_loaded, 16)
        act.dma_start(dst_i[:, :], dst).then_inc(small_loaded, 16)
        act.dma_start(bq_sb[:, :], bq).then_inc(small_loaded, 16)
        act.dma_start(ba_sb[:, :], b_a.partition_broadcast(P)).then_inc(small_loaded, 16)
        act.dma_start(wa_bc[:, :], w_a.partition_broadcast(P)).then_inc(small_loaded, 16)
        steps = [0]

        def step(ins):
            steps[0] += 1
            ins.then_inc(act_step, 1)
            act.wait_ge(act_step, steps[0])

        def split_hi(loaded, prod, slot, bias=None):
            act.wait_ge(prod_ready, prod)
            for h in range(2):
                act.wait_ge(raw_loaded[h], loaded)
                act.activation(w_hi[:, slot, h * HALF:(h + 1) * HALF], raw[:, h, :], ACT.Copy).then_inc(w_hi_done, 1)
            if bias is not None:
                n, bs = bias
                act.wait_ge(bias_loaded, n * 32 + 32)
                act.activation(b_hl[0:64, bs, :], b_raw[0:64, :], ACT.Copy).then_inc(bias_hi_done, 1)

        def split_chunk(c):
            split_hi(16 * (c + 1), (FIRST[BON0] + 5 if c == BHN0 else FIRST[c - 1]) + HEAD, c % 2, (bias_no(c), bias_no(c) % 2) if c in BIASED else None)

        act.wait_ge(dve_consts, 1)
        split_hi(16, HEAD, 0, (0, 0))
        for k in range(KT):
            act.wait_ge(xT_psum, k + 1)
            act.activation(xT_hi[:, k, :], bank[k][:, :], ACT.Copy).then_inc(xT_hi_done, 1)

        def evac_stage(n, slot, free, b):
            act.wait_ge(prod_ready, n + 1 + HEAD)
            if not (isinstance(free, int) and free == 0):
                act.wait_ge(stage_stored[slot], free)
            act.activation(stage[:, slot, :], bank[b][:, :], ACT.Copy).then_inc(evac_done, 1)

        def four_tables(i):
            for cc in range(4):
                nb = {3: i * 2 + 2, 0: i * 2 + 1}.get(cc)
                split_hi(i * 64 + 16 * (cc + 2), i * 16 + (4 * cc + HEAD), (cc + 1) % 2,
                         None if nb is None else (nb, {3: 0, 0: 1}[cc]))
                for m in range(MT):
                    evac_stage(i * 16 + (4 * cc + m), m % 2, i * 128 + 16 * ((4 * cc + m) // 2), m)

        def split_feat(side):
            dest = (feat_src_hi, feat_dst_hi)[side]
            act.wait_ge(feat_psum, side + 1)
            for b in range(4):
                act.activation(dest[:, 2 * b:2 * b + 2, :].rearrange("p k e -> p (k e)"), bank[4 + b][:, :], ACT.Copy).then_inc(feat_hi_done, 1)

        four_tables(0)
        split_feat(0)
        four_tables(1)

        def copy_mlp_weights():
            for n, (b, dest) in enumerate(((4, w1T[:, :, :].rearrange("p k h -> p (k h)")), (5, w2T[:, :]))):
                act.wait_ge(wqT_psum, n + 1)
                act.activation(dest, bank[b][:, :].bitcast(BF16), ACT.Copy).then_inc(wqT_done, 1)

        def positive_part(c, i, use, dest, **by):
            t, ps = tmp[:, use % 2, :], bank[bank_of[c, i]][:, :]
            act.wait_ge(prod_ready, FIRST[c] + i + 1 + HEAD)
            if use >= 2:
                act.wait_ge(tmp_used, use - 1)
            neg = by.get("neg", 0.0)
            step(act.activation(t, ps, ACT.Relu, scale=-1.0, bias=neg))
            act.activation(dest, ps, ACT.Relu, bias=by.get("pos", 0.0)).then_inc(evac_done, 1)
            act.activation(t, t, ACT.Exp, scale=-1.0).then_inc(kq_exp_done, 1)

        def copy_kv(a):
            act.wait_ge(kv_psum, a + 1)
            act.wait_ge(kv_cleared, 1)
            pv = bank[6][:, :].rearrange("p (j e) -> p j e", j=4)
            for g in range(2):
                r = slice(64 * g, 64 * g + 64)
                act.activation(kvb[r, 4 * a:4 * a + 4, r], pv[r, :, r], ACT.Copy).then_inc(kvb_done, 1)

        def attend(a, j):
            u = use_of("z", a, j)
            act.wait_ge(att_psum, 4 * a + j + 1)
            act.wait_ge(tmp_used, u - 1)
            act.activation(tmp[:, u % 2, :], bank[6][:, :], ACT.Copy).then_inc(zb_copied, 1)
            act.wait_ge(tmp_used, u + 1)
            act.activation(oT_hi[4 * a + j][:, :], qT[a][:, j, :], ACT.Copy).then_inc(oT_hi_done, 1)

        act.wait_ge(dve_consts, 2)
        for c in range(TABLES, BON0):
            split_chunk(c + 1)
            if c == HHT0:
                split_feat(1)
            for i, m in enumerate(ROWS[c]):
                n = FIRST[c] + i
                if c in (K0, K1):
                    a = int(c == K1)
                    if a:
                        act.wait_ge(kv_psum, 1)
                    positive_part(c, i, use_of("k", a, m), kbuf[:, m, :])
                elif c in (V0, V1):
                    act.wait_ge(prod_ready, n + 1 + HEAD)
                    act.activation(vbuf[:, m, :], bank[bank_of[c, i]][:, :], ACT.Copy).then_inc(evac_done, 1)
                elif c in (Q0, Q1):
                    a = int(c == Q1)
                    if a:
                        act.wait_ge(kv_psum, 2)
                    pair = 4 * a + i
                    positive_part(c, i, use_of("q", a, i), qT[a][:, i, :], neg=nbq[:, pair:pair + 1], pos=bq_sb[:, pair:pair + 1])
                elif c not in HH:
                    s = stored_no(c) + i
                    evac_stage(n, s % 2, 16 * (s // 2), bank_of[c, i])
                for a, j in ATTEND.get((c, i), ()):
                    attend(a, j)
            if c == HHB1:
                copy_mlp_weights()
            if c == V0:
                copy_kv(0)
            if c == V1:
                copy_kv(1)

        def exponents(n, a, b):
            act.wait_ge(ex_asked, n)
            act.activation(ex[:, a:b], ex[:, a:b], ACT.Exp).then_inc(ex_done, 1)

        exponents(1, 0, T_EARLY)
        act.wait_ge(xnr_loaded, 16 * MT)
        for k in range(KT):
            act.activation(xn_hi[k][:, :, :], xn_raw[:, :, k * P:(k + 1) * P], ACT.Copy).then_inc(xn_hi_done, 1)
        exponents(2, T_EARLY, ET)
        split_chunk(BON1)
        act.wait_ge(A_psum, 1)
        for s in range(MT):
            act.activation(AT_hi[:, s, :], bank[4 + s][:, :], ACT.Copy).then_inc(A_hi_done, 1)
        for k in range(KT):
            act.wait_ge(z_scaled, k + 1)
            act.activation(xT_hi[:, k, :], ZT[k], ACT.Copy).then_inc(z_hi_done, 1)

        def copy_qT(j):
            act.wait_ge(qT_psum, j + 1)
            act.activation(q8T[ORDER[j]][:, :, :].rearrange("p k h -> p (k h)"), bank[4][:, :].bitcast(BF16), ACT.Copy).then_inc(qT_done, 1)

        def gelu(j):
            y = y1[ORDER[j]][:, :]
            act.wait_ge(y_read, j + 1)
            act.activation(y, y, ACT.Gelu).then_inc(gelu_done, 1)

        def copy_q2T(j):
            act.wait_ge(q2T_psum, j + 1)
            act.activation(q2T[ORDER[j]][:, :], bank[6][:, 0:P // 2].bitcast(BF16), ACT.Copy).then_inc(q2T_done, 1)

        copy_qT(0)
        gelu(0)
        split_chunk(BHN0)
        copy_qT(1)
        copy_q2T(0)
        gelu(1)
        split_chunk(BHN1)
        copy_qT(2)
        gelu(2)
        copy_q2T(1)
        copy_qT(3)
        copy_q2T(2)
        gelu(3)
        copy_q2T(3)

    @block.vector
    def _(dve):
        steps = [0]
        asked = [0]

        def step(ins):
            steps[0] += 1
            ins.then_inc(dve_step, 1)
            dve.wait_ge(dve_step, steps[0])

        def ask(ins):
            asked[0] += 1
            ins.then_inc(rstd_asked, 1)
            return asked[0]

        dve.memset(sel8, 0.0)
        dve.memset(b_raw[0:64, :], 0.0).then_inc(dve_consts, 1)
        dve.sem_inc(edge_dot, 8)
        dve.sem_inc(hot_used, 2)
        dve.memset(ones2[:, :], 1.0)
        dve.memset(zeros[:, :], 0.0)
        dve.memset(f32(ones_r[:, :]), 1.0)
        dve.memset(f32(ones_b[:, :]), 0.0).then_inc(dve_step, 1)
        dve.memset(run[:, :], NEG).then_inc(dve_step, 1)
        dve.memset(ks8[:, :], 0.0)
        steps[0] += 2
        dve.wait_ge(dve_step, steps[0])
        dve.memset(f32(ones_b[0:1, :]), 1.0)
        step(dve.memset(f32(ones_b[32:33, :]), 1.0))

        def normalise(m):
            dve.wait_ge(rstd_done, m + 1)
            v, y, a, r = (sm[:, i, m:m + 1] for i in range(4))
            step(dve.tensor_tensor(a, y, y, ALU.mult))
            step(dve.tensor_tensor(a, a, v, ALU.mult))
            step(dve.tensor_scalar(a, a, -0.5, 1.5, ALU.mult, ALU.add))
            step(dve.tensor_tensor(r, y, a, ALU.mult))
            dve.tensor_scalar(xn[:, m, :], x_in[:, m, :], mv[:, m, 0:1], r, ALU.subtract, ALU.mult).then_inc(xn_ready, 1)

        for m in range(MT):
            dve.wait_ge(x_loaded[m], 16)
            dve.bn_stats(stats[:, m, 0, :], x_in[:, m, 0:512])
            step(dve.bn_stats(stats[:, m, 1, :], x_in[:, m, 512:1024]))
            step(dve.bn_aggr(mv[:, m, :], stats[:, m, :, :]))
            ask(dve.tensor_scalar(sm[:, 0, m:m + 1], mv[:, m, 1:2], LN_EPS, None, ALU.add))
            if m:
                normalise(m - 1)
        normalise(MT - 1)

        def split_lo(hi_count, slot, bias=None):
            for h in range(2):
                dve.wait_ge(w_hi_done, hi_count + h)
                dve.tensor_tensor(w_lo[:, slot, h * HALF:(h + 1) * HALF], raw[:, h, :],
                                  f32(w_hi[:, slot, h * HALF:(h + 1) * HALF]), ALU.subtract).then_inc(w_lo_done, 1)
            if bias is not None:
                n, bs = bias
                dve.wait_ge(bias_hi_done, n + 1)
                dve.tensor_tensor(b_hl[32:64, bs, :], b_raw[32:64, :], f32(b_hl[32:64, bs, :]), ALU.subtract).then_inc(bias_lo_done, 1)

        def split_chunk(c):
            split_lo(2 * c + 1, c % 2, (bias_no(c), bias_no(c) % 2) if c in BIASED else None)

        split_chunk(0)
        for k in range(KT):
            dve.wait_ge(xT_hi_done, k + 1)
            dve.tensor_tensor(xT_lo[:, k, :], bank[k][:, :], f32(xT_hi[:, k, :]), ALU.subtract).then_inc(xT_lo_done, 1)

        split_chunk(1)
        dve.wait_ge(small_loaded, 16 * 5)
        dve.tensor_scalar(nbq[:, :], bq_sb[:, :], -1.0, None, ALU.mult).then_inc(dve_consts, 1)
        dve.tensor_copy(src_f[:, :], src_i[:, :])
        step(dve.tensor_copy(dst_f[:, :], dst_i[:, :]))
        for kind, (a, b) in enumerate(((0, T_HO), (T_HO, T_HO + T_OO), (T_HO + T_OO, ET))):
            dve.tensor_scalar(src_row[:, a:b], src_f[:, a:b], float(2 * kind * N), None, ALU.add)
            last = dve.tensor_scalar(dst_row[:, a:b], dst_f[:, a:b], float((2 * kind + 1) * N), None, ALU.add)
        last.then_inc(idx_ready, 1)

        dve.wait_ge(w12_loaded, 32)
        w2_flat = w2_raw[:, :, :].rearrange("p k h -> p (k h)")
        for n, w in enumerate((w1_raw[:, :], w2_flat)):
            dve.tensor_reduce(wsum[:, n:n + 1], w, AX.X, ALU.add, apply_absolute_value=True).then_inc(wsum_done, 1)
        split_chunk(2)
        dve.wait_ge(wtot_done, 1)
        step(dve.tensor_scalar(wmean[:, :], wtot[:, :], 1.0 / (H * D), 1e-5, ALU.mult, ALU.max))
        step(dve.reciprocal(wscale[:, :], wmean[:, :]))
        step(dve.tensor_scalar(wback[:, :], wmean[:, :], 1.0 / 127.0, None, ALU.mult))
        for n, (w, dest) in enumerate(((w1_raw[:, :], w1T[:, :, :].rearrange("p k h -> p (k h)")), (w2_flat, w2T[:, :]))):
            step(dve.tensor_scalar(wq_tmp[:, :], w, wscale[:, n:n + 1], ROUND, ALU.mult, ALU.add))
            step(dve.tensor_scalar(wq_tmp[:, :], wq_tmp[:, :], ROUND + 1.0, ROUND - 1.0, ALU.min, ALU.max))
            ins = dve.tensor_scalar(dest, wq_tmp[:, :], ROUND, None, ALU.subtract)
            ins.then_inc(wq_done, 1)
            dve.wait_ge(wq_done, n + 1)
        split_chunk(3)
        split_chunk(4)

        def edge_pair(t):
            for u in range(2):
                s = (t + u) % SLOTS
                mask_others(t + u)
                dve.wait_ge(dst_added[s], 16 * ((t + u) // SLOTS + 1))
                dve.scalar_tensor_tensor(out=rows_sum[:, s, :], in0=rows_sum[:, s, :], scalar=0.0, in1=wa_bc[:, :], op0=ALU.max, op1=ALU.mult,
                                         accum_out=logit[:, t + u:t + u + 1]).then_inc(edge_dot, 1)
            for u in range(2):
                dve.wait_ge(edge_dot, t + u + 9)
                take_max(t + u)

        def mask_others(t):
            dve.tensor_scalar(other[:, t % 2, :], iota[:, :], dst_f[:, t:t + 1], NEG, ALU.not_equal, ALU.mult).then_inc(edge_mask, 1)

        def take_max(t):
            k = order_of_max[0] = order_of_max[0] + 1
            dve.wait_ge(edge_mask, k)
            dve.scalar_tensor_tensor(out=run[:, :], in0=other[:, t % 2, :], scalar=logit[:, t:t + 1], in1=run[:, :],
                                     op0=ALU.add, op1=ALU.max).then_inc(edge_max, 1)
            dve.wait_ge(edge_max, k)

        order_of_max = [0]
        next_pair = [0]

        def edge_work(c, between=()):
            between = list(between)
            for i in range(PAIRS.get(c, 0)):
                edge_pair(2 * next_pair[0])
                next_pair[0] += 1
                share = -(-len(between) // (PAIRS[c] - i))
                for w in between[:share]:
                    w()
                del between[:share]
            for w in between:
                w()

        def split_feat(side):
            dest, hi = ((feat_src_lo, feat_src_hi), (feat_dst_lo, feat_dst_hi))[side]
            for b in range(4):
                dve.wait_ge(feat_hi_done, 4 * side + b + 1)
                two = (slice(None), slice(2 * b, 2 * b + 2), slice(None))
                dve.tensor_tensor(dest[two].rearrange("p k e -> p (k e)"), bank[4 + b][:, :],
                                  f32(hi[two]).rearrange("p k e -> p (k e)"), ALU.subtract).then_inc(feat_lo_done, 1)

        def hh_logits(half, i):
            c = (HHB0, HHB1)[half]
            dve.wait_ge(prod_ready, FIRST[c] + i + 1 + HEAD)
            dve.scalar_tensor_tensor(out=other[:, i, :], in0=bank[bank_of[c, i]][:, :], scalar=0.0,
                                     in1=wa_bc[:, half * CW:(half + 1) * CW], op0=ALU.max, op1=ALU.mult,
                                     accum_out=logit_hh[:, half, i:i + 1]).then_inc(hh_read, 1)
            dve.wait_ge(hh_read, 2 * half + i + 1)

        def finish_hh():
            dve.wait_ge(hh_read, 4)
            step(dve.tensor_tensor(logit[:, T_GATHERED:ET], logit_hh[:, 0, :], logit_hh[:, 1, :], ALU.add))
            for t in (T_GATHERED, T_GATHERED + 1):
                mask_others(t)
            for t in (T_GATHERED, T_GATHERED + 1):
                take_max(t)

        dve.wait_ge(consts_ready, 5)
        split_feat(0)
        for c in range(4, TABLES):
            split_chunk(c + 1)
            edge_work(c)

        def add_kq(kind, a, j):
            u = use_of(kind, a, j)
            n_exp = {("k", 0): 0, ("k", 1): 4, ("q", 0): 8, ("q", 1): 12}[kind, a] + j
            dest = kbuf[:, j, :] if kind == "k" else qT[a][:, j, :]
            dve.wait_ge(kq_exp_done, n_exp + 1)
            dve.tensor_tensor(dest, dest, tmp[:, u % 2, :], ALU.add).then_inc(tmp_used, 1)

        def spread_ks(a):
            dve.wait_ge(kv_psum, a + 1)
            for g in range(2):
                r = slice(64 * g, 64 * g + 64)
                dve.tensor_copy(ks8[r, 32 * a + g:32 * a + g + 31:10], bank[7][r, 0:8:2]).then_inc(ks_done, 1)

        def attend(a, j):
            u = use_of("z", a, j)
            dve.wait_ge(zb_copied, 4 * a + j + 1)
            dve.tensor_tensor(qT[a][:, j, :], bank[4 + j % 2][:, :], tmp[:, u % 2, :], ALU.mult).then_inc(tmp_used, 1)
            dve.wait_ge(oT_hi_done, 4 * a + j + 1)
            dve.tensor_tensor(oT_lo[4 * a + j][:, :], qT[a][:, j, :], f32(oT_hi[4 * a + j][:, :]), ALU.subtract).then_inc(oT_lo_done, 1)

        def invert_den(a):
            dve.wait_ge(den8_psum, a + 1)
            if a:
                dve.wait_ge(att_psum, 4)
            step(dve.tensor_scalar(rz, bank[7][0:8, :], 1e-8, None, ALU.add))
            dve.reciprocal(rz, rz).then_inc(rz_done, 1)

        def take_maxima(first, end):
            if first == 0:
                dve.wait_ge(max_done, 1)
                dve.sem_inc(mx_gathered, 2)
            with dve.Fori(first // 4, end // 4) as i:
                for u in range(4):
                    take_maximum(i * 4 + u, other[:, u % 2, :])

        def take_maximum(t, thrown_away):
            dve.wait_ge(mx_gathered, t + 1)
            dve.scalar_tensor_tensor(out=thrown_away, in0=iota[:, :], scalar=dst_f[:, bass.ds(t, 1)], in1=m_bc[:, :],
                                     op0=ALU.is_equal, op1=ALU.mult, accum_out=mx_e[:, bass.ds(t, 1)]).then_inc(mx_gathered, 1)

        for c in range(TABLES, PR1 + 1):
            split_chunk(c + 1)
            work = []
            if c == HHT0:
                split_feat(1)
            if c in (HHB0, HHB1):
                work = [lambda i=i, half=int(c == HHB1): hh_logits(half, i) for i in range(2)]
            if c == K0:
                finish_hh()
                dve.memset(kvb[:, :, :], 0.0).then_inc(kv_cleared, 1)
            if c in (K0, K1):
                work = [lambda j=j, a=int(c == K1): add_kq("k", a, j) for j in range(4)]
            if c == K1:
                spread_ks(0)
            if c == Q0:
                spread_ks(1)
                work = [lambda j=j: add_kq("q", 0, j) for j in range(4)]
            if c == Q1:
                work = [lambda: add_kq("q", 1, 0), lambda: invert_den(0), lambda: add_kq("q", 1, 1), lambda: add_kq("q", 1, 2),
                        lambda: attend(0, 0), lambda: attend(0, 1), lambda: add_kq("q", 1, 3), lambda: attend(0, 2), lambda: attend(0, 3)]
            if c == ON0:
                work = [lambda: invert_den(1), lambda: attend(1, 0), lambda: attend(1, 1)]
            if c == ON1:
                work = [lambda: attend(1, 2), lambda: attend(1, 3)]
            edge_work(c, work)
            if c in MAXIMA:
                take_maxima(*MAXIMA[c])

        def exponents(a, b):
            cols = slice(a, b)
            dve.wait_ge(mx_gathered, b + 2)
            step(dve.tensor_scalar(logit[:, cols], logit[:, cols], ba_sb[:, 0:1], None, ALU.add))
            step(dve.tensor_scalar(mx_e[:, cols], mx_e[:, cols], ba_sb[:, 0:1], None, ALU.add))
            dve.tensor_tensor(ex[:, cols], logit[:, cols], mx_e[:, cols], ALU.subtract).then_inc(ex_asked, 1)
            dve.wait_ge(ex_done, 1 if a == 0 else 2)
            step(dve.tensor_copy(ex16[:, cols], ex[:, cols]))
            step(dve.tensor_copy(ex_hi[:, cols], ex16[:, cols]))
            step(dve.tensor_tensor(ex_lo[:, cols], ex[:, cols], ex_hi[:, cols], ALU.subtract))

        def hot_rows(t, s):
            dve.wait_ge(hot_used, t + 1)
            dve.tensor_scalar(hot_src[:, s, :], iota[:, :], src_f[:, bass.ds(t, 1)], None, ALU.is_equal).then_inc(hot_done, 1)
            dve.tensor_scalar(hot_hi[:, s, :], iota[:, :], dst_f[:, bass.ds(t, 1)], ex_hi[:, bass.ds(t, 1)], ALU.is_equal, ALU.mult).then_inc(hot_done, 1)
            dve.tensor_scalar(hot_lo[:, s, :], iota[:, :], dst_f[:, bass.ds(t, 1)], ex_lo[:, bass.ds(t, 1)], ALU.is_equal, ALU.mult).then_inc(hot_done, 1)

        def hot_tiles(first, end):
            with dve.Fori(first // 2, end // 2) as i:
                for s in range(2):
                    hot_rows(i * 2 + s, s)

        exponents(0, T_EARLY)
        late = ET - T_EARLY
        with dve.Fori(0, late // 2) as i:
            for s in range(2):
                hot_rows(i * 2 + s, s)
                take_maximum(i * 2 + (T_EARLY + s), thrown_away[:, s, :])
        exponents(T_EARLY, ET)
        hot_tiles(late, late + 4)
        for h in range(2):
            dve.wait_ge(w_hi_done, 2 * BON1 + h + 1)
            for part in range(2):
                a = h * HALF + part * HALF // 2
                ins = dve.tensor_tensor(w_lo[:, BON1 % 2, a:a + HALF // 2], raw[:, h, part * HALF // 2:(part + 1) * HALF // 2],
                                        f32(w_hi[:, BON1 % 2, a:a + HALF // 2]), ALU.subtract)
                if part:
                    ins.then_inc(w_lo_done, 1)
                n = 2 * h + part + 1
                hot_tiles(late + 4 * n, late + 4 * n + 4)
        hot_tiles(late + 20, ET)
        for s in range(MT):
            dve.wait_ge(A_hi_done, s + 1)
            dve.tensor_tensor(AT_lo[:, s, :], bank[4 + s][:, :], f32(AT_hi[:, s, :]), ALU.subtract).then_inc(A_lo_done, 1)
        dve.wait_ge(den_psum, 1)
        step(dve.tensor_scalar(den_tmp[:, :], bank[0][:, :], 1e-30, None, ALU.max))
        step(dve.reciprocal(rden[:, :], den_tmp[:, :]))
        for k in range(KT):
            dve.wait_ge(z_psum, k + 1)
            if k >= 2:
                dve.wait_ge(z_lo_done, k - 1)
            dve.tensor_tensor(ZT[k], bank[1 + k % 3][:, :], rden[:, :], ALU.mult).then_inc(z_scaled, 1)
            dve.wait_ge(z_hi_done, k + 1)
            dve.tensor_tensor(xT_lo[:, k, :], ZT[k], f32(xT_hi[:, k, :]), ALU.subtract).then_inc(z_lo_done, 1)

        dve.wait_ge(top_loaded, 16 * MT)

        def finish_rows(j):
            m = ORDER[j]
            for c in range(2):
                q = 2 * j + c
                cols = slice(c * CW, (c + 1) * CW)
                dve.wait_ge(prod_ready, FIRST[BON0] + q + 1 + HEAD)
                dve.tensor_tensor(top[:, m, cols], bank[q % 3][:, :], top[:, m, cols], ALU.add).then_inc(bot_evac, 1)
                dve.wait_ge(mix_loaded[m], 16)
                dve.wait_ge(bot_evac, q + 1)
                step(dve.scalar_tensor_tensor(out=x2[:, m, cols], in0=top[:, m, cols], scalar=0.0, in1=x2[:, m, cols],
                                              op0=ALU.max, op1=ALU.add))
                ins = dve.bn_stats(stats[:, m, c, :], x2[:, m, cols])
            step(ins)

        def small(i, m):
            return sm[:, i, m:m + 1]

        def rstd_wait(n):
            dve.wait_ge(rstd_done, n)

        def quantise(h, amax_col, scale_col, back_col, m, which, dest):
            step(dve.tensor_reduce(small(amax_col, m), h, AX.X, ALU.max, apply_absolute_value=True))
            step(dve.tensor_scalar(small(amax_col, m), small(amax_col, m), 1e-5, None, ALU.max))
            step(dve.reciprocal(small(scale_col, m), small(amax_col, m)))
            step(dve.tensor_scalar(small(scale_col, m), small(scale_col, m), 127.0, None, ALU.mult))
            dve.tensor_scalar(small(back_col, m), small(amax_col, m), wback[:, which:which + 1], None, ALU.mult)
            step(dve.tensor_scalar(h, h, small(scale_col, m), ROUND, ALU.mult, ALU.add))
            return dve.tensor_scalar(dest, h, ROUND + 127.0, ROUND, ALU.min, ALU.subtract)

        def asked_no(m, which):
            return MT + POWERS.index((m, which)) + 1

        def norm_in(j):
            m = ORDER[j]
            step(dve.bn_aggr(mv[:, m, :], stats[:, m, :, :]))
            ask(dve.tensor_scalar(small(0, m), mv[:, m, 1:2], LN_EPS, None, ALU.add))
            dve.wait_ge(bc_loaded, 16 * 6)
            dve.scalar_tensor_tensor(out=hbuf[:, m, :], in0=x2[:, m, :], scalar=mv[:, m, 0:1], in1=g1_bc[:, :],
                                     op0=ALU.subtract, op1=ALU.mult).then_inc(x2_done, 1)

        def norm_again(j):
            m = ORDER[j]
            rstd_wait(asked_no(m, "r1"))
            step(dve.tensor_tensor(small(2, m), small(1, m), small(1, m), ALU.mult))
            ask(dve.tensor_scalar(small(2, m), small(2, m), mv[:, m, 1:2], LN_EPS, ALU.mult, ALU.add))

        def quantise_in(j):
            m = ORDER[j]
            h = hbuf[:, m, :]
            rstd_wait(asked_no(m, "r2"))
            step(dve.tensor_tensor(small(3, m), small(3, m), small(1, m), ALU.mult))
            dve.wait_ge(x2_done, j + 1)
            step(dve.scalar_tensor_tensor(out=h, in0=h, scalar=small(3, m), in1=bb1_bc[:, :], op0=ALU.mult, op1=ALU.add))
            quantise(h, 4, 5, 6, m, 0, q8[m][:, :]).then_inc(q_ready, 1)

        def hidden(j):
            m = ORDER[j]
            dve.wait_ge(y_psum, j + 1)
            dve.scalar_tensor_tensor(out=y1[m][:, :], in0=bank[5][:, 0:H], scalar=small(6, m), in1=b1_bc[:, :], op0=ALU.mult,
                                     op1=ALU.add).then_inc(y_read, 1)

        def norm_hidden(j):
            m = ORDER[j]
            y, yn = y1[m][:, :], y2[m][:, :]
            dve.wait_ge(gelu_done, j + 1)
            step(dve.bn_stats(stats[:, m, 0, :], y))
            step(dve.bn_aggr(mv2[:, m, :], stats[:, m, 0, :]))
            ask(dve.tensor_scalar(small(8, m), mv2[:, m, 1:2], LN_EPS, None, ALU.add))
            step(dve.scalar_tensor_tensor(out=yn, in0=y, scalar=mv2[:, m, 0:1], in1=g2_bc[:, :], op0=ALU.subtract, op1=ALU.mult))

        def quantise_hidden(j):
            m = ORDER[j]
            yn = y2[m][:, :]
            rstd_wait(asked_no(m, "r3"))
            step(dve.scalar_tensor_tensor(out=yn, in0=yn, scalar=small(9, m), in1=bb2_bc[:, :], op0=ALU.mult, op1=ALU.add))
            quantise(yn, 10, 11, 12, m, 1, q2[m][:, :]).then_inc(q2_ready, 1)

        def mlp_out(j):
            m = ORDER[j]
            dve.wait_ge(xb_done, j + 1)
            for c in range(2):
                col = slice(c * CW, (c + 1) * CW)
                dve.wait_ge(o_psum, 2 * j + c + 1)
                dve.scalar_tensor_tensor(out=hbuf[:, m, col], in0=bank[7 if c == 0 else 3][:, :], scalar=small(12, m),
                                         in1=x2[:, m, col], op0=ALU.mult, op1=ALU.add).then_inc(o_done, 1)

        finish_rows(0)
        norm_in(0)
        norm_again(0)
        quantise_in(0)
        finish_rows(1)
        norm_in(1)
        hidden(0)
        norm_again(1)
        norm_hidden(0)
        quantise_in(1)
        quantise_hidden(0)
        split_chunk(BHN0)
        finish_rows(2)
        norm_in(2)
        hidden(1)
        norm_again(2)
        norm_hidden(1)
        quantise_in(2)
        split_chunk(BHN1)
        quantise_hidden(1)
        mlp_out(0)
        hidden(2)
        norm_hidden(2)
        quantise_hidden(2)
        finish_rows(3)
        norm_in(3)
        norm_again(3)
        mlp_out(1)
        quantise_in(3)
        hidden(3)
        norm_hidden(3)
        mlp_out(2)
        quantise_hidden(3)
        mlp_out(3)

    @block.tensor
    def _(pe):
        pe.sem_inc(prod_ready, HEAD)
        pe.wait_ge(consts_ready, 5)
        pe.wait_ge(dve_consts, 1)
        for m in range(MT):
            pe.wait_ge(xn_ready, m + 1)
            for k in range(KT):
                ins = pe.transpose(bank[k][:, m * P:(m + 1) * P], xn[:, m, k * P:(k + 1) * P], ident[:, :])
                if m == MT - 1:
                    ins.then_inc(xT_psum, 1)

        def split_product(dest, pairs, start, stop):
            last = None
            for i, (lh, ll, rh, rl) in enumerate(pairs):
                last_one = stop and i == len(pairs) - 1
                pe.matmul(dest, lh, rh, start=start and i == 0, stop=False)
                pe.matmul(dest, lh, rl, start=False, stop=False)
                last = pe.matmul(dest, ll, rh, start=False, stop=last_one)
            return last

        def rows_product(b, slot, m, lhs_hi, lhs_lo, bias_slot=None, start=True, stop=True, each_k=None):
            if bias_slot is not None:
                pe.matmul(bank[b][:, :], ones_b[:, :], b_hl[0:64, bias_slot, :], start=True, stop=False)
            for k in range(KT):
                if each_k:
                    each_k(k)
                pair = (lhs_hi[k][:, m * P:(m + 1) * P], lhs_lo[k][:, m * P:(m + 1) * P],
                        w_hi[:, slot, k * CW:(k + 1) * CW], w_lo[:, slot, k * CW:(k + 1) * CW])
                last = split_product(bank[b][:, :], [pair], start and bias_slot is None and k == 0, stop and k == KT - 1)
            return last

        def transpose_feat(side):
            pe.wait_ge(feat_gathered, 64)
            if side:
                pe.wait_ge(feat_lo_done, 4)
            for k in range(KT):
                for u in range(2):
                    ins = pe.transpose(bank[4 + k // 2][:, (k % 2) * E_HH + u * P:(k % 2) * E_HH + (u + 1) * P],
                                       feat_raw[:, side, u, k * P:(k + 1) * P], ident[:, :])
            ins.then_inc(feat_psum, 1)

        def four_tables(i):
            for cc in range(4):
                pe.wait_ge(w_lo_done, i * 8 + 2 * (cc + 1))
                if cc < 2:
                    pe.wait_ge(bias_lo_done, i * 2 + (cc + 1))
                for m in range(MT):
                    pe.wait_ge(evac_done, i * 16 + (4 * cc + m + 1))
                    if i == 0 and cc == 0 and m == 0:
                        pe.wait_ge(xT_lo_done, 4)
                    rows_product(m, cc % 2, m, *xT, cc if cc < 2 else None,
                                 each_k=(lambda k: pe.wait_ge(xT_lo_done, k + 1)) if i == 0 and cc == 0 and m == 0 else None).then_inc(prod_ready, 1)

        def transpose_mlp_weights():
            pe.wait_ge(feat_lo_done, 8)
            pe.wait_ge(wq_done, 2)
            for k in range(KT):
                last = pe.transpose(bank[4][:, :].bitcast(BF16)[:, k * P:(k + 1) * P], w1T[:, k, :], ident16[:, :])
            last.then_inc(wqT_psum, 1)
            for k in range(KT):
                last = pe.transpose(bank[5][:, :].bitcast(BF16)[:, k * P:(k + 1) * P], w2T[:, k * H:(k + 1) * H], ident16[:, :])
            last.then_inc(wqT_psum, 1)

        def kv_product(a):
            pe.wait_ge(tmp_used, use_of("k", a, 3) + 1)
            pe.wait_ge(evac_done, evac_no((V0, V1)[a], 3) + HEAD)
            if a:
                pe.wait_ge(kvb_done, 2)
                pe.wait_ge(ks_done, 2)
            for j in range(4):
                cols = slice(j * P, (j + 1) * P)
                for m in range(MT):
                    pe.matmul(bank[6][:, j * P:(j + 1) * P], kbuf[:, m, cols], vbuf[:, m, cols], start=m == 0, stop=m == MT - 1)
                for m in range(MT):
                    last = pe.matmul(bank[7][:, 2 * j:2 * j + 2], kbuf[:, m, cols], ones2[:, :], start=m == 0, stop=m == MT - 1)
            last.then_inc(kv_psum, 1)

        def den8(a):
            pe.wait_ge(tmp_used, use_of("q", a, 3) + 1)
            pe.wait_ge(ks_done, 4)
            if a:
                pe.wait_ge(rz_done, 1)
            for j in range(4):
                pair = 4 * a + j
                last = pe.matmul(bank[7][0:8, :], ks8[:, 8 * pair:8 * pair + 8], qT[a][:, j, :], start=j == 0, stop=j == 3)
            last.then_inc(den8_psum, 1)

        def attend(a, j):
            n = 4 * a + j
            if j == 0:
                pe.wait_ge(rz_done, a + 1)
                pe.wait_ge(kvb_done, 4)
                if a == 0:
                    pe.wait_ge(wqT_done, 2)
            if j >= 2:
                pe.wait_ge(tmp_used, use_of("z", a, j - 2) + 1)
            if n >= 1:
                pe.wait_ge(zb_copied, n)
            pe.matmul(bank[4 + j % 2][:, :], kvb[:, n, :], qT[a][:, j, :], start=True, stop=True)
            pe.matmul(bank[6][:, :], sel8[:, j, :], rz, start=True, stop=True).then_inc(att_psum, 1)

        def free(c, i):
            reader = bank_free[c, i]
            if reader:
                pe.wait_ge(*((hh_read, reader[1]) if reader[0] == "hh" else (evac_done, reader[1] + HEAD)))

        four_tables(0)
        transpose_feat(0)
        four_tables(1)
        transpose_feat(1)
        for c in range(TABLES, BON0):
            slot = c % 2
            pe.wait_ge(w_lo_done, 2 * (c + 1))
            if c in BIASED:
                pe.wait_ge(bias_lo_done, bias_no(c) + 1)
            if c == PR0:
                pe.wait_ge(oT_lo_done, KT)
            if c == HHT0:
                pe.wait_ge(feat_lo_done, 4)
            if c == HHB0:
                pe.wait_ge(feat_lo_done, 8)
            lhs = {PR0: oT, PR1: oT, HHT0: feat_src, HHT1: feat_src, HHB0: feat_dst, HHB1: feat_dst}.get(c, xT)
            for i, m in enumerate(ROWS[c]):
                b = bank_of[c, i]
                free(c, i)
                if c in (Q0, Q1):
                    pairs = [(w_hi[:, slot, k * CW + i * P:k * CW + (i + 1) * P], w_lo[:, slot, k * CW + i * P:k * CW + (i + 1) * P],
                              xT_hi[:, k, :], xT_lo[:, k, :]) for k in range(KT)]
                    last = split_product(bank[b][:, :], pairs, True, True)
                else:
                    last = rows_product(b, slot, m, *lhs, bias_no(c) % 2 if c in BIASED else None,
                                        start=c not in (HHB0, HHB1), stop=c not in (HHT0, HHT1))
                last.then_inc(prod_ready, 1)
                if (c, i) in DEN8:
                    den8(DEN8[c, i])
                for a, j in ATTEND.get((c, i), ()):
                    attend(a, j)
            if c == HHB1:
                transpose_mlp_weights()
            if c == V0:
                kv_product(0)
            if c == V1:
                kv_product(1)

        pe.wait_ge(tmp_used, use_of("z", 1, 3) + 1)
        for s in range(MT):
            pe.matmul(bank[4 + s][:, :], zeros[:, :], iota[:, :], start=True, stop=True)
        with pe.Fori(0, ET // 2) as i:
            for u in range(2):
                pe.wait_ge(hot_done, i * 6 + 3 * (u + 1))
                for s in range(MT):
                    pe.matmul(bank[4 + s][:, :], hot_src[:, u, s * P:(s + 1) * P], hot_hi[:, u, :], start=False, stop=True, skip_group_check=True)
                    last = pe.matmul(bank[4 + s][:, :], hot_src[:, u, s * P:(s + 1) * P], hot_lo[:, u, :], start=False, stop=True, skip_group_check=True)
                last.then_inc(hot_used, 1)
        pe.matmul(bank[7][:, :], zeros[:, :], iota[:, :], start=False, stop=True, skip_group_check=True).then_inc(A_psum, 1)

        pe.wait_ge(evac_done, evac_no(PR1, 3) + HEAD)
        for s in range(MT):
            pe.wait_ge(A_lo_done, s + 1)
            pe.matmul(bank[0][:, :], ones_r[:, :], AT_hi[:, s, :], start=s == 0, stop=False)
            last = pe.matmul(bank[0][:, :], ones_r[:, :], AT_lo[:, s, :], start=False, stop=s == MT - 1)
        last.then_inc(den_psum, 1)
        for k in range(KT):
            if k >= 3:
                pe.wait_ge(z_scaled, k - 2)
            pe.wait_ge(xn_lo_done, k + 1)
            pairs = [(xn_hi[k][:, s, :], xn_lo[k][:, s, :], AT_hi[:, s, :], AT_lo[:, s, :]) for s in range(MT)]
            split_product(bank[1 + k % 3][:, :], pairs, True, True).then_inc(z_psum, 1)
        def up(j):
            m = ORDER[j]
            pe.wait_ge(q_ready, j + 1)
            if j >= 1:
                pe.wait_ge(qT_done, j)
            for k in range(KT):
                last = pe.transpose(bank[4][:, :].bitcast(BF16)[:, k * P:(k + 1) * P], q8[m][:, k * P:(k + 1) * P], ident16[:, :])
            last.then_inc(qT_psum, 1)
            pe.wait_ge(qT_done, j + 1)
            if j >= 1:
                pe.wait_ge(y_read, j)
            for k in range(KT):
                last = pe.matmul(bank[5][:, 0:H], q8T[m][:, k, :], w1T[:, k, :], start=k == 0, stop=k == KT - 1)
            last.then_inc(y_psum, 1)

        def down(j):
            m = ORDER[j]
            pe.wait_ge(q2_ready, j + 1)
            if j >= 1:
                pe.wait_ge(q2T_done, j)
            pe.transpose(bank[6][:, 0:P // 2].bitcast(BF16), q2[m][:, :], ident16[:, :]).then_inc(q2T_psum, 1)
            pe.wait_ge(q2T_done, j + 1)
            for c in range(2):
                if j >= 1:
                    pe.wait_ge(o_done, 2 * j + c - 1)
                pe.matmul(bank[7 if c == 0 else 3][:, :], q2T[m][:, :], w2T[:, c * CW:(c + 1) * CW], start=True, stop=True).then_inc(o_psum, 1)

        def bottom(j, c):
            q = 2 * j + c
            chunk = ((BHN0, BHN1) if ORDER[j] == 0 else (BON0, BON1))[c]
            pe.wait_ge(w_lo_done, 2 * (chunk + 1))
            if q >= 3:
                pe.wait_ge(bot_evac, q - 2)
            rows_product(q % 3, chunk % 2, ORDER[j], *xT,
                         each_k=(lambda k: pe.wait_ge(z_lo_done, k + 1)) if q == 0 else None).then_inc(prod_ready, 1)

        bottom(0, 0)
        bottom(0, 1)
        bottom(1, 0)
        bottom(1, 1)
        up(0)
        bottom(2, 0)
        bottom(2, 1)
        up(1)
        down(0)
        bottom(3, 0)
        up(2)
        bottom(3, 1)
        down(1)
        up(3)
        down(2)
        down(3)

    block_cm.__exit__(None, None, None)


def kernel(**inputs):
    import concourse.bacc as bacc
    from concourse.bass_utils import run_bass_kernel_spmd

    def arr(name):
        return np.ascontiguousarray(inputs[name])

    def chunk(w, col):
        return w[:, col:col + CW].reshape(KT, P, CW).transpose(1, 0, 2).reshape(P, KT * CW)

    def halves(w):
        return [w[0:D], w[D:2 * D]]

    chunks = []
    for kind in ("ho", "oo"):
        for w in halves(arr(f"L0_gnn_W_{kind}")):
            chunks += [chunk(w, 0), chunk(w, CW)]
    qkv = arr("L0_mix_w_qkv")
    wq, wk, wv = qkv[:, 0:D], qkv[:, D:2 * D], qkv[:, 2 * D:3 * D]
    hn, on, pr = halves(arr("L0_gnn_W_hn")), halves(arr("L0_gnn_W_on")), arr("L0_mix_w_proj")
    hh = halves(arr("L0_gnn_W_hh"))
    chunks += [chunk(hh[0], 0), chunk(hh[1], 0), chunk(hh[0], CW), chunk(hh[1], CW),
               chunk(wk, 0), chunk(hn[0], 0), chunk(wv, 0), chunk(hn[0], CW), chunk(wk, CW), chunk(wv, CW), chunk(wq, 0), chunk(wq, CW),
               chunk(on[0], 0), chunk(on[0], CW), chunk(pr, 0), chunk(pr, CW),
               chunk(on[1], 0), chunk(on[1], CW), chunk(hn[1], 0), chunk(hn[1], CW)]
    bqkv = arr("L0_mix_b_qkv")
    b_hn, b_on, b_pr = arr("L0_gnn_b_hn"), arr("L0_gnn_b_on"), arr("L0_mix_b_proj")
    bk, bv = bqkv[D:2 * D], bqkv[2 * D:3 * D]
    rows = []
    for kind in ("ho", "oo"):
        b = arr(f"L0_gnn_b_{kind}")
        rows += [b[0:CW], b[CW:D]]
    b_hh = arr("L0_gnn_b_hh")
    rows += [b_hh[0:CW], b_hh[CW:D], bk[0:CW], b_hn[0:CW], bv[0:CW], b_hn[CW:D], bk[CW:D], bv[CW:D],
             b_on[0:CW], b_on[CW:D], b_pr[0:CW], b_pr[CW:D]]

    def edge_cols(name):
        e = arr(name)
        e = np.concatenate([e[E_HH + E_OO:], e[E_HH:E_HH + E_OO], e[:E_HH]])
        return np.ascontiguousarray(e.reshape(ET, P).T)

    laid = {
        "x": arr("x").reshape(MT, P, D),
        "src": edge_cols("src"),
        "dst": edge_cols("dst"),
        "wt": np.stack(chunks),
        "bias_rows": np.stack(rows).reshape(len(BIASED), 1, CW),
        "bq": np.ascontiguousarray(bqkv[0:D].reshape(KT, P).T),
        "w_a": arr("L0_gnn_W_a").reshape(D),
        "b_a": arr("L0_gnn_b_a"),
        "ln1_g": arr("L0_ffn_ln1_g"),
        "ln1_b": arr("L0_ffn_ln1_b"),
        "w1": arr("L0_ffn_w1"),
        "b1": arr("L0_ffn_b1"),
        "ln2_g": arr("L0_ffn_ln2_g"),
        "ln2_b": arr("L0_ffn_ln2_b"),
        "w2": np.ascontiguousarray(arr("L0_ffn_w2").reshape(KT, P, H).transpose(1, 0, 2)),
        "b2": arr("L0_ffn_b2"),
    }
    nc = bacc.Bacc("TRN2", target_bir_lowering=False, num_devices=1)
    args = {n: nc.dram_tensor(f"in_{n}", a.shape, mybir.dt.from_np(a.dtype), kind="ExternalInput").ap() for n, a in laid.items()}
    out = nc.dram_tensor("out_x", (MT, P, D), F32, kind="ExternalOutput").ap()
    build(nc, **args, out=out)
    r = run_bass_kernel_spmd(nc, [{f"in_{n}": a for n, a in laid.items()}], core_ids=[0])
    return r.results[0]["out_x"].reshape(N, D)
```

```python
import numpy as np

import concourse.bass as bass
from concourse import mybir

F32 = mybir.dt.float32
F32R = mybir.dt.float32r
BF16 = mybir.dt.bfloat16
FP16 = mybir.dt.float16
I32 = mybir.dt.int32
U32 = mybir.dt.uint32
ALU = mybir.AluOpType
ACT = mybir.ActivationFunctionType
AX = mybir.AxisListType
RMAX = bass.bass_isa.ReduceOp.max
RADD = bass.bass_isa.ReduceOp.add

P = 128
N = 512
D = 1024
H = 128
HEADS = 16
HD = D // HEADS
MT = N // P
KT = D // P
CW = 512
HALF = KT * CW // 2
E = 8192
ET = E // P
E_HH, E_OO = 256, 1280
T_HO = (E - E_HH - E_OO) // P
T_OO = E_OO // P
LN_EPS = 1e-5
ROUND = 12582912.0
NEG = -3.0e38

TABLES = 8
(HHT0, HHB0, HHT1, HHB1, K0, HN0, V0, HN1, K1, V1, Q0, Q1, ON0, ON1, PR0, PR1,
 BON0, BON1, BHN0, BHN1) = range(TABLES, TABLES + 20)
CHUNKS = TABLES + 20
BIASED = [c for c in range(TABLES) if c % 4 < 2] + [HHT0, HHT1, K0, HN0, V0, HN1, K1, V1, ON0, ON1, PR0, PR1]
STORED = list(range(TABLES)) + [HN0, HN1, ON0, ON1, PR0, PR1]
HH = (HHT0, HHB0, HHT1, HHB1)
ROWS = {c: list(range(MT)) for c in range(CHUNKS)}
ROWS.update({c: [0] for c in (HN0, HN1, BHN0, BHN1)})
ROWS.update({c: [1, 2, 3] for c in (ON0, ON1, BON0, BON1)})
ROWS.update({c: [0, 1] for c in HH})
FIRST = {}
_n = 0
for _c in range(CHUNKS):
    FIRST[_c] = _n
    _n += len(ROWS[_c])
T_GATHERED = T_HO + T_OO
PAIRS = {4: 2, 5: 2, 6: 2, 7: 2, HHT0: 1, HHT1: 1, K0: 2, V0: 3, HN1: 1, K1: 3, V1: 3, Q0: 2, Q1: 3, ON0: 3, ON1: 1}
assert sum(PAIRS.values()) * 2 == T_GATHERED
MAXIMA = {PR0: (0, 16), PR1: (16, 32)}
T_EARLY = 32
SLOTS = 6
ROUND_TILES = 2 * SLOTS
HEAD = 4


ORDER = [1, 2, 3, 0]
POWERS = [(ORDER[j], r) for j, r in ((0, "r1"), (0, "r2"), (1, "r1"), (1, "r2"), (0, "r3"), (2, "r1"), (2, "r2"), (1, "r3"),
                                     (3, "r1"), (3, "r2"), (2, "r3"), (3, "r3"))]


USES = [("k", a, j) for a in range(2) for j in range(4)] + [("q", 0, j) for j in range(4)] + \
       [("q", 1, 0), ("q", 1, 1), ("q", 1, 2), ("z", 0, 0), ("z", 0, 1), ("q", 1, 3), ("z", 0, 2), ("z", 0, 3)] + \
       [("z", 1, j) for j in range(4)]
ATTEND = {(Q1, 2): [(0, 0), (0, 1)], (Q1, 3): [(0, 2), (0, 3)], (ON0, 2): [(1, 0), (1, 1)], (ON1, 0): [(1, 2)], (ON1, 1): [(1, 3)]}
DEN8 = {(Q1, 0): 0, (ON0, 0): 1}


def build(nc, x, src, dst, wt, bias_rows, bq, w_a, b_a, ln1_g, ln1_b, w1, b1, ln2_g, ln2_b, w2, b2, out):
    xn_d = nc.dram_tensor("xn_scratch", (MT, P, D), F32, kind="Internal").ap()
    table_d = nc.dram_tensor("edge_tables", (2 * 2 * N, D), F32, kind="Internal").ap()
    table_tiles = table_d.rearrange("(b m p) d -> b m p d", m=MT, p=P)
    top_d = nc.dram_tensor("node_top", (MT, P, D), F32, kind="Internal").ap()
    mix_d = nc.dram_tensor("mix_out", (MT, P, D), F32, kind="Internal").ap()

    place = [16512]

    def region(nbytes):
        at = place[0]
        place[0] += (nbytes + 31) // 32 * 32
        assert place[0] <= 229344, place[0]
        return at

    def sb(name, shape, dt, at=None):
        size = int(np.prod(shape[1:])) * mybir.dt.size(dt)
        return nc.alloc_sbuf_tensor_at(name, shape, dt, offset=region(size) if at is None else at)

    xT_hi = sb("xT_hi", [P, KT, N], F32R)
    xT_lo = sb("xT_lo", [P, KT, N], F32R)
    raw = sb("w_raw", [P, 2, HALF], F32)
    at_w_hi = region(2 * KT * CW * 4)
    w_hi = sb("w_hi", [P, 2, KT * CW], F32R, at_w_hi)
    bhn1 = sb("bhn1", [P, 2, HALF], F32, at_w_hi)
    w_lo = sb("w_lo", [P, 2, KT * CW], F32R)
    at_b = region(16384 + 64)
    w1_raw = sb("w1_raw", [P, D], F32, at_b)
    w2_raw = sb("w2_raw", [P, KT, H], F32, at_b + 4096)
    wq_tmp = sb("wq_tmp", [P, D], F32, at_b + 8192)
    feat_raw = sb("feat_raw", [P, 2, 2, D], F32, at_b)
    feat_dst_hi = sb("feat_dst_hi", [P, KT, E_HH], F32R, at_b)
    feat_dst_lo = sb("feat_dst_lo", [P, KT, E_HH], F32R, at_b + 8192)
    kbuf = sb("kbuf", [P, MT, CW], F32, at_b)
    vbuf = sb("vbuf", [P, MT, 4, P + 1], F32, at_b + 8192)
    qT1 = sb("qT1", [P, 4, N], F32, at_b)
    xn_raw = sb("xn_raw", [P, MT, D], F32, at_b)
    top = sb("top", [P, MT, D], F32, at_b)
    q8 = [sb(f"q8_{m}", [P, D], BF16, at_b + 4096 * m) for m in range(MT)]
    q8T = [sb(f"q8T_{m}", [P, KT, P], BF16, at_b + 4096 * m + 2048) for m in range(MT)]
    at_edge = region(4096 + 2048)
    wa_bc = sb("wa_bc", [P, D], F32, at_edge)
    other = sb("other_node", [P, 2, N], BF16, at_edge + 4096)
    hot_src = sb("hot_src", [P, 2, N], FP16, at_edge)
    hot_hi = sb("hot_hi", [P, 2, N], FP16, at_edge + 2048)
    hot_lo = sb("hot_lo", [P, 2, N], FP16, at_edge + 4096)
    z_scaled_T = sb("z_scaled_T", [P, 2, N], F32, at_edge)
    at_stage = region(4096)
    stage = sb("stage", [P, 2, CW], F32, at_stage)
    y1 = [sb(f"y1_{m}", [P, H], F32, at_stage + 1024 * m) for m in range(MT)]
    y2 = [sb(f"y2_{m}", [P, H], F32, at_stage + 1024 * m + 512) for m in range(MT)]
    at_big = region(32768)
    x_in = sb("x_in", [P, MT, D], F32, at_big)
    xn = sb("xn", [P, MT, D], F32, at_big + 16384)
    rows_sum = sb("gathered_rows", [P, SLOTS, D], F32, at_big)
    xn_hi = [sb(f"xn_hi{k}", [P, MT, P], F32R, at_big + 4096 * k) for k in range(KT)]
    xn_lo = [sb(f"xn_lo{k}", [P, MT, P], F32R, at_big + 4096 * k + 2048) for k in range(KT)]
    x2 = sb("x2", [P, MT, D], F32, at_big)
    hbuf = sb("hbuf", [P, MT, D], F32, at_big + 16384)
    at_q = region(8192)
    feat_src_hi = sb("feat_src_hi", [P, KT, E_HH], F32R, at_q)
    qT0 = sb("qT0", [P, 4, N], F32, at_q)
    AT_hi = sb("AT_hi", [P, MT, N], F32R, at_q)
    g1_bc = sb("g1_bc", [P, D], F32, at_q)
    bb1_bc = sb("bb1_bc", [P, D], F32, at_q + 4096)
    oT_hi = [sb(f"oT_hi{k}", [P, N], F32R, (at_b + 8192, at_big + SLOTS * 4096)[k // 4] + 2048 * (k % 4))
             for k in range(KT)]
    oT_lo = [sb(f"oT_lo{k}", [P, N], F32R, (at_q, at_b)[k // 4] + 2048 * (k % 4)) for k in range(KT)]
    at_kv = region(8192)
    feat_src_lo = sb("feat_src_lo", [P, KT, E_HH], F32R, at_kv)
    tmp = sb("tmp", [P, 2, N], F32, at_kv)
    x_part = sb("x_part", [P, MT, CW], F32, at_kv)
    kvb = sb("kvb", [P, KT, P], F32, at_kv + 4096)
    AT_lo = sb("AT_lo", [P, MT, N], F32R, at_kv)
    b2_bc = sb("b2_bc", [P, D], F32, at_kv)
    b1_bc = sb("b1_bc", [P, H], F32, at_kv + 4096)
    g2_bc = sb("g2_bc", [P, H], F32, at_kv + 4608)
    bb2_bc = sb("bb2_bc", [P, H], F32, at_kv + 5120)
    at_braw = region(2048)
    b_raw = sb("b_raw", [P, CW], F32, at_braw)
    q2 = [sb(f"q2_{m}", [P, H], BF16, at_braw + 512 * m) for m in range(MT)]
    q2T = [sb(f"q2T_{m}", [P, P], BF16, at_braw + 512 * m + 256) for m in range(MT)]
    at_bhl = region(4096)
    b_hl = sb("b_hl", [P, 2, CW], F32R, at_bhl)
    at_run = region(4096)
    run = sb("running_max", [P, N], F32, at_run)
    m_bc = sb("max_bc", [P, N], F32, at_run + 2048)
    thrown_away = sb("thrown_away", [P, 2, N], BF16, at_run)
    den_tmp = sb("den_tmp", [P, N], F32, at_run)
    rden = sb("rden", [P, N], F32, at_run + 2048)
    iota = sb("iota", [P, N], FP16)
    ks8 = sb("ks8", [P, KT * 8], F32)
    rz = sb("rz", [P, N], F32, at_braw)[64:72, :]
    sel8 = sb("sel8", [P, 4, P], F32R, at_bhl)
    z0 = sb("z0", [P, KT, P], F32, at_bhl)
    rz_hl = sb("rz_hl", [P, N], F32R, at_bhl + 2048)
    ident = sb("ident", [P, P], F32)
    ident16 = sb("ident16", [P, P], BF16)
    ones_b = sb("ones_b", [64, P], F32R)
    ones_r = sb("ones_r", [P, P], F32R)
    zeros = sb("zeros", [P, P], FP16)
    w1T = sb("w1T", [P, KT, H], BF16)
    w2T = sb("w2T", [P, D], BF16)
    src_i = sb("src_i", [P, ET], I32)
    dst_i = sb("dst_i", [P, ET], I32)
    src_f = sb("src_f", [P, ET], F32)
    dst_f = sb("dst_f", [P, ET], F32)
    src_row = sb("src_row", [P, ET], I32)
    dst_row = sb("dst_row", [P, ET], I32)
    idx_now = sb("idx_now", [P, ROUND_TILES // 3, 2, 3], I32)
    logit_hh = sb("logit_hh", [P, 2, 2], F32)
    logit = sb("logit", [P, ET], F32)
    mx_e = sb("max_of_edge", [P, ET], F32)
    ex = sb("ex", [P, ET], F32)
    ex16 = sb("ex16", [P, ET], FP16)
    ex_hi = sb("ex_hi", [P, ET], F32)
    ex_lo = sb("ex_lo", [P, ET], F32)
    bq_sb = sb("bq_sb", [P, KT], F32)
    nbq = sb("nbq", [P, KT], F32)
    ba_sb = sb("ba_sb", [P, 1], F32)
    nhalf = sb("nhalf", [P, MT], F32)
    stats = sb("stats", [P, MT, 2, 6], F32)
    mv = sb("mv", [P, MT, 2], F32)
    sm = sb("small", [P, 16, MT], F32)
    wsum = sb("wsum", [P, 2], F32)
    wtot = sb("wtot", [P, 2], F32)
    wmean = sb("wmean", [P, 2], F32)
    wscale = sb("wscale", [P, 2], F32)
    wback = sb("wback", [P, 2], F32)
    mv2 = sb("mv2", [P, MT, 2], F32)

    bank = [nc.alloc_psum_tensor(f"bank{i}", [P, CW], F32) for i in range(8)]

    def sem(name):
        return nc.alloc_semaphore(name)

    x_loaded = [sem(f"x_loaded{m}") for m in range(MT)]
    small_loaded = sem("small_loaded")
    w12_loaded = sem("w12_loaded")
    raw_loaded = [sem(f"raw_loaded{h}") for h in range(2)]
    bias_loaded = sem("bias_loaded")
    consts_ready = sem("consts_ready")
    dve_consts = sem("dve_consts")
    idx_ready = sem("idx_ready")
    rstd_asked = sem("rstd_asked")
    rstd_done = sem("rstd_done")
    xn_ready = sem("xn_ready")
    xn_stored = sem("xn_stored")
    xT_psum = sem("xT_psum")
    xT_hi_done = sem("xT_hi_done")
    xT_lo_done = sem("xT_lo_done")
    w_hi_done = sem("w_hi_done")
    w_lo_done = sem("w_lo_done")
    bias_hi_done = sem("bias_hi_done")
    bias_lo_done = sem("bias_lo_done")
    prod_ready = sem("prod_ready")
    evac_done = sem("evac_done")
    stage_stored = [sem(f"stage_stored{s}") for s in range(2)]
    feat_gathered = sem("feat_gathered")
    feat_psum = sem("feat_psum")
    feat_hi_done = sem("feat_hi_done")
    feat_lo_done = sem("feat_lo_done")
    hh_read = sem("hh_read")
    kv_cleared = sem("kv_cleared")
    wsum_done = sem("wsum_done")
    wtot_done = sem("wtot_done")
    wq_done = sem("wq_done")
    wqT_psum = sem("wqT_psum")
    wqT_done = sem("wqT_done")
    idx_copied = sem("idx_copied")
    src_landed = [sem(f"src_landed{s}") for s in range(SLOTS)]
    dst_added = [sem(f"dst_added{s}") for s in range(SLOTS)]
    edge_dot = sem("edge_dot")
    edge_mask = sem("edge_mask")
    edge_max = sem("edge_max")
    kq_exp_done = sem("kq_exp_done")
    tmp_used = sem("tmp_used")
    kv_psum = sem("kv_psum")
    kvb_done = sem("kvb_done")
    ks_done = sem("ks_done")
    den8_psum = sem("den8_psum")
    rz_done = sem("rz_done")
    att_psum = sem("att_psum")
    zb_copied = sem("zb_copied")
    oT_hi_done = sem("oT_hi_done")
    oT_lo_done = sem("oT_lo_done")
    max_done = sem("max_done")
    mx_gathered = sem("mx_gathered")
    ex_asked = sem("ex_asked")
    ex_done = sem("ex_done")
    hot_done = sem("hot_done")
    hot_used = sem("hot_used")
    A_psum = sem("A_psum")
    A_hi_done = sem("A_hi_done")
    A_lo_done = sem("A_lo_done")
    den_psum = sem("den_psum")
    z_psum = sem("z_psum")
    z_scaled = sem("z_scaled")
    z_hi_done = sem("z_hi_done")
    z_lo_done = sem("z_lo_done")
    z0_done = sem("z0_done")
    bhn1_loaded = sem("bhn1_loaded")
    xnr_loaded = sem("xnr_loaded")
    xn_hi_done = sem("xn_hi_done")
    xn_lo_done = sem("xn_lo_done")
    x_part_loaded = sem("x_part_loaded")
    x_added = sem("x_added")
    mix_loaded = [sem(f"mix_loaded{m}") for m in range(MT)]
    top_loaded = sem("top_loaded")
    bc_loaded = sem("bc_loaded")
    bot_evac = sem("bot_evac")
    x2_done = sem("x2_done")
    xb_done = sem("xb_done")
    q_ready = sem("q_ready")
    qT_psum = sem("qT_psum")
    qT_done = sem("qT_done")
    y_psum = sem("y_psum")
    y_read = sem("y_read")
    gelu_done = sem("gelu_done")
    q2_ready = sem("q2_ready")
    q2T_psum = sem("q2T_psum")
    q2T_done = sem("q2T_done")
    o_psum = sem("o_psum")
    o_done = sem("o_done")
    out_stored = sem("out_stored")
    pool_turn = sem("pool_turn")
    dve_step = sem("dve_step")
    act_step = sem("act_step")
    pool_step = sem("pool_step")

    qT = (qT0, qT1)
    xT, feat_src, feat_dst = ([[t[:, k, :] for k in range(KT)] for t in pair]
                              for pair in ((xT_hi, xT_lo), (feat_src_hi, feat_src_lo), (feat_dst_hi, feat_dst_lo)))
    oT = [[t[:, :] for t in half] for half in (oT_hi, oT_lo)]
    ZT = [z_scaled_T[:, k % 2, :] for k in range(KT)]

    def f32(ap):
        return ap.bitcast(F32)

    def piece(t, m, g):
        return t[:, 4 * g:4 * g + 4, m * P:(m + 1) * P]

    def piece_psum(m, g):
        return bank[4 + 2 * (m % 2) + g][:, :].rearrange("p (k n) -> p k n", k=4)

    def use_of(kind, a, j):
        return USES.index((kind, a, j))

    def bias_no(c):
        return sum(b < c for b in BIASED)

    def evac_no(c, i):
        return FIRST[c] + i + 1 - sum(len(ROWS[b]) for b in HH if b < c)

    bank_of, bank_free, last = {}, {}, {}
    turn = 0
    for c in range(BON0):
        for i in range(len(ROWS[c])):
            if c in (HHB0, HHB1):
                bank_of[c, i] = bank_of[c - 1, i]
                bank_free[c, i] = None
                last[bank_of[c, i]] = ("hh", 2 * (c == HHB1) + i + 1)
            else:
                b = bank_of[c, i] = turn % 4
                turn += 1
                bank_free[c, i] = last.get(b)
                last[b] = ("act", evac_no(c, i))

    def stored_no(c):
        return sum(len(ROWS[b]) for b in STORED if b < c)

    block_cm = nc.Block()
    block = block_cm.__enter__()

    @block.sync
    def _(sp):
        def load_x(m):
            sp.dma_start(x_in[:, m, :], x[m]).then_inc(x_loaded[m], 16)

        def load_half(c, h):
            sp.dma_start(raw[:, h, :], wt[c, :, h * HALF:(h + 1) * HALF]).then_inc(raw_loaded[h], 16)

        def load_bias(b):
            for row in (0, 32):
                sp.dma_start(b_raw[row:row + 1, :], bias_rows[b]).then_inc(bias_loaded, 16)

        def store(n_tile, slot, dram, ready=None):
            sp.wait_ge(*(ready or (evac_done, n_tile + HEAD)))
            sp.dma_start(dram, stage[:, slot, :]).then_inc(stage_stored[slot], 16)

        def load_x_part(c):
            col = 0 if c == PR0 else CW
            if c == PR0:
                sp.wait_ge(oT_lo_done, KT)
            else:
                sp.wait_ge(x_added, MT)
            for m in range(MT):
                sp.dma_start(x_part[:, m, :], x[m, :, col:col + CW]).then_inc(x_part_loaded, 16)

        load_x(0)
        load_half(0, 0)
        load_x(1)
        load_half(0, 1)
        load_x(2)
        load_x(3)
        sp.wait_ge(dve_consts, 1)
        load_bias(0)
        sp.dma_start(w1_raw[:, :], w1).then_inc(w12_loaded, 16)
        sp.dma_start(w2_raw[:, :, :], w2).then_inc(w12_loaded, 16)
        for h in range(2):
            sp.wait_ge(w_lo_done, h + 1)
            load_half(1, h)
        sp.wait_ge(bias_lo_done, 1)
        load_bias(1)
        for m in range(MT):
            sp.wait_ge(xn_ready, m + 1)
            sp.dma_start(xn_d[m], xn[:, m, :]).then_inc(xn_stored, 16)

        for c in range(TABLES):
            for h in range(2):
                sp.wait_ge(w_lo_done, 2 * (c + 1) + h + 1)
                load_half(c + 2, h)
            if c + 2 in BIASED:
                sp.wait_ge(bias_lo_done, bias_no(c + 2))
                load_bias(bias_no(c + 2))
            for m in range(MT):
                store(4 * c + m + 1, m % 2, table_tiles[c // 2, m, :, (c % 2) * CW:(c % 2 + 1) * CW])
        for c in range(TABLES, PR1):
            for h in range(2):
                sp.wait_ge(w_lo_done, 2 * (c + 1) + h + 1)
                load_half(c + 2, h)
            if c + 2 in BIASED:
                sp.wait_ge(bias_lo_done, bias_no(c + 2))
                load_bias(bias_no(c + 2))
            if c == PR0:
                load_x_part(PR0)
            if c in STORED:
                dram = mix_d if c == PR0 else top_d
                col = 0 if c in (HN0, ON0, PR0) else CW
                for i, m in enumerate(ROWS[c]):
                    s = (stored_no(c) + i) % 2
                    store(evac_no(c, i), s, dram[m, :, col:col + CW], (x_added, i + 1) if c == PR0 else None)
        load_x_part(PR1)
        for i, m in enumerate(ROWS[PR1]):
            store(evac_no(PR1, i), (stored_no(PR1) + i) % 2, mix_d[m, :, CW:D], (x_added, MT + i + 1))
        sp.wait_ge(prod_ready, FIRST[BON0] + HEAD)
        sp.wait_ge(xn_stored, 16 * MT)
        for m in range(MT):
            sp.dma_start(xn_raw[:, m, :], xn_d[m]).then_inc(xnr_loaded, 16)
        for c in (BON1, BHN0):
            for h in range(2):
                sp.wait_ge(w_lo_done, 2 * (c - 1) + h + 1)
                load_half(c, h)
        for s in range(2):
            sp.wait_ge(stage_stored[s], 16 * (stored_no(PR1 + 1) // 2))
        sp.wait_ge(xn_lo_done, KT)
        for m in range(MT):
            sp.dma_start(top[:, m, :], top_d[m]).then_inc(top_loaded, 16)
        for m in range(MT):
            sp.wait_ge(z_psum, m + 1)
            sp.dma_start(x2[:, m, :], mix_d[m]).then_inc(mix_loaded[m], 16)
        sp.wait_ge(z_psum, KT)
        sp.dma_start(g1_bc[:, :], ln1_g.partition_broadcast(P)).then_inc(bc_loaded, 16)
        sp.dma_start(bb1_bc[:, :], ln1_b.partition_broadcast(P)).then_inc(bc_loaded, 16)
        sp.dma_start(b2_bc[:, :], b2.partition_broadcast(P)).then_inc(bc_loaded, 16)
        sp.dma_start(b1_bc[:, :], b1.partition_broadcast(P)).then_inc(bc_loaded, 16)
        sp.dma_start(g2_bc[:, :], ln2_g.partition_broadcast(P)).then_inc(bc_loaded, 16)
        sp.dma_start(bb2_bc[:, :], ln2_b.partition_broadcast(P)).then_inc(bc_loaded, 16)
        for h in range(2):
            sp.wait_ge(prod_ready, FIRST[BON0] + 5 + HEAD)
            sp.dma_start(bhn1[:, h, :], wt[BHN1, :, h * HALF:(h + 1) * HALF]).then_inc(bhn1_loaded, 16)
        for j, m in enumerate(ORDER):
            sp.wait_ge(o_done, 2 * (j + 1))
            sp.dma_start(out[m], hbuf[:, m, :]).then_inc(out_stored, 16)
        sp.wait_ge(out_stored, 16 * MT)

    @block.gpsimd
    def _(pool):
        pool.memset(ident[:, :], 0.0).then_inc(pool_step, 1)
        pool.memset(ident16[:, :], 0.0).then_inc(pool_step, 1)
        pool.iota(iota[:, :], pattern=[[1, N]], base=0, channel_multiplier=0,
                  allow_small_or_imprecise_dtypes=True).then_inc(consts_ready, 1)
        pool.memset(nhalf[:, :], -0.5).then_inc(consts_ready, 1)
        pool.wait_ge(pool_step, 2)
        pool.affine_select(out=ident[:, :], in_=ident[:, :], compare_op=ALU.not_equal, fill=1.0,
                           base=0, pattern=[[-1, P]], channel_multiplier=1).then_inc(consts_ready, 1)
        pool.affine_select(out=ident16[:, :], in_=ident16[:, :], compare_op=ALU.not_equal, fill=1.0,
                           base=0, pattern=[[-1, P]], channel_multiplier=1).then_inc(consts_ready, 1)
        pool.wait_ge(dve_consts, 1)
        pool.wait_ge(consts_ready, 4)
        for n, row in enumerate((64, 96)):
            if n:
                pool.wait_ge(consts_ready, 5)
            sel_v = sel8[row:row + 8, :, :].rearrange("r j (g e) -> r j g e", g=2)
            pool.affine_select(out=sel_v, in_=sel_v, compare_op=ALU.not_equal, fill=1.0,
                               base=0, pattern=[[-2, 4], [-1, 2], [0, HD]], channel_multiplier=1).then_inc(consts_ready, 1)
        pool.wait_ge(consts_ready, 6)
        for m in range(MT):
            pool.wait_ge(rstd_asked, m + 1)
            pool.tensor_tensor(sm[:, 1, m:m + 1], sm[:, 0, m:m + 1], nhalf[:, 0:1], ALU.pow).then_inc(rstd_done, 1)
        pool.wait_ge(wsum_done, 2)
        pool.partition_all_reduce(wtot[:, :], wsum[:, :], P, RADD).then_inc(wtot_done, 1)

        pool.wait_ge(idx_ready, 1)
        pool.wait_ge(wq_done, 2)
        pool.wait_ge(xn_stored, 16 * MT)
        for side, index in enumerate((src_i, dst_i)):
            for u in range(2):
                pool.indirect_dma_start(
                    feat_raw[:, side, u, :], None, xn_d.rearrange("m p d -> (m p) d"),
                    bass.IndirectOffsetOnAxis(ap=index[:, T_GATHERED + u:T_GATHERED + u + 1].bitcast(U32), axis=0),
                ).then_inc(feat_gathered, 16)
        for s in range(2):
            pool.wait_ge(stage_stored[s], 16 * (4 * MT // 2))

        def gather(s, index, rows, landed, op=ALU.bypass):
            pool.indirect_dma_start(
                rows_sum[:, s, :], None, table_d[0:rows, :],
                bass.IndirectOffsetOnAxis(ap=index.bitcast(U32), axis=0), compute_op=op,
            ).then_inc(landed[s], 16)

        def add_rows(s, count, index, rows):
            pool.wait_ge(src_landed[s], count)
            pool.sem_inc(pool_turn, 1)
            gather(s, index, rows, dst_added, ALU.add)

        LAG = 2

        def gather_round(i, first):
            for u in range(ROUND_TILES):
                b, v = divmod(u, 3)
                t = i * ROUND_TILES + u
                if v == 0:
                    if not first:
                        pool.wait_ge(edge_dot, i * ROUND_TILES + (3 * (b + 1) - ROUND_TILES + 8))
                        pool.sem_inc(pool_turn, 1)
                    pool.tensor_copy(idx_now[:, b, 0, :], src_row[:, bass.ds(t, 3)]).then_inc(idx_copied, 1)
                    pool.tensor_copy(idx_now[:, b, 1, :], dst_row[:, bass.ds(t, 3)]).then_inc(idx_copied, 1)
                    pool.wait_ge(idx_copied, i * (2 * ROUND_TILES // 3) + 2 * (b + 1))
                    pool.sem_inc(pool_turn, 1)
                pool.wait_ge(edge_dot, i * ROUND_TILES + (u + 1 - SLOTS + 8))
                pool.sem_inc(pool_turn, 1)
                gather(u % SLOTS, idx_now[:, b, 0, v:v + 1], 2 * N, src_landed)
                if u >= LAG or not first:
                    w = (u - LAG) % ROUND_TILES
                    add_rows(w % SLOTS, i * 32 + (16 * ((u - LAG) // SLOTS + 1)), idx_now[:, w // 3, 1, w % 3:w % 3 + 1], 2 * N)

        gather_round(0, True)
        with pool.Fori(1, T_HO // ROUND_TILES) as i:
            gather_round(i, False)
        first = T_HO // ROUND_TILES * ROUND_TILES
        for t in range(first, T_GATHERED + LAG):
            if t == T_HO:
                for s in range(2):
                    pool.wait_ge(stage_stored[s], 16 * (TABLES * MT // 2))
            if t < T_GATHERED:
                pool.wait_ge(edge_dot, t + 1 - SLOTS + 8)
                gather(t % SLOTS, src_row[:, t:t + 1], 2 * N if t < T_HO else 4 * N, src_landed)
            t -= LAG
            add_rows(t % SLOTS, 16 * (t // SLOTS + 1), dst_row[:, t:t + 1], 2 * N if t < T_HO else 4 * N)

        pool.wait_ge(edge_max, ET)
        pool.partition_all_reduce(m_bc[:, :], run[:, :], P, RMAX).then_inc(max_done, 1)
        for c in (PR0, PR1):
            for i in range(MT):
                n = MT * int(c == PR1) + i
                pool.wait_ge(evac_done, evac_no(c, i) + HEAD)
                pool.wait_ge(x_part_loaded, 16 * MT * (1 + int(c == PR1)))
                s = (stored_no(c) + i) % 2
                pool.tensor_tensor(stage[:, s, :], stage[:, s, :], x_part[:, i, :], ALU.add).then_inc(x_added, 1)
        for k in range(KT):
            pool.wait_ge(xn_hi_done, k + 1)
            pool.tensor_tensor(xn_lo[k][:, :, :], xn_raw[:, :, k * P:(k + 1) * P], f32(xn_hi[k][:, :, :]), ALU.subtract).then_inc(xn_lo_done, 1)

        def power(n):
            pool.wait_ge(rstd_asked, n + MT + 1)
            m, which = POWERS[n]
            src_c, dst_c = {"r1": (0, 1), "r2": (2, 3), "r3": (8, 9)}[which]
            pool.tensor_tensor(sm[:, dst_c, m:m + 1], sm[:, src_c, m:m + 1], nhalf[:, 0:1], ALU.pow).then_inc(rstd_done, 1)

        for n, (m, which) in enumerate(POWERS):
            power(n)
            if which == "r2":
                pool.wait_ge(bc_loaded, 16 * 6)
                pool.wait_ge(x2_done, ORDER.index(m) + 1)
                pool.tensor_tensor(x2[:, m, :], x2[:, m, :], b2_bc[:, :], ALU.add).then_inc(xb_done, 1)

    @block.scalar
    def _(act):
        act.sem_inc(evac_done, HEAD)
        act.dma_start(src_i[:, :], src).then_inc(small_loaded, 16)
        act.dma_start(dst_i[:, :], dst).then_inc(small_loaded, 16)
        act.dma_start(bq_sb[:, :], bq).then_inc(small_loaded, 16)
        act.dma_start(ba_sb[:, :], b_a.partition_broadcast(P)).then_inc(small_loaded, 16)
        act.dma_start(wa_bc[:, :], w_a.partition_broadcast(P)).then_inc(small_loaded, 16)
        steps = [0]

        def step(ins):
            steps[0] += 1
            ins.then_inc(act_step, 1)
            act.wait_ge(act_step, steps[0])

        def split_hi(loaded, prod, slot, bias=None):
            act.wait_ge(prod_ready, prod)
            if bias is not None:
                n, bs = bias
                act.wait_ge(bias_loaded, n * 32 + 32)
                act.activation(b_hl[0:64, bs, :], b_raw[0:64, :], ACT.Copy).then_inc(bias_hi_done, 1)
            for h in range(2):
                act.wait_ge(raw_loaded[h], loaded)
                act.activation(w_hi[:, slot, h * HALF:(h + 1) * HALF], raw[:, h, :], ACT.Copy).then_inc(w_hi_done, 1)

        def split_chunk(c):
            split_hi(16 * (c + 1), FIRST[c - 1] + HEAD, c % 2, (bias_no(c), bias_no(c) % 2) if c in BIASED else None)

        def transposed_hi(m):
            for g in range(2):
                act.wait_ge(xT_psum, 2 * m + g + 1)
                act.activation(piece(xT_hi, m, g), piece_psum(m, g), ACT.Copy).then_inc(xT_hi_done, 1)

        act.wait_ge(raw_loaded[0], 16)
        act.activation(w_hi[:, 0, 0:HALF], raw[:, 0, :], ACT.Copy).then_inc(w_hi_done, 1)
        transposed_hi(0)
        act.wait_ge(raw_loaded[1], 16)
        act.activation(w_hi[:, 0, HALF:2 * HALF], raw[:, 1, :], ACT.Copy).then_inc(w_hi_done, 1)
        act.wait_ge(bias_loaded, 32)
        act.activation(b_hl[0:64, 0, :], b_raw[0:64, :], ACT.Copy).then_inc(bias_hi_done, 1)
        transposed_hi(1)
        transposed_hi(2)

        def evac_stage(n, slot, free, b):
            act.wait_ge(prod_ready, n + 1 + HEAD)
            if not (isinstance(free, int) and free == 0):
                act.wait_ge(stage_stored[slot], free)
            act.activation(stage[:, slot, :], bank[b][:, :], ACT.Copy).then_inc(evac_done, 1)

        def four_tables(i):
            for cc in range(4):
                nb = {3: i * 2 + 2, 0: i * 2 + 1}.get(cc)
                split_hi(i * 64 + 16 * (cc + 2), i * 16 + (4 * cc + HEAD), (cc + 1) % 2,
                         None if nb is None else (nb, {3: 0, 0: 1}[cc]))
                if i == 0 and cc == 0:
                    transposed_hi(3)
                for m in range(MT):
                    evac_stage(i * 16 + (4 * cc + m), m % 2, i * 128 + 16 * ((4 * cc + m) // 2), m)

        def split_feat(side):
            dest = (feat_src_hi, feat_dst_hi)[side]
            act.wait_ge(feat_psum, side + 1)
            for b in range(4):
                act.activation(dest[:, 2 * b:2 * b + 2, :].rearrange("p k e -> p (k e)"), bank[4 + b][:, :], ACT.Copy).then_inc(feat_hi_done, 1)

        four_tables(0)
        split_feat(0)
        four_tables(1)

        def copy_mlp_weights():
            for n, (b, dest) in enumerate(((4, w1T[:, :, :].rearrange("p k h -> p (k h)")), (5, w2T[:, :]))):
                act.wait_ge(wqT_psum, n + 1)
                act.activation(dest, bank[b][:, :].bitcast(BF16), ACT.Copy).then_inc(wqT_done, 1)

        def positive_part(c, i, use, dest, **by):
            t, ps = tmp[:, use % 2, :], bank[bank_of[c, i]][:, :]
            act.wait_ge(prod_ready, FIRST[c] + i + 1 + HEAD)
            if use >= 2:
                act.wait_ge(tmp_used, use - 1)
            neg = by.get("neg", 0.0)
            step(act.activation(t, ps, ACT.Relu, scale=-1.0, bias=neg))
            act.activation(dest, ps, ACT.Relu, bias=by.get("pos", 0.0)).then_inc(evac_done, 1)
            act.activation(t, t, ACT.Exp, scale=-1.0).then_inc(kq_exp_done, 1)

        def copy_kv(a):
            act.wait_ge(kv_psum, a + 1)
            act.wait_ge(kv_cleared, 1)
            for b in range(2):
                pv = bank[6 + b][:, :].rearrange("p (j e) -> p j e", j=2)
                for g in range(2):
                    r = slice(64 * g, 64 * g + 64)
                    act.activation(kvb[r, 4 * a + 2 * b:4 * a + 2 * b + 2, r], pv[r, :, r], ACT.Copy).then_inc(kvb_done, 1)

        def attend(a, j):
            u = use_of("z", a, j)
            act.wait_ge(att_psum, 4 * a + j + 1)
            act.wait_ge(tmp_used, u - 1)
            act.activation(tmp[:, u % 2, :], bank[6 + j % 2][:, :], ACT.Copy).then_inc(zb_copied, 1)
            act.wait_ge(tmp_used, u + 1)
            act.activation(oT_hi[4 * a + j][:, :], qT[a][:, j, :], ACT.Copy).then_inc(oT_hi_done, 1)

        act.wait_ge(dve_consts, 2)
        for c in range(TABLES, BON0):
            split_chunk(c + 1)
            if c == HHT0:
                split_feat(1)
            for i, m in enumerate(ROWS[c]):
                n = FIRST[c] + i
                if c in (K0, K1):
                    a = int(c == K1)
                    if a:
                        act.wait_ge(kv_psum, 1)
                    positive_part(c, i, use_of("k", a, m), kbuf[:, m, :])
                elif c in (V0, V1):
                    act.wait_ge(prod_ready, n + 1 + HEAD)
                    act.activation(vbuf[:, m, :, 0:P], bank[bank_of[c, i]][:, :].rearrange("p (j e) -> p j e", j=4), ACT.Copy).then_inc(evac_done, 1)
                elif c in (Q0, Q1):
                    a = int(c == Q1)
                    if a:
                        act.wait_ge(kv_psum, 2)
                    pair = 4 * a + i
                    positive_part(c, i, use_of("q", a, i), qT[a][:, i, :], neg=nbq[:, pair:pair + 1], pos=bq_sb[:, pair:pair + 1])
                elif c not in HH:
                    s = stored_no(c) + i
                    evac_stage(n, s % 2, 16 * (s // 2), bank_of[c, i])
                for a, j in ATTEND.get((c, i), ()):
                    attend(a, j)
            if c == HHB1:
                copy_mlp_weights()
            if c == V0:
                copy_kv(0)
            if c == V1:
                copy_kv(1)

        def exponents(n, a, b):
            act.wait_ge(ex_asked, n)
            act.activation(ex[:, a:b], ex[:, a:b], ACT.Exp).then_inc(ex_done, 1)

        exponents(1, 0, T_EARLY)
        act.wait_ge(xnr_loaded, 16 * MT)
        for k in range(KT):
            act.activation(xn_hi[k][:, :, :], xn_raw[:, :, k * P:(k + 1) * P], ACT.Copy).then_inc(xn_hi_done, 1)
        exponents(2, T_EARLY, ET)
        split_chunk(BON1)
        act.wait_ge(A_psum, 1)
        for s in range(MT):
            act.activation(AT_hi[:, s, :], bank[4 + s][:, :], ACT.Copy).then_inc(A_hi_done, 1)
        for k in range(KT):
            act.wait_ge(z_scaled, k + 1)
            act.activation(xT_hi[:, k, :], ZT[k], ACT.Copy).then_inc(z_hi_done, 1)
            act.activation(z0[:, k, :], ZT[k][:, 0:P], ACT.Copy).then_inc(z0_done, 1)

        def copy_qT(j):
            act.wait_ge(qT_psum, j + 1)
            act.activation(q8T[ORDER[j]][:, :, :].rearrange("p k h -> p (k h)"), bank[4][:, :].bitcast(BF16), ACT.Copy).then_inc(qT_done, 1)

        def gelu(j):
            y = y1[ORDER[j]][:, :]
            act.wait_ge(y_read, j + 1)
            act.activation(y, y, ACT.Gelu).then_inc(gelu_done, 1)

        def copy_q2T(j):
            act.wait_ge(q2T_psum, j + 1)
            act.activation(q2T[ORDER[j]][:, :], bank[6][:, 0:P // 2].bitcast(BF16), ACT.Copy).then_inc(q2T_done, 1)

        copy_qT(0)
        gelu(0)
        copy_qT(1)
        copy_q2T(0)
        gelu(1)
        copy_qT(2)
        gelu(2)
        copy_qT(3)
        copy_q2T(1)
        copy_q2T(2)
        gelu(3)
        copy_q2T(3)

    @block.vector
    def _(dve):
        steps = [0]
        asked = [0]

        def step(ins):
            steps[0] += 1
            ins.then_inc(dve_step, 1)
            dve.wait_ge(dve_step, steps[0])

        def ask(ins):
            asked[0] += 1
            ins.then_inc(rstd_asked, 1)
            return asked[0]

        dve.memset(f32(sel8[64:128, :, :]), 0.0)
        dve.memset(b_raw[0:64, :], 0.0).then_inc(dve_consts, 1)
        dve.sem_inc(edge_dot, 8)
        dve.sem_inc(hot_used, 2)
        dve.memset(zeros[:, :], 0.0)
        dve.memset(f32(ones_r[:, :]), 1.0)
        dve.memset(f32(ones_b[:, :]), 0.0).then_inc(dve_step, 1)
        dve.memset(run[:, :], NEG).then_inc(dve_step, 1)
        dve.memset(ks8[:, :], 0.0)
        dve.memset(f32(rz_hl[64:128, :]), 0.0)
        steps[0] += 2
        dve.wait_ge(dve_step, steps[0])
        dve.memset(f32(ones_b[0:1, :]), 1.0)
        step(dve.memset(f32(ones_b[32:33, :]), 1.0))

        def normalise(m):
            dve.wait_ge(rstd_done, m + 1)
            v, y, a, r = (sm[:, i, m:m + 1] for i in range(4))
            step(dve.tensor_tensor(a, y, y, ALU.mult))
            step(dve.tensor_tensor(a, a, v, ALU.mult))
            step(dve.tensor_scalar(a, a, -0.5, 1.5, ALU.mult, ALU.add))
            step(dve.tensor_tensor(r, y, a, ALU.mult))
            dve.tensor_scalar(xn[:, m, :], x_in[:, m, :], mv[:, m, 0:1], r, ALU.subtract, ALU.mult).then_inc(xn_ready, 1)

        def statistics(m):
            dve.wait_ge(x_loaded[m], 16)
            dve.bn_stats(stats[:, m, 0, :], x_in[:, m, 0:512])
            step(dve.bn_stats(stats[:, m, 1, :], x_in[:, m, 512:1024]))
            step(dve.bn_aggr(mv[:, m, :], stats[:, m, :, :]))
            ask(dve.tensor_scalar(sm[:, 0, m:m + 1], mv[:, m, 1:2], LN_EPS, None, ALU.add))

        def split_lo(hi_count, slot, bias=None):
            if bias is not None:
                n, bs = bias
                dve.wait_ge(bias_hi_done, n + 1)
                dve.tensor_tensor(b_hl[32:64, bs, :], b_raw[32:64, :], f32(b_hl[32:64, bs, :]), ALU.subtract).then_inc(bias_lo_done, 1)
            for h in range(2):
                dve.wait_ge(w_hi_done, hi_count + h)
                dve.tensor_tensor(w_lo[:, slot, h * HALF:(h + 1) * HALF], raw[:, h, :],
                                  f32(w_hi[:, slot, h * HALF:(h + 1) * HALF]), ALU.subtract).then_inc(w_lo_done, 1)

        def split_chunk(c):
            split_lo(2 * c + 1, c % 2, (bias_no(c), bias_no(c) % 2) if c in BIASED else None)

        def lo_half(h):
            dve.wait_ge(w_hi_done, h + 1)
            dve.tensor_tensor(w_lo[:, 0, h * HALF:(h + 1) * HALF], raw[:, h, :],
                              f32(w_hi[:, 0, h * HALF:(h + 1) * HALF]), ALU.subtract).then_inc(w_lo_done, 1)

        def transposed_lo(m):
            for g in range(2):
                dve.wait_ge(xT_hi_done, 2 * m + g + 1)
                dve.tensor_tensor(piece(xT_lo, m, g), piece_psum(m, g), f32(piece(xT_hi, m, g)), ALU.subtract).then_inc(xT_lo_done, 1)

        statistics(0)
        normalise(0)
        statistics(1)
        lo_half(0)
        transposed_lo(0)
        normalise(1)
        lo_half(1)
        dve.wait_ge(bias_hi_done, 1)
        dve.tensor_tensor(b_hl[32:64, 0, :], b_raw[32:64, :], f32(b_hl[32:64, 0, :]), ALU.subtract).then_inc(bias_lo_done, 1)
        transposed_lo(1)
        statistics(2)
        normalise(2)
        statistics(3)
        transposed_lo(2)
        normalise(3)
        split_chunk(1)
        transposed_lo(3)
        dve.wait_ge(small_loaded, 16 * 5)
        dve.tensor_scalar(nbq[:, :], bq_sb[:, :], -1.0, None, ALU.mult).then_inc(dve_consts, 1)
        dve.tensor_copy(src_f[:, :], src_i[:, :])
        step(dve.tensor_copy(dst_f[:, :], dst_i[:, :]))
        for kind, (a, b) in enumerate(((0, T_HO), (T_HO, T_HO + T_OO), (T_HO + T_OO, ET))):
            dve.tensor_scalar(src_row[:, a:b], src_f[:, a:b], float(2 * kind * N), None, ALU.add)
            last = dve.tensor_scalar(dst_row[:, a:b], dst_f[:, a:b], float((2 * kind + 1) * N), None, ALU.add)
        last.then_inc(idx_ready, 1)

        dve.wait_ge(w12_loaded, 32)
        w2_flat = w2_raw[:, :, :].rearrange("p k h -> p (k h)")
        for n, w in enumerate((w1_raw[:, :], w2_flat)):
            dve.tensor_reduce(wsum[:, n:n + 1], w, AX.X, ALU.add, apply_absolute_value=True).then_inc(wsum_done, 1)
        split_chunk(2)
        dve.wait_ge(wtot_done, 1)
        step(dve.tensor_scalar(wmean[:, :], wtot[:, :], 1.0 / (H * D), 1e-5, ALU.mult, ALU.max))
        step(dve.reciprocal(wscale[:, :], wmean[:, :]))
        step(dve.tensor_scalar(wback[:, :], wmean[:, :], 1.0 / 127.0, None, ALU.mult))
        for n, (w, dest) in enumerate(((w1_raw[:, :], w1T[:, :, :].rearrange("p k h -> p (k h)")), (w2_flat, w2T[:, :]))):
            step(dve.tensor_scalar(wq_tmp[:, :], w, wscale[:, n:n + 1], ROUND, ALU.mult, ALU.add))
            step(dve.tensor_scalar(wq_tmp[:, :], wq_tmp[:, :], ROUND + 1.0, ROUND - 1.0, ALU.min, ALU.max))
            ins = dve.tensor_scalar(dest, wq_tmp[:, :], ROUND, None, ALU.subtract)
            ins.then_inc(wq_done, 1)
            dve.wait_ge(wq_done, n + 1)
        split_chunk(3)
        split_chunk(4)

        def edge_pair(t):
            for u in range(2):
                s = (t + u) % SLOTS
                mask_others(t + u)
                dve.wait_ge(dst_added[s], 16 * ((t + u) // SLOTS + 1))
                dve.scalar_tensor_tensor(out=rows_sum[:, s, :], in0=rows_sum[:, s, :], scalar=0.0, in1=wa_bc[:, :], op0=ALU.max, op1=ALU.mult,
                                         accum_out=logit[:, t + u:t + u + 1]).then_inc(edge_dot, 1)
            for u in range(2):
                dve.wait_ge(edge_dot, t + u + 9)
                take_max(t + u)

        def mask_others(t):
            dve.tensor_scalar(other[:, t % 2, :], iota[:, :], dst_f[:, t:t + 1], NEG, ALU.not_equal, ALU.mult).then_inc(edge_mask, 1)

        def take_max(t):
            k = order_of_max[0] = order_of_max[0] + 1
            dve.wait_ge(edge_mask, k)
            dve.scalar_tensor_tensor(out=run[:, :], in0=other[:, t % 2, :], scalar=logit[:, t:t + 1], in1=run[:, :],
                                     op0=ALU.add, op1=ALU.max).then_inc(edge_max, 1)
            dve.wait_ge(edge_max, k)

        order_of_max = [0]
        next_pair = [0]

        def edge_work(c, between=()):
            between = list(between)
            for i in range(PAIRS.get(c, 0)):
                edge_pair(2 * next_pair[0])
                next_pair[0] += 1
                share = -(-len(between) // (PAIRS[c] - i))
                for w in between[:share]:
                    w()
                del between[:share]
            for w in between:
                w()

        def split_feat(side):
            dest, hi = ((feat_src_lo, feat_src_hi), (feat_dst_lo, feat_dst_hi))[side]
            for b in range(4):
                dve.wait_ge(feat_hi_done, 4 * side + b + 1)
                two = (slice(None), slice(2 * b, 2 * b + 2), slice(None))
                dve.tensor_tensor(dest[two].rearrange("p k e -> p (k e)"), bank[4 + b][:, :],
                                  f32(hi[two]).rearrange("p k e -> p (k e)"), ALU.subtract).then_inc(feat_lo_done, 1)

        def hh_logits(half, i):
            c = (HHB0, HHB1)[half]
            dve.wait_ge(prod_ready, FIRST[c] + i + 1 + HEAD)
            dve.scalar_tensor_tensor(out=other[:, i, :], in0=bank[bank_of[c, i]][:, :], scalar=0.0,
                                     in1=wa_bc[:, half * CW:(half + 1) * CW], op0=ALU.max, op1=ALU.mult,
                                     accum_out=logit_hh[:, half, i:i + 1]).then_inc(hh_read, 1)
            dve.wait_ge(hh_read, 2 * half + i + 1)

        def finish_hh():
            dve.wait_ge(hh_read, 4)
            step(dve.tensor_tensor(logit[:, T_GATHERED:ET], logit_hh[:, 0, :], logit_hh[:, 1, :], ALU.add))
            for t in (T_GATHERED, T_GATHERED + 1):
                mask_others(t)
            for t in (T_GATHERED, T_GATHERED + 1):
                take_max(t)

        dve.wait_ge(consts_ready, 5)
        split_feat(0)
        for c in range(4, TABLES):
            split_chunk(c + 1)
            edge_work(c)

        def add_kq(kind, a, j):
            u = use_of(kind, a, j)
            n_exp = {("k", 0): 0, ("k", 1): 4, ("q", 0): 8, ("q", 1): 12}[kind, a] + j
            dest = kbuf[:, j, :] if kind == "k" else qT[a][:, j, :]
            dve.wait_ge(kq_exp_done, n_exp + 1)
            dve.tensor_tensor(dest, dest, tmp[:, u % 2, :], ALU.add).then_inc(tmp_used, 1)

        def spread_ks(a):
            dve.wait_ge(kv_psum, a + 1)
            for b in range(2):
                for g in range(2):
                    r, at = slice(64 * g, 64 * g + 64), 32 * a + 20 * b + g
                    dve.tensor_copy(ks8[r, at:at + 11:10], bank[6 + b][r, P:P + 257:256]).then_inc(ks_done, 1)

        def attend(a, j):
            u = use_of("z", a, j)
            dve.wait_ge(zb_copied, 4 * a + j + 1)
            dve.tensor_tensor(qT[a][:, j, :], bank[4 + j % 2][:, :], tmp[:, u % 2, :], ALU.mult).then_inc(tmp_used, 1)
            dve.wait_ge(oT_hi_done, 4 * a + j + 1)
            dve.tensor_tensor(oT_lo[4 * a + j][:, :], qT[a][:, j, :], f32(oT_hi[4 * a + j][:, :]), ALU.subtract).then_inc(oT_lo_done, 1)

        def invert_den(a):
            dve.wait_ge(den8_psum, a + 1)
            if a:
                dve.wait_ge(att_psum, 4)
            step(dve.tensor_scalar(rz, bank[7][0:8, :], 1e-8, None, ALU.add))
            step(dve.reciprocal(rz, rz))
            step(dve.tensor_copy(rz_hl[64:72, :], rz))
            dve.tensor_tensor(rz_hl[96:104, :], rz, f32(rz_hl[64:72, :]), ALU.subtract).then_inc(rz_done, 1)

        def take_maxima(first, end):
            if first == 0:
                dve.wait_ge(max_done, 1)
                dve.sem_inc(mx_gathered, 2)
            with dve.Fori(first // 4, end // 4) as i:
                for u in range(4):
                    take_maximum(i * 4 + u, other[:, u % 2, :])

        def take_maximum(t, thrown_away):
            dve.wait_ge(mx_gathered, t + 1)
            dve.scalar_tensor_tensor(out=thrown_away, in0=iota[:, :], scalar=dst_f[:, bass.ds(t, 1)], in1=m_bc[:, :],
                                     op0=ALU.is_equal, op1=ALU.mult, accum_out=mx_e[:, bass.ds(t, 1)]).then_inc(mx_gathered, 1)

        for c in range(TABLES, PR1 + 1):
            split_chunk(c + 1)
            work = []
            if c == HHT0:
                split_feat(1)
            if c in (HHB0, HHB1):
                work = [lambda i=i, half=int(c == HHB1): hh_logits(half, i) for i in range(2)]
            if c == K0:
                finish_hh()
                dve.memset(kvb[:, :, :], 0.0).then_inc(kv_cleared, 1)
                dve.memset(vbuf[:, :, :, P:P + 1], 1.0).then_inc(kv_cleared, 1)
            if c in (K0, K1):
                work = [lambda j=j, a=int(c == K1): add_kq("k", a, j) for j in range(4)]
            if c == K1:
                spread_ks(0)
            if c == Q0:
                spread_ks(1)
                work = [lambda j=j: add_kq("q", 0, j) for j in range(4)]
            if c == Q1:
                work = [lambda: add_kq("q", 1, 0), lambda: invert_den(0), lambda: add_kq("q", 1, 1), lambda: add_kq("q", 1, 2),
                        lambda: attend(0, 0), lambda: attend(0, 1), lambda: add_kq("q", 1, 3), lambda: attend(0, 2), lambda: attend(0, 3)]
            if c == ON0:
                work = [lambda: invert_den(1), lambda: attend(1, 0), lambda: attend(1, 1)]
            if c == ON1:
                work = [lambda: attend(1, 2), lambda: attend(1, 3)]
            edge_work(c, work)
            if c in MAXIMA:
                take_maxima(*MAXIMA[c])

        def exponents(a, b):
            cols = slice(a, b)
            dve.wait_ge(mx_gathered, b + 2)
            step(dve.tensor_scalar(logit[:, cols], logit[:, cols], ba_sb[:, 0:1], None, ALU.add))
            step(dve.tensor_scalar(mx_e[:, cols], mx_e[:, cols], ba_sb[:, 0:1], None, ALU.add))
            dve.tensor_tensor(ex[:, cols], logit[:, cols], mx_e[:, cols], ALU.subtract).then_inc(ex_asked, 1)
            dve.wait_ge(ex_done, 1 if a == 0 else 2)
            step(dve.tensor_copy(ex16[:, cols], ex[:, cols]))
            step(dve.tensor_copy(ex_hi[:, cols], ex16[:, cols]))
            step(dve.tensor_tensor(ex_lo[:, cols], ex[:, cols], ex_hi[:, cols], ALU.subtract))

        def hot_rows(t, s):
            dve.wait_ge(hot_used, t + 1)
            dve.tensor_scalar(hot_src[:, s, :], iota[:, :], src_f[:, bass.ds(t, 1)], None, ALU.is_equal).then_inc(hot_done, 1)
            dve.tensor_scalar(hot_hi[:, s, :], iota[:, :], dst_f[:, bass.ds(t, 1)], ex_hi[:, bass.ds(t, 1)], ALU.is_equal, ALU.mult).then_inc(hot_done, 1)
            dve.tensor_scalar(hot_lo[:, s, :], iota[:, :], dst_f[:, bass.ds(t, 1)], ex_lo[:, bass.ds(t, 1)], ALU.is_equal, ALU.mult).then_inc(hot_done, 1)

        def hot_tiles(first, end):
            with dve.Fori(first // 2, end // 2) as i:
                for s in range(2):
                    hot_rows(i * 2 + s, s)

        exponents(0, T_EARLY)
        late = ET - T_EARLY
        with dve.Fori(0, late // 2) as i:
            for s in range(2):
                hot_rows(i * 2 + s, s)
                take_maximum(i * 2 + (T_EARLY + s), thrown_away[:, s, :])
        exponents(T_EARLY, ET)
        hot_tiles(late, late + 4)
        for h in range(2):
            dve.wait_ge(w_hi_done, 2 * BON1 + h + 1)
            for part in range(2):
                a = h * HALF + part * HALF // 2
                ins = dve.tensor_tensor(w_lo[:, BON1 % 2, a:a + HALF // 2], raw[:, h, part * HALF // 2:(part + 1) * HALF // 2],
                                        f32(w_hi[:, BON1 % 2, a:a + HALF // 2]), ALU.subtract)
                if part:
                    ins.then_inc(w_lo_done, 1)
                n = 2 * h + part + 1
                hot_tiles(late + 4 * n, late + 4 * n + 4)
        hot_tiles(late + 20, ET)
        for s in range(MT):
            dve.wait_ge(A_hi_done, s + 1)
            dve.tensor_tensor(AT_lo[:, s, :], bank[4 + s][:, :], f32(AT_hi[:, s, :]), ALU.subtract).then_inc(A_lo_done, 1)
        dve.wait_ge(den_psum, 1)
        step(dve.tensor_scalar(den_tmp[:, :], bank[0][:, :], 1e-30, None, ALU.max))
        step(dve.reciprocal(rden[:, :], den_tmp[:, :]))
        for k in range(KT):
            dve.wait_ge(z_psum, k + 1)
            if k >= 2:
                dve.wait_ge(z_lo_done, k - 1)
                dve.wait_ge(z0_done, k - 1)
            dve.tensor_tensor(ZT[k], bank[1 + k % 3][:, :], rden[:, :], ALU.mult).then_inc(z_scaled, 1)
            dve.wait_ge(z_hi_done, k + 1)
            dve.tensor_tensor(xT_lo[:, k, :], ZT[k], f32(xT_hi[:, k, :]), ALU.subtract).then_inc(z_lo_done, 1)

        dve.wait_ge(top_loaded, 16 * MT)

        def finish_rows(j):
            m = ORDER[j]
            for c in range(2):
                q = 2 * j + c
                cols = slice(c * CW, (c + 1) * CW)
                dve.wait_ge(prod_ready, FIRST[BON0] + q + 1 + HEAD)
                dve.tensor_tensor(top[:, m, cols], bank[q % 3][:, :], top[:, m, cols], ALU.add).then_inc(bot_evac, 1)
                dve.wait_ge(mix_loaded[m], 16)
                dve.wait_ge(bot_evac, q + 1)
                step(dve.scalar_tensor_tensor(out=x2[:, m, cols], in0=top[:, m, cols], scalar=0.0, in1=x2[:, m, cols],
                                              op0=ALU.max, op1=ALU.add))
                ins = dve.bn_stats(stats[:, m, c, :], x2[:, m, cols])
            step(ins)

        def small(i, m):
            return sm[:, i, m:m + 1]

        def rstd_wait(n):
            dve.wait_ge(rstd_done, n)

        def quantise(h, amax_col, scale_col, back_col, m, which, dest):
            step(dve.tensor_reduce(small(amax_col, m), h, AX.X, ALU.max, apply_absolute_value=True))
            step(dve.tensor_scalar(small(amax_col, m), small(amax_col, m), 1e-5, None, ALU.max))
            step(dve.reciprocal(small(scale_col, m), small(amax_col, m)))
            step(dve.tensor_scalar(small(scale_col, m), small(scale_col, m), 127.0, None, ALU.mult))
            dve.tensor_scalar(small(back_col, m), small(amax_col, m), wback[:, which:which + 1], None, ALU.mult)
            step(dve.tensor_scalar(h, h, small(scale_col, m), ROUND, ALU.mult, ALU.add))
            return dve.tensor_scalar(dest, h, ROUND + 127.0, ROUND, ALU.min, ALU.subtract)

        def asked_no(m, which):
            return MT + POWERS.index((m, which)) + 1

        def norm_in(j):
            m = ORDER[j]
            step(dve.bn_aggr(mv[:, m, :], stats[:, m, :, :]))
            ask(dve.tensor_scalar(small(0, m), mv[:, m, 1:2], LN_EPS, None, ALU.add))
            dve.wait_ge(bc_loaded, 16 * 6)
            dve.scalar_tensor_tensor(out=hbuf[:, m, :], in0=x2[:, m, :], scalar=mv[:, m, 0:1], in1=g1_bc[:, :],
                                     op0=ALU.subtract, op1=ALU.mult).then_inc(x2_done, 1)

        def norm_again(j):
            m = ORDER[j]
            rstd_wait(asked_no(m, "r1"))
            step(dve.tensor_tensor(small(2, m), small(1, m), small(1, m), ALU.mult))
            ask(dve.tensor_scalar(small(2, m), small(2, m), mv[:, m, 1:2], LN_EPS, ALU.mult, ALU.add))

        def quantise_in(j):
            m = ORDER[j]
            h = hbuf[:, m, :]
            rstd_wait(asked_no(m, "r2"))
            step(dve.tensor_tensor(small(3, m), small(3, m), small(1, m), ALU.mult))
            dve.wait_ge(x2_done, j + 1)
            step(dve.scalar_tensor_tensor(out=h, in0=h, scalar=small(3, m), in1=bb1_bc[:, :], op0=ALU.mult, op1=ALU.add))
            quantise(h, 4, 5, 6, m, 0, q8[m][:, :]).then_inc(q_ready, 1)

        def hidden(j):
            m = ORDER[j]
            dve.wait_ge(y_psum, j + 1)
            dve.scalar_tensor_tensor(out=y1[m][:, :], in0=bank[5][:, 0:H], scalar=small(6, m), in1=b1_bc[:, :], op0=ALU.mult,
                                     op1=ALU.add).then_inc(y_read, 1)

        def norm_hidden(j):
            m = ORDER[j]
            y, yn = y1[m][:, :], y2[m][:, :]
            dve.wait_ge(gelu_done, j + 1)
            step(dve.bn_stats(stats[:, m, 0, :], y))
            step(dve.bn_aggr(mv2[:, m, :], stats[:, m, 0, :]))
            ask(dve.tensor_scalar(small(8, m), mv2[:, m, 1:2], LN_EPS, None, ALU.add))
            step(dve.scalar_tensor_tensor(out=yn, in0=y, scalar=mv2[:, m, 0:1], in1=g2_bc[:, :], op0=ALU.subtract, op1=ALU.mult))

        def quantise_hidden(j):
            m = ORDER[j]
            yn = y2[m][:, :]
            rstd_wait(asked_no(m, "r3"))
            step(dve.scalar_tensor_tensor(out=yn, in0=yn, scalar=small(9, m), in1=bb2_bc[:, :], op0=ALU.mult, op1=ALU.add))
            quantise(yn, 10, 11, 12, m, 1, q2[m][:, :]).then_inc(q2_ready, 1)

        def mlp_out(j):
            m = ORDER[j]
            dve.wait_ge(xb_done, j + 1)
            for c in range(2):
                col = slice(c * CW, (c + 1) * CW)
                dve.wait_ge(o_psum, 2 * j + c + 1)
                dve.scalar_tensor_tensor(out=hbuf[:, m, col], in0=bank[7 if c == 0 else 3][:, :], scalar=small(12, m),
                                         in1=x2[:, m, col], op0=ALU.mult, op1=ALU.add).then_inc(o_done, 1)

        finish_rows(0)
        norm_in(0)
        norm_again(0)
        quantise_in(0)
        finish_rows(1)
        norm_in(1)
        hidden(0)
        norm_again(1)
        norm_hidden(0)
        quantise_in(1)
        quantise_hidden(0)
        finish_rows(2)
        norm_in(2)
        hidden(1)
        norm_again(2)
        mlp_out(0)
        norm_hidden(1)
        quantise_in(2)
        finish_rows(3)
        norm_in(3)
        norm_again(3)
        quantise_hidden(1)
        quantise_in(3)
        hidden(2)
        norm_hidden(2)
        quantise_hidden(2)
        hidden(3)
        norm_hidden(3)
        mlp_out(1)
        quantise_hidden(3)
        mlp_out(2)
        mlp_out(3)

    @block.tensor
    def _(pe):
        pe.sem_inc(prod_ready, HEAD)
        pe.wait_ge(consts_ready, 6)
        pe.wait_ge(dve_consts, 1)
        def transpose_rows(m):
            pe.wait_ge(xn_ready, m + 1)
            if m >= 2:
                pe.wait_ge(xT_lo_done, 2 * (m - 1))
            for k in range(KT):
                ins = pe.transpose(piece_psum(m, k // 4)[:, k % 4, :], xn[:, m, k * P:(k + 1) * P], ident[:, :])
                if k % 4 == 3:
                    ins.then_inc(xT_psum, 1)

        def split_product(dest, pairs, start, stop):
            last = None
            for i, (lh, ll, rh, rl) in enumerate(pairs):
                last_one = stop and i == len(pairs) - 1
                pe.matmul(dest, lh, rh, start=start and i == 0, stop=False)
                pe.matmul(dest, lh, rl, start=False, stop=False)
                last = pe.matmul(dest, ll, rh, start=False, stop=last_one)
            return last

        def rows_product(b, slot, m, lhs_hi, lhs_lo, bias_slot=None, start=True, stop=True, each_k=None, bias_last=False):
            if bias_slot is not None and not bias_last:
                pe.matmul(bank[b][:, :], ones_b[:, :], b_hl[0:64, bias_slot, :], start=True, stop=False)
            for k in range(KT):
                if each_k:
                    each_k(k)
                pair = (lhs_hi[k][:, m * P:(m + 1) * P], lhs_lo[k][:, m * P:(m + 1) * P],
                        w_hi[:, slot, k * CW:(k + 1) * CW], w_lo[:, slot, k * CW:(k + 1) * CW])
                last = split_product(bank[b][:, :], [pair], start and (bias_slot is None or bias_last) and k == 0,
                                     stop and not bias_last and k == KT - 1)
            if bias_last:
                pe.wait_ge(bias_lo_done, 1)
                last = pe.matmul(bank[b][:, :], ones_b[:, :], b_hl[0:64, bias_slot, :], start=False, stop=True)
            return last

        def transpose_feat(side):
            pe.wait_ge(feat_gathered, 64)
            if side:
                pe.wait_ge(feat_lo_done, 4)
            for k in range(KT):
                for u in range(2):
                    ins = pe.transpose(bank[4 + k // 2][:, (k % 2) * E_HH + u * P:(k % 2) * E_HH + (u + 1) * P],
                                       feat_raw[:, side, u, k * P:(k + 1) * P], ident[:, :])
            ins.then_inc(feat_psum, 1)

        def wait_split(c, i, also=None):
            def at(k):
                if i == 0 and k % 4 == 0:
                    pe.wait_ge(w_lo_done, 2 * c + k // 4 + 1)
                if also:
                    also(k)
            return at

        def wait_first(m, k):
            if k == 4 and m < MT - 1:
                transpose_rows(m + 1)
            if k % 4 == 0:
                pe.wait_ge(xT_lo_done, 2 * m + k // 4 + 1)
                if m == 0:
                    pe.wait_ge(w_lo_done, k // 4 + 1)

        def four_tables(i):
            for cc in range(4):
                if cc < 2 and (i, cc) != (0, 0):
                    pe.wait_ge(bias_lo_done, i * 2 + (cc + 1))
                for m in range(MT):
                    pe.wait_ge(evac_done, i * 16 + (4 * cc + m + 1))
                    rows_product(m, cc % 2, m, *xT, cc if cc < 2 else None,
                                 each_k=(lambda k: wait_first(m, k)) if i == cc == 0 else wait_split(4 * i + cc, m),
                                 bias_last=i == cc == m == 0).then_inc(prod_ready, 1)

        def transpose_mlp_weights():
            pe.wait_ge(feat_lo_done, 8)
            pe.wait_ge(wq_done, 2)
            for k in range(KT):
                last = pe.transpose(bank[4][:, :].bitcast(BF16)[:, k * P:(k + 1) * P], w1T[:, k, :], ident16[:, :])
            last.then_inc(wqT_psum, 1)
            for k in range(KT):
                last = pe.transpose(bank[5][:, :].bitcast(BF16)[:, k * P:(k + 1) * P], w2T[:, k * H:(k + 1) * H], ident16[:, :])
            last.then_inc(wqT_psum, 1)

        def kv_product(a):
            pe.wait_ge(tmp_used, use_of("k", a, 3) + 1)
            pe.wait_ge(evac_done, evac_no((V0, V1)[a], 3) + HEAD)
            pe.wait_ge(kv_cleared, 2)
            if a:
                pe.wait_ge(kvb_done, 4)
                pe.wait_ge(ks_done, 4)
            for j in range(4):
                cols = slice(j * P, (j + 1) * P)
                for m in range(MT):
                    last = pe.matmul(bank[6 + j // 2][:, (j % 2) * 256:(j % 2) * 256 + P + 1], kbuf[:, m, cols], vbuf[:, m, j, :],
                                     start=m == 0, stop=m == MT - 1)
            last.then_inc(kv_psum, 1)

        def den8(a):
            pe.wait_ge(tmp_used, use_of("q", a, 3) + 1)
            pe.wait_ge(ks_done, 8)
            if a:
                pe.wait_ge(rz_done, 1)
                pe.wait_ge(zb_copied, 4)
            for j in range(4):
                pair = 4 * a + j
                last = pe.matmul(bank[7][0:8, :], ks8[:, 8 * pair:8 * pair + 8], qT[a][:, j, :], start=j == 0, stop=j == 3)
            last.then_inc(den8_psum, 1)

        def attend(a, j):
            n = 4 * a + j
            if j == 0:
                pe.wait_ge(rz_done, a + 1)
                pe.wait_ge(kvb_done, 8)
                if a == 0:
                    pe.wait_ge(wqT_done, 2)
            if j >= 2:
                pe.wait_ge(tmp_used, use_of("z", a, j - 2) + 1)
            if n >= 2:
                pe.wait_ge(zb_copied, n - 1)
            pe.matmul(bank[4 + j % 2][:, :], kvb[:, n, :], qT[a][:, j, :], start=True, stop=True)
            pe.matmul(bank[6 + j % 2][:, :], sel8[64:128, j, :], rz_hl[64:128, :], start=True, stop=True).then_inc(att_psum, 1)

        def free(c, i):
            reader = bank_free[c, i]
            if reader:
                pe.wait_ge(*((hh_read, reader[1]) if reader[0] == "hh" else (evac_done, reader[1] + HEAD)))

        transpose_rows(0)
        four_tables(0)
        transpose_feat(0)
        four_tables(1)
        transpose_feat(1)
        for c in range(TABLES, BON0):
            slot = c % 2
            if c in BIASED:
                pe.wait_ge(bias_lo_done, bias_no(c) + 1)
            if c == HHT0:
                pe.wait_ge(feat_lo_done, 4)
            if c == HHB0:
                pe.wait_ge(feat_lo_done, 8)
            lhs = {PR0: oT, PR1: oT, HHT0: feat_src, HHT1: feat_src, HHB0: feat_dst, HHB1: feat_dst}.get(c, xT)
            for i, m in enumerate(ROWS[c]):
                b = bank_of[c, i]
                free(c, i)
                if c in (Q0, Q1):
                    pe.wait_ge(w_lo_done, 2 * (c + 1))
                    pairs = [(w_hi[:, slot, k * CW + i * P:k * CW + (i + 1) * P], w_lo[:, slot, k * CW + i * P:k * CW + (i + 1) * P],
                              xT_hi[:, k, :], xT_lo[:, k, :]) for k in range(KT)]
                    last = split_product(bank[b][:, :], pairs, True, True)
                else:
                    last = rows_product(b, slot, m, *lhs, bias_no(c) % 2 if c in BIASED else None,
                                        each_k=wait_split(c, i, (lambda k: pe.wait_ge(oT_lo_done, k + 1)) if c == PR0 and i == 0 else None),
                                        start=c not in (HHB0, HHB1), stop=c not in (HHT0, HHT1))
                last.then_inc(prod_ready, 1)
                if (c, i) in DEN8:
                    den8(DEN8[c, i])
                for a, j in ATTEND.get((c, i), ()):
                    attend(a, j)
            if c == HHB1:
                transpose_mlp_weights()
            if c == V0:
                kv_product(0)
            if c == V1:
                kv_product(1)

        pe.wait_ge(tmp_used, use_of("z", 1, 3) + 1)
        for s in range(MT):
            pe.matmul(bank[4 + s][:, :], zeros[:, :], iota[:, :], start=True, stop=True)
        with pe.Fori(0, ET // 2) as i:
            for u in range(2):
                pe.wait_ge(hot_done, i * 6 + 3 * (u + 1))
                for s in range(MT):
                    pe.matmul(bank[4 + s][:, :], hot_src[:, u, s * P:(s + 1) * P], hot_hi[:, u, :], start=False, stop=True, skip_group_check=True)
                    last = pe.matmul(bank[4 + s][:, :], hot_src[:, u, s * P:(s + 1) * P], hot_lo[:, u, :], start=False, stop=True, skip_group_check=True)
                last.then_inc(hot_used, 1)
        pe.matmul(bank[7][:, :], zeros[:, :], iota[:, :], start=False, stop=True, skip_group_check=True).then_inc(A_psum, 1)

        pe.wait_ge(evac_done, evac_no(PR1, 3) + HEAD)
        for s in range(MT):
            pe.wait_ge(A_lo_done, s + 1)
            pe.matmul(bank[0][:, :], ones_r[:, :], AT_hi[:, s, :], start=s == 0, stop=False)
            last = pe.matmul(bank[0][:, :], ones_r[:, :], AT_lo[:, s, :], start=False, stop=s == MT - 1)
        last.then_inc(den_psum, 1)
        for k in range(KT):
            if k >= 3:
                pe.wait_ge(z_scaled, k - 2)
            pe.wait_ge(xn_lo_done, k + 1)
            pairs = [(xn_hi[k][:, s, :], xn_lo[k][:, s, :], AT_hi[:, s, :], AT_lo[:, s, :]) for s in range(MT)]
            split_product(bank[1 + k % 3][:, :], pairs, True, True).then_inc(z_psum, 1)
        def up(j):
            m = ORDER[j]
            pe.wait_ge(q_ready, j + 1)
            if j >= 1:
                pe.wait_ge(qT_done, j)
            for k in range(KT):
                last = pe.transpose(bank[4][:, :].bitcast(BF16)[:, k * P:(k + 1) * P], q8[m][:, k * P:(k + 1) * P], ident16[:, :])
            last.then_inc(qT_psum, 1)
            pe.wait_ge(qT_done, j + 1)
            if j >= 1:
                pe.wait_ge(y_read, j)
            for k in range(KT):
                last = pe.matmul(bank[5][:, 0:H], q8T[m][:, k, :], w1T[:, k, :], start=k == 0, stop=k == KT - 1)
            last.then_inc(y_psum, 1)

        def down(j):
            m = ORDER[j]
            pe.wait_ge(q2_ready, j + 1)
            if j >= 1:
                pe.wait_ge(q2T_done, j)
            pe.transpose(bank[6][:, 0:P // 2].bitcast(BF16), q2[m][:, :], ident16[:, :]).then_inc(q2T_psum, 1)
            pe.wait_ge(q2T_done, j + 1)
            for c in range(2):
                if j >= 1:
                    pe.wait_ge(o_done, 2 * j + c - 1)
                pe.matmul(bank[7 if c == 0 else 3][:, :], q2T[m][:, :], w2T[:, c * CW:(c + 1) * CW], start=True, stop=True).then_inc(o_psum, 1)

        def bottom(j, c):
            q = 2 * j + c
            if q >= 3:
                pe.wait_ge(bot_evac, q - 2)
            if ORDER[j] == 0:
                for k in range(KT):
                    if k % 4 == 0:
                        if c == 0:
                            pe.wait_ge(z0_done, KT)
                            pe.wait_ge(raw_loaded[k // 4], 16 * (BHN0 + 1))
                        else:
                            pe.wait_ge(bhn1_loaded, 32)
                    w = (raw, bhn1)[c][:, k // 4, (k % 4) * CW:(k % 4 + 1) * CW]
                    last = pe.matmul(bank[q % 3][:, :], z0[:, k, :], w, start=k == 0, stop=k == KT - 1)
                last.then_inc(prod_ready, 1)
                return
            chunk = (BON0, BON1)[c]
            pe.wait_ge(w_lo_done, 2 * (chunk + 1))
            rows_product(q % 3, chunk % 2, ORDER[j], *xT,
                         each_k=(lambda k: pe.wait_ge(z_lo_done, k + 1)) if q == 0 else None).then_inc(prod_ready, 1)

        bottom(0, 0)
        bottom(0, 1)
        bottom(1, 0)
        bottom(1, 1)
        up(0)
        bottom(2, 0)
        bottom(2, 1)
        up(1)
        down(0)
        bottom(3, 0)
        bottom(3, 1)
        up(2)
        up(3)
        down(1)
        down(2)
        down(3)

    block_cm.__exit__(None, None, None)


def kernel(**inputs):
    import concourse.bacc as bacc
    from concourse.bass_utils import run_bass_kernel_spmd

    def arr(name):
        return np.ascontiguousarray(inputs[name])

    def chunk(w, col):
        return w[:, col:col + CW].reshape(KT, P, CW).transpose(1, 0, 2).reshape(P, KT * CW)

    def halves(w):
        return [w[0:D], w[D:2 * D]]

    chunks = []
    for kind in ("ho", "oo"):
        for w in halves(arr(f"L0_gnn_W_{kind}")):
            chunks += [chunk(w, 0), chunk(w, CW)]
    qkv = arr("L0_mix_w_qkv")
    wq, wk, wv = qkv[:, 0:D], qkv[:, D:2 * D], qkv[:, 2 * D:3 * D]
    hn, on, pr = halves(arr("L0_gnn_W_hn")), halves(arr("L0_gnn_W_on")), arr("L0_mix_w_proj")
    hh = halves(arr("L0_gnn_W_hh"))
    chunks += [chunk(hh[0], 0), chunk(hh[1], 0), chunk(hh[0], CW), chunk(hh[1], CW),
               chunk(wk, 0), chunk(hn[0], 0), chunk(wv, 0), chunk(hn[0], CW), chunk(wk, CW), chunk(wv, CW), chunk(wq, 0), chunk(wq, CW),
               chunk(on[0], 0), chunk(on[0], CW), chunk(pr, 0), chunk(pr, CW),
               chunk(on[1], 0), chunk(on[1], CW), chunk(hn[1], 0), chunk(hn[1], CW)]
    bqkv = arr("L0_mix_b_qkv")
    b_hn, b_on, b_pr = arr("L0_gnn_b_hn"), arr("L0_gnn_b_on"), arr("L0_mix_b_proj")
    bk, bv = bqkv[D:2 * D], bqkv[2 * D:3 * D]
    rows = []
    for kind in ("ho", "oo"):
        b = arr(f"L0_gnn_b_{kind}")
        rows += [b[0:CW], b[CW:D]]
    b_hh = arr("L0_gnn_b_hh")
    rows += [b_hh[0:CW], b_hh[CW:D], bk[0:CW], b_hn[0:CW], bv[0:CW], b_hn[CW:D], bk[CW:D], bv[CW:D],
             b_on[0:CW], b_on[CW:D], b_pr[0:CW], b_pr[CW:D]]

    def edge_cols(name):
        e = arr(name)
        e = np.concatenate([e[E_HH + E_OO:], e[E_HH:E_HH + E_OO], e[:E_HH]])
        return np.ascontiguousarray(e.reshape(ET, P).T)

    laid = {
        "x": arr("x").reshape(MT, P, D),
        "src": edge_cols("src"),
        "dst": edge_cols("dst"),
        "wt": np.stack(chunks),
        "bias_rows": np.stack(rows).reshape(len(BIASED), 1, CW),
        "bq": np.ascontiguousarray(bqkv[0:D].reshape(KT, P).T),
        "w_a": arr("L0_gnn_W_a").reshape(D),
        "b_a": arr("L0_gnn_b_a"),
        "ln1_g": arr("L0_ffn_ln1_g"),
        "ln1_b": arr("L0_ffn_ln1_b"),
        "w1": arr("L0_ffn_w1"),
        "b1": arr("L0_ffn_b1"),
        "ln2_g": arr("L0_ffn_ln2_g"),
        "ln2_b": arr("L0_ffn_ln2_b"),
        "w2": np.ascontiguousarray(arr("L0_ffn_w2").reshape(KT, P, H).transpose(1, 0, 2)),
        "b2": arr("L0_ffn_b2"),
    }
    nc = bacc.Bacc("TRN2", target_bir_lowering=False, num_devices=1)
    args = {n: nc.dram_tensor(f"in_{n}", a.shape, mybir.dt.from_np(a.dtype), kind="ExternalInput").ap() for n, a in laid.items()}
    out = nc.dram_tensor("out_x", (MT, P, D), F32, kind="ExternalOutput").ap()
    build(nc, **args, out=out)
    r = run_bass_kernel_spmd(nc, [{f"in_{n}": a for n, a in laid.items()}], core_ids=[0])
    return r.results[0]["out_x"].reshape(N, D)
```
